# Optimizing a Trainium2 kernel written in Bass

```python
import numpy as np
import jax
import jax.numpy as jnp

def _softmax(x, axis=-1):
    return jax.nn.softmax(x, axis=axis)

def _gelu(x):
    return jax.nn.gelu(x, approximate=True)

def _silu(x):
    return jax.nn.silu(x)

def _sigmoid(x):
    return jax.nn.sigmoid(x)

def _layernorm(x, axis=-1, eps=1e-05):
    m = jnp.mean(x, axis=axis, keepdims=True)
    v = jnp.var(x, axis=axis, keepdims=True)
    return (x - m) / jnp.sqrt(v + eps)

def _scatter_add(tgt, idx, src, axis=0):
    return tgt.at[idx].add(src)

def _segment_sum(src, seg, n):
    return jax.ops.segment_sum(src, seg, n)
kernel_name = 'mk_gnn_preln_d2_gnn_r32_d3bf32'

def setup_inputs(seed: int=0):
    np.random.seed(seed)
    _w = jnp.asarray

    def _rec_inputs():
        import jax
        import jax.numpy as jnp
        _gk = jax.random.key(seed)
        x = 0.0002542 + 0.9999 * jax.random.normal(jax.random.fold_in(_gk, 1), (6250, 64), jnp.float32)
        _s = jax.random.randint(jax.random.fold_in(_gk, 2), (100000,), 0, 6250, jnp.int32)
        _d = jax.random.randint(jax.random.fold_in(_gk, 3), (100000,), 0, 6250, jnp.int32)
        _loop = jnp.arange(6250, dtype=jnp.int32)
        src = jnp.concatenate([_s, _d, _loop])
        dst = jnp.concatenate([_d, _s, _loop])
        _o = jnp.argsort(dst, stable=True)
        src = src[_o]
        dst = dst[_o]
        edge_attr_32 = 0.000196303 + 1.00016 * jax.random.normal(jax.random.fold_in(_gk, 11), (206250, 32), jnp.float32)
        edge_type_2 = jax.random.randint(jax.random.fold_in(_gk, 13), (206250,), 0, 2, jnp.int32)
        return (x, src, dst, edge_attr_32, edge_type_2)
    x, src, dst, edge_attr_32, edge_type_2 = _rec_inputs()

    def _L0_gnn_setup():
        import jax, jax.numpy as jnp
        import numpy as np
        N_ENTITIES = 6250
        N_RELATIONS = 2
        EMBED_DIM = 64
        N_EDGES = 62500
        key = jax.random.key(seed)
        k1, k2, k3, k4, k5, k6, k7, k8 = jax.random.split(key, 8)
        edge_index = jax.random.randint(k1, (2, N_EDGES), 0, N_ENTITIES, dtype=jnp.int32)
        edge_type = jax.random.randint(k2, (N_EDGES,), 0, N_RELATIONS, dtype=jnp.int32)
        entity_emb = jax.random.normal(k3, (N_ENTITIES, EMBED_DIM), dtype=jnp.float32)
        relation_emb = jax.random.normal(k4, (N_RELATIONS, EMBED_DIM), dtype=jnp.float32)
        att_w = jax.random.normal(k5, (2 * EMBED_DIM, 1), dtype=jnp.float32) * 0.08
        att_b = jax.random.normal(k6, (1,), dtype=jnp.float32) * 0.08
        W_w = jax.random.normal(k7, (EMBED_DIM, EMBED_DIM), dtype=jnp.float32) * 0.12
        W_b = jax.random.normal(k8, (EMBED_DIM,), dtype=jnp.float32) * 0.12
        return {'edge_index': edge_index, 'edge_type': edge_type, 'entity_emb': entity_emb, 'relation_emb': relation_emb, 'att_w': att_w, 'att_b': att_b, 'W_w': W_w, 'W_b': W_b}
    _L0_gnn_all = _L0_gnn_setup()
    _L0_gnn_in = {k: v for k, v in _L0_gnn_all.items() if k in ('relation_emb', 'att_w', 'att_b', 'W_w', 'W_b')}
    del _L0_gnn_all

    def _L1_gnn_setup():
        import jax, jax.numpy as jnp
        import numpy as np
        N, E = (50000, 25000)
        H, KC, EC, NH = (64, 64, 32, 4)
        HPH, KPH = (H // NH, KC // NH)

        def ssp(x):
            return jax.nn.softplus(x) - jnp.log(2.0).astype(x.dtype)

        def grouped_lin(x, w):
            return jnp.einsum('nhi,hoi->nho', x, w)

        def lin(x, w, b):
            return x @ w.T + b

        def segment_softmax(logits, seg, num_segments):
            m = jax.ops.segment_max(logits, seg, num_segments=num_segments)
            m = jnp.where(jnp.isfinite(m), m, 0.0)
            e = jnp.exp(logits - m[seg])
            s = jax.ops.segment_sum(e, seg, num_segments=num_segments)
            return e / s[seg]
        key = jax.random.key(seed)
        ks = jax.random.split(key, 24)
        sc = 0.05
        inp = {'x': jax.random.normal(ks[0], (N, H), jnp.float32), 'edge_index': jax.random.randint(ks[1], (2, E), 0, N, jnp.int64), 'edge_attr': jax.random.normal(ks[2], (E, EC), jnp.float32), 'k_w': jax.random.normal(ks[3], (NH, KPH, HPH), jnp.float32) * sc, 'q_w': jax.random.normal(ks[4], (NH, KPH, HPH), jnp.float32) * sc, 'v_w': jax.random.normal(ks[5], (NH, HPH, HPH), jnp.float32) * sc, 'wkn_w1': jax.random.normal(ks[6], (KPH, EC), jnp.float32) * sc, 'wkn_b1': jnp.zeros((KPH,), jnp.float32), 'wkn_w2': jax.random.normal(ks[7], (KPH, KPH), jnp.float32) * sc, 'wkn_b2': jnp.zeros((KPH,), jnp.float32), 'wkl_w': jax.random.normal(ks[8], (KPH, KPH), jnp.float32) * sc, 'wkl_b': jnp.zeros((KPH,), jnp.float32), 'wvn_w1': jax.random.normal(ks[9], (HPH, EC), jnp.float32) * sc, 'wvn_b1': jnp.zeros((HPH,), jnp.float32), 'wvn_w2': jax.random.normal(ks[10], (HPH, HPH), jnp.float32) * sc, 'wvn_b2': jnp.zeros((HPH,), jnp.float32), 'wvl_w': jax.random.normal(ks[11], (HPH, HPH), jnp.float32) * sc, 'wvl_b': jnp.zeros((HPH,), jnp.float32), 'cen_w': jax.random.normal(ks[12], (H, H), jnp.float32) * sc, 'cen_b': jnp.zeros((H,), jnp.float32), 'out_w': jax.random.normal(ks[13], (H, H), jnp.float32) * sc, 'out_b': jnp.zeros((H,), jnp.float32)}
        return inp
    _L1_gnn_all = _L1_gnn_setup()
    _L1_gnn_in = {k: v for k, v in _L1_gnn_all.items() if k in ('k_w', 'q_w', 'v_w', 'wkn_w1', 'wkn_b1', 'wkn_w2', 'wkn_b2', 'wkl_w', 'wkl_b', 'wvn_w1', 'wvn_b1', 'wvn_w2', 'wvn_b2', 'wvl_w', 'wvl_b', 'cen_w', 'cen_b', 'out_w', 'out_b')}
    del _L1_gnn_all
    return {'x': x, 'src': src, 'dst': dst, 'edge_attr_32': edge_attr_32, 'edge_type_2': edge_type_2, 'L0_gnn_relation_emb': _L0_gnn_in['relation_emb'], 'L0_gnn_att_w': _L0_gnn_in['att_w'], 'L0_gnn_att_b': _L0_gnn_in['att_b'], 'L0_gnn_W_w': _L0_gnn_in['W_w'], 'L0_gnn_W_b': _L0_gnn_in['W_b'], 'L1_gnn_k_w': _L1_gnn_in['k_w'], 'L1_gnn_q_w': _L1_gnn_in['q_w'], 'L1_gnn_v_w': _L1_gnn_in['v_w'], 'L1_gnn_wkn_w1': _L1_gnn_in['wkn_w1'], 'L1_gnn_wkn_b1': _L1_gnn_in['wkn_b1'], 'L1_gnn_wkn_w2': _L1_gnn_in['wkn_w2'], 'L1_gnn_wkn_b2': _L1_gnn_in['wkn_b2'], 'L1_gnn_wkl_w': _L1_gnn_in['wkl_w'], 'L1_gnn_wkl_b': _L1_gnn_in['wkl_b'], 'L1_gnn_wvn_w1': _L1_gnn_in['wvn_w1'], 'L1_gnn_wvn_b1': _L1_gnn_in['wvn_b1'], 'L1_gnn_wvn_w2': _L1_gnn_in['wvn_w2'], 'L1_gnn_wvn_b2': _L1_gnn_in['wvn_b2'], 'L1_gnn_wvl_w': _L1_gnn_in['wvl_w'], 'L1_gnn_wvl_b': _L1_gnn_in['wvl_b'], 'L1_gnn_cen_w': _L1_gnn_in['cen_w'], 'L1_gnn_cen_b': _L1_gnn_in['cen_b'], 'L1_gnn_out_w': _L1_gnn_in['out_w'], 'L1_gnn_out_b': _L1_gnn_in['out_b']}

def reference(x, src, dst, edge_attr_32, edge_type_2, L0_gnn_relation_emb, L0_gnn_att_w, L0_gnn_att_b, L0_gnn_W_w, L0_gnn_W_b, L1_gnn_k_w, L1_gnn_q_w, L1_gnn_v_w, L1_gnn_wkn_w1, L1_gnn_wkn_b1, L1_gnn_wkn_w2, L1_gnn_wkn_b2, L1_gnn_wkl_w, L1_gnn_wkl_b, L1_gnn_wvn_w1, L1_gnn_wvn_b1, L1_gnn_wvn_w2, L1_gnn_wvn_b2, L1_gnn_wvl_w, L1_gnn_wvl_b, L1_gnn_cen_w, L1_gnn_cen_b, L1_gnn_out_w, L1_gnn_out_b):
    import jax
    import jax.numpy as jnp

    def _L0_gnn_ref(edge_index, edge_type, entity_emb, relation_emb, att_w, att_b, W_w, W_b):
        import jax, jax.numpy as jnp
        import numpy as np
        N_ENTITIES = 6250
        N_RELATIONS = 2
        EMBED_DIM = 64
        N_EDGES = 62500
        head = entity_emb[edge_index[0]]
        tail = entity_emb[edge_index[1]]
        rel = relation_emb[edge_type]
        head_rel = jnp.concatenate([head, rel], axis=-1)
        att_scores = jax.nn.sigmoid(head_rel @ att_w + att_b)
        neighbor_emb = att_scores * tail
        aggr_emb = jax.ops.segment_sum(neighbor_emb, edge_index[0], num_segments=N_ENTITIES)
        return jnp.tanh(aggr_emb @ W_w.T + W_b)

    def _L1_gnn_ref(x, edge_index, edge_attr, k_w, q_w, v_w, wkn_w1, wkn_b1, wkn_w2, wkn_b2, wkl_w, wkl_b, wvn_w1, wvn_b1, wvn_w2, wvn_b2, wvl_w, wvl_b, cen_w, cen_b, out_w, out_b):
        import jax, jax.numpy as jnp
        import numpy as np
        N, E = (50000, 25000)
        H, KC, EC, NH = (64, 64, 32, 4)
        HPH, KPH = (H // NH, KC // NH)

        def ssp(x):
            return jax.nn.softplus(x) - jnp.log(2.0).astype(x.dtype)

        def grouped_lin(x, w):
            return jnp.einsum('nhi,hoi->nho', x, w)

        def lin(x, w, b):
            return x @ w.T + b

        def segment_softmax(logits, seg, num_segments):
            m = jax.ops.segment_max(logits, seg, num_segments=num_segments)
            m = jnp.where(jnp.isfinite(m), m, 0.0)
            e = jnp.exp(logits - m[seg])
            s = jax.ops.segment_sum(e, seg, num_segments=num_segments)
            return e / s[seg]
        n = x.shape[0]
        row, col = (edge_index[0], edge_index[1])
        xh = x.reshape(n, NH, HPH)
        h_keys = grouped_lin(xh, k_w)
        h_queries = grouped_lin(xh, q_w)
        h_values = grouped_lin(xh, v_w)
        W_k = lin(ssp(lin(edge_attr, wkn_w1, wkn_b1)), wkn_w2, wkn_b2)
        keys_j = lin(W_k[:, None, :] * h_keys[col], wkl_w, wkl_b)
        queries_i = h_queries[row]
        qk_ij = jnp.sum(queries_i * keys_j, axis=-1)
        alpha = segment_softmax(qk_ij, row, n)
        W_v = lin(ssp(lin(edge_attr, wvn_w1, wvn_b1)), wvn_w2, wvn_b2)
        msg_j = lin(W_v[:, None, :] * h_values[col], wvl_w, wvl_b)
        msg_j = alpha[:, :, None] * msg_j
        aggr = jax.ops.segment_sum(msg_j, row, num_segments=n).reshape(n, H)
        out = lin(x, cen_w, cen_b) + aggr
        return lin(ssp(out), out_w, out_b)
    edge_index = jnp.stack([src, dst])
    h = jnp.maximum(_layernorm(x, axis=-1), 0.0)
    x = x + _L0_gnn_ref(edge_index, edge_type_2, h, L0_gnn_relation_emb, L0_gnn_att_w, L0_gnn_att_b, L0_gnn_W_w, L0_gnn_W_b)
    h = jnp.maximum(_layernorm(x, axis=-1), 0.0)
    x = x + _L1_gnn_ref(h, edge_index, edge_attr_32, L1_gnn_k_w, L1_gnn_q_w, L1_gnn_v_w, L1_gnn_wkn_w1, L1_gnn_wkn_b1, L1_gnn_wkn_w2, L1_gnn_wkn_b2, L1_gnn_wkl_w, L1_gnn_wkl_b, L1_gnn_wvn_w1, L1_gnn_wvn_b1, L1_gnn_wvn_w2, L1_gnn_wvn_b2, L1_gnn_wvl_w, L1_gnn_wvl_b, L1_gnn_cen_w, L1_gnn_cen_b, L1_gnn_out_w, L1_gnn_out_b)
    return x

_drawn_inputs = setup_inputs


def setup_inputs(seed=0):
    import zlib

    import numpy as np

    out = dict(_drawn_inputs(seed))
    spreads = {'L1_gnn_wkn_b1': (0.0, 0.8),
     'L1_gnn_wkn_b2': (0.0, 0.8),
     'L1_gnn_wkl_b': (0.0, 2.0),
     'L1_gnn_wvn_b1': (0.0, 0.8),
     'L1_gnn_wvn_b2': (0.0, 0.8),
     'L1_gnn_wvl_b': (0.0, 2.0),
     'L1_gnn_cen_b': (0.0, 2.0),
     'L1_gnn_out_b': (0.0, 0.8)}
    factors = {'edge_attr_32': 8.0,
     'L1_gnn_k_w': 8.0,
     'L1_gnn_q_w': 8.0,
     'L1_gnn_v_w': 8.0,
     'L1_gnn_wkn_w1': 8.0,
     'L1_gnn_wkn_w2': 8.0,
     'L1_gnn_wkl_w': 8.0,
     'L1_gnn_wvn_w1': 8.0,
     'L1_gnn_wvn_w2': 8.0,
     'L1_gnn_wvl_w': 8.0,
     'L1_gnn_cen_w': 7.6}
    for name, (base, spread) in spreads.items():
        noise = np.random.default_rng([zlib.crc32(name.encode()), seed]).standard_normal(out[name].shape)
        drawn = base * np.exp(spread * noise) if base else spread * noise
        out[name] = jnp.asarray(drawn.astype(out[name].dtype))
    for name, factor in factors.items():
        out[name] = (out[name] * factor).astype(out[name].dtype)
    return out
```

```python
from contextlib import ExitStack

import concourse.bass as bass
from concourse import mybir

F32, BF16, I32 = mybir.dt.float32, mybir.dt.bfloat16, mybir.dt.int32
ALU, ACT, AX = mybir.AluOpType, mybir.ActivationFunctionType, mybir.AxisListType

P = 128
N, D, E, EC = 6250, 64, 206250, 32
NH, HD = 4, 16
HI = -(-N // P)
ROWS = HI * P
LAST_ROWS = N - (HI - 1) * P
NT = -(-E // P)
FULL = E // P
REM = E - FULL * P
STREAM = NT * P
T = 26
CHUNKS = NT // T
PAIRS = CHUNKS // 2
G = 4
GROUPS = -(-T // G)
TP = GROUPS * G
T1 = T + 1
REC = 36
DST, SRC, GATE = EC, EC + 1, EC + 2
QW = D + NH
SW = D + 2 * NH
NODE_W = 2 * D + QW + D
FAR = 1e30
EPS = 1e-5
assert CHUNKS * T == NT and PAIRS * 2 == CHUNKS and NT == FULL + 1

SCATTERED = 16 * T


WEIGHTS = ["rel", "att_w", "att_b", "W_w", "W_b", "k_w", "q_w", "v_w", "kn_w1", "kn_b1", "kn_w2",
           "kn_b2", "kl_w", "kl_b", "vn_w1", "vn_b1", "vn_w2", "vn_b2", "vl_w", "vl_b", "cen_w",
           "cen_b", "out_w", "out_b"]


class Kernel:
    pass


def by_node(table):
    return table.rearrange("(h l) c -> l h c", l=P)


def by_run(stream):
    return stream[0:STREAM, :].rearrange("(p t) c -> p t c", t=NT)


def bc(ap, dim, n):
    a = ap.unsqueeze(dim)
    shape = list(a.shape)
    shape[dim] = n
    return a.broadcast_to(shape)


def wait(eng, s, n):
    if not isinstance(n, int) or n > 0:
        eng.wait_ge(s, n)


def loop(eng, body):
    body(0)
    with eng.Fori(1, PAIRS - 1) as i:
        body(i)
    body(PAIRS - 1)


class Chain:

    def __init__(self, eng, s, per_turn=0):
        self.eng, self.s, self.per_turn, self.turn, self.n, self.fewer = eng, s, per_turn, 0, 0, 0

    def begin(self, turn):
        self.turn, self.n = turn, 0

    def mark(self, ins):
        ins.then_inc(self.s, 1)
        self.n += 1

    def wait(self):
        self.eng.wait_ge(self.s, self.turn * self.per_turn + (self.n - self.fewer))

    def then(self, ins):
        self.mark(ins)
        self.wait()

    def end(self):
        if isinstance(self.turn, int) and self.turn == 0:
            self.fewer = self.per_turn - self.n
        else:
            assert self.n == self.per_turn, (self.n, self.per_turn)


def layer_norm(c, xs, work, h, mean, std, s_var, s_std, s_h):
    v = c.eng
    c.then(v.tensor_reduce(mean[:], xs[:], AX.X, ALU.add))
    c.then(v.tensor_scalar(mean[:], mean[:], -1.0 / D, None, ALU.mult))
    c.then(v.tensor_tensor(h[:], xs[:], bc(mean[:], 2, D), ALU.add))
    c.then(v.tensor_tensor(work[:], h[:], h[:], ALU.mult))
    v.tensor_reduce(std[:], work[:], AX.X, ALU.add).then_inc(s_var, 1)
    v.wait_ge(s_std, 1)
    c.then(v.reciprocal(std[:], std[:]))
    v.scalar_tensor_tensor(h[:], h[:], 0.0, bc(std[:], 2, D), ALU.max, ALU.mult).then_inc(s_h, 1)
    v.wait_ge(s_h, 1)


def split3(c, parts, value, rest):
    v = c.eng
    c.then(v.tensor_copy(parts[:, 0, :], value))
    c.then(v.tensor_tensor(rest, value, parts[:, 0, :], ALU.subtract))
    c.then(v.tensor_copy(parts[:, 1, :], rest))
    c.then(v.tensor_tensor(parts[:, 2, :], rest, parts[:, 1, :], ALU.subtract))


def at_start(i, b=0):
    return isinstance(i, int) and i == 0 and b == 0


def at_end(i, b=1):
    return isinstance(i, int) and i == PAIRS - 1 and b == 1


def helpers(k, ctx):
    nc = k.nc

    def tile(name, shape, dt=F32):
        return ctx.enter_context(nc.sbuf_tensor(name, shape, dt))

    def bank(name, dt=F32):
        return ctx.enter_context(nc.psum_tensor(name, [P, 512 if dt == F32 else 1024], dt))

    def sem(name):
        return ctx.enter_context(nc.semaphore(name))

    return tile, bank, sem


def setup(k):
    nc = k.nc
    with ExitStack() as ctx:
        tile, bank, sem = helpers(k, ctx)
        src_i, dst_i, typ_i, tmp_i = (tile(n, [P, NT], I32) for n in ("src_i", "dst_i", "typ_i", "tmp_i"))
        iota_i = tile("iota_i", [P, P], I32)
        typ_f = tile("typ_f", [P, NT])
        big = tile("big", [P, HI, D])
        h = tile("h0", [P, HI, D])
        mean, std, gate, gate_r = (tile(n, [P, HI]) for n in ("mean0", "std0", "gate", "gate_r"))
        a_r = tile("a_r", [P, 2, D])
        rel_r = tile("rel_r", [P, 2, D])
        b_r = tile("b_r", [P, 1])
        r01 = tile("r01", [P, 2])
        q_nat = tile("q_nat", [D, D])
        kl_bd = tile("kl_bd", [D, QW])
        q_fold = bank("q_fold")
        s_pad, s_zero, s_edges, s_x, s_small, s_w, s_pool = (
            sem(n) for n in ("s_pad", "s_zero", "s_edges", "s_x", "s_small", "s_w", "s_pool"))
        s_var, s_std, s_h, s_fold, s_table, s_dve = (
            sem(n) for n in ("s_var0", "s_std0", "s_h0", "s_fold", "s_table0", "s_dve0"))
        small, loaded = 12, 6 * G + 3 + 6 * NH

        with nc.Block() as block:
            @block.sync
            def _(sp):
                sp.wait_ge(s_pad, 5)
                for t, v in ((src_i, k.src), (dst_i, k.dst), (typ_i, k.etype)):
                    sp.dma_start(t[:, 0:FULL], v[0:FULL * P].rearrange("(p t) -> p t", t=FULL)).then_inc(s_edges, 16)
                    with nc.allow_non_contiguous_dma(reason="the last tile's edges"):
                        sp.dma_start(t[0:REM, FULL:NT], v[FULL * P:E].rearrange("(p t) -> p t", t=1)).then_inc(s_edges, 16)
                sp.dma_start(k.xs[:, 0:HI - 1, :], k.x[0:(HI - 1) * P, :].rearrange("(h l) c -> l h c", l=P)).then_inc(s_x, 16)
                sp.dma_start(k.xs[0:LAST_ROWS, HI - 1, :], k.x[(HI - 1) * P:N, :]).then_inc(s_x, 16)
                sp.dma_start(k.last_attr[0:REM, :], k.attr[FULL * P:E, :]).then_inc(s_x, 16)
                sp.wait_ge(s_h, 1)
                sp.dma_start(by_node(k.h_table), h[:]).then_inc(s_table, 16)
                sp.wait_ge(s_table, 16)

            @block.scalar
            def _(act):
                def row(to, vec, n):
                    act.dma_start(to, vec.rearrange("(a n) -> a n", a=1).broadcast_to([P, n])).then_inc(s_small, 16)

                row(a_r[:].rearrange("p a d -> p (a d)"), k.att_w.rearrange("a b -> (a b)"), 2 * D)
                row(rel_r[:].rearrange("p a d -> p (a d)"), k.rel.rearrange("a b -> (a b)"), 2 * D)
                row(b_r[:], k.att_b, 1)
                for to, b in ((k.W_br, k.W_b), (k.cen_br, k.cen_b), (k.out_br, k.out_b)):
                    row(to[:], b, D)
                row(k.b2_r[:, 0:HD], k.kn_b2, HD)
                row(k.b2_r[:, HD:EC], k.vn_b2, HD)
                row(k.vl_br[:, 0:HD], k.vl_b, HD)
                row(k.vl_br[:, HD:2 * HD], k.vl_b, HD)
                row(k.vl_br[:, 2 * HD:3 * HD], k.vl_b, HD)
                row(k.vl_br[:, 3 * HD:4 * HD], k.vl_b, HD)
                act.wait_ge(s_zero, 6)
                with nc.allow_non_contiguous_dma(reason="small weights, transposed as they are loaded"):
                    def load(to, w):
                        act.dma_start(to, w).then_inc(s_w, 16)

                    for p0 in range(0, P, EC):
                        for c0, w1, w2, b1 in ((0, k.kn_w1, k.kn_w2, k.kn_b1), (HD, k.vn_w1, k.vn_w2, k.vn_b1)):
                            r = slice(p0 + c0, p0 + c0 + HD)
                            load(k.w1_t[p0:p0 + EC, r], w1.rearrange("o i -> i o"))
                            load(k.w2_t[r, r], w2.rearrange("o i -> i o"))
                            load(k.b1_c[r, :], b1.rearrange("(o a) -> o a", a=1))
                    for w, to in ((k.W_w, k.W_t[:]), (k.cen_w, k.node_w[:, 2 * D + QW:NODE_W]), (k.out_w, k.out_t[:])):
                        load(to, w.rearrange("o i -> i o"))
                    for hd in range(NH):
                        r = slice(hd * HD, (hd + 1) * HD)
                        load(k.node_w[r, r], k.k_w[hd].rearrange("o i -> i o"))
                        load(k.node_w[r, D + hd * HD:D + (hd + 1) * HD], k.v_w[hd].rearrange("o i -> i o"))
                        load(k.vl_t[r, r], k.vl_w.rearrange("o i -> i o"))
                        load(q_nat[r, r], k.q_w[hd])
                        load(kl_bd[r, r], k.kl_w)
                        load(kl_bd[r, D + hd:D + hd + 1], k.kl_b.rearrange("(o a) -> o a", a=1))
                act.wait_ge(s_var, 1)
                nc.scalar.activation(std[:], std[:], ACT.Sqrt, bias=k.eps[:], scale=1.0 / D).then_inc(s_std, 1)

            @block.gpsimd
            def _(pool):
                nc.gpsimd.iota(iota_i[:], [[1, P]], base=0, channel_multiplier=0).then_inc(s_pool, 1)
                nc.gpsimd.memset(k.ident[:], 0.0).then_inc(s_pool, 1)
                nc.gpsimd.memset(k.less[:], 1.0).then_inc(s_pool, 1)
                nc.gpsimd.memset(k.ones[:], 1.0).then_inc(s_pool, 1)
                pool.wait_ge(s_pool, 4)
                nc.gpsimd.affine_select(out=k.ident[:], in_=k.ident[:], compare_op=ALU.not_equal, fill=1.0,
                                        base=0, pattern=[[-1, P]], channel_multiplier=1).then_inc(s_pool, 1)
                nc.gpsimd.affine_select(out=k.less[:], in_=k.less[:], compare_op=ALU.is_gt, fill=0.0,
                                        base=0, pattern=[[1, P]], channel_multiplier=-1).then_inc(s_pool, 1)

            @block.tensor
            def _(pe):
                pe.wait_ge(s_w, 16 * loaded)
                nc.tensor.matmul(q_fold[0:D, 0:QW], q_nat[:], kl_bd[:], start=True, stop=True).then_inc(s_fold, 1)

            @block.vector
            def _(dve):
                c = Chain(dve, s_dve)
                for t, v in ((src_i, ROWS - 1), (dst_i, 0), (typ_i, 0)):
                    nc.vector.memset(t[:, FULL:NT], v).then_inc(s_pad, 1)
                nc.vector.memset(k.xs[:, HI - 1, :], 0.0).then_inc(s_pad, 1)
                nc.vector.memset(k.last_attr[:], 0.0).then_inc(s_pad, 1)
                for t in (k.w1_t, k.w2_t, k.node_w, k.vl_t, q_nat, kl_bd):
                    nc.vector.memset(t[:], 0.0).then_inc(s_zero, 1)
                c.mark(nc.vector.memset(k.eps[:], EPS))
                dve.wait_ge(s_edges, 96)
                c.then(nc.vector.tensor_single_scalar(tmp_i[:], src_i[:], P - 1, ALU.bitwise_and))
                c.then(nc.vector.tensor_copy(k.lo_b[:], tmp_i[:]))
                c.then(nc.vector.tensor_single_scalar(tmp_i[:], src_i[:], 7, ALU.arith_shift_right))
                c.mark(nc.vector.tensor_copy(k.hi_b[:], tmp_i[:]))
                c.mark(nc.vector.tensor_copy(k.src_f[:], src_i[:]))
                c.mark(nc.vector.tensor_copy(k.dst_f[:], dst_i[:]))
                c.mark(nc.vector.tensor_copy(typ_f[:], typ_i[:]))
                dve.wait_ge(s_pool, 6)
                c.mark(nc.vector.tensor_copy(k.iota_p[:], iota_i[:]))
                c.mark(nc.vector.tensor_copy(k.iota_b[:], iota_i[:]))
                c.mark(nc.vector.tensor_copy(k.identb[:], k.ident[:]))
                dve.wait_ge(s_small, 16 * small)
                c.then(nc.vector.tensor_tensor(rel_r[:], rel_r[:], bc(a_r[:, 1, :], 1, 2), ALU.mult))
                c.then(nc.vector.tensor_reduce(r01[:], rel_r[:], AX.X, ALU.add))
                c.then(nc.vector.tensor_tensor(r01[:], r01[:], b_r[:].broadcast_to([P, 2]), ALU.add))
                c.then(nc.vector.tensor_scalar(k.rel_gate[:], typ_f[:], r01[:, 1:2], None, ALU.mult))
                c.then(nc.vector.tensor_scalar(typ_f[:], typ_f[:], -1.0, 1.0, ALU.mult, ALU.add))
                c.then(nc.vector.scalar_tensor_tensor(k.rel_gate[:], typ_f[:], r01[:, 0:1], k.rel_gate[:], ALU.mult, ALU.add))
                dve.wait_ge(s_x, 48)
                layer_norm(c, k.xs, big, h, mean, std, s_var, s_std, s_h)
                c.then(nc.vector.tensor_tensor(big[:], h[:], bc(a_r[:, 0, :], 1, HI), ALU.mult))
                c.then(nc.vector.tensor_reduce(gate[:], big[:], AX.X, ALU.add))
                split3(c, k.parts[0][:, :, 1, :], gate[:], gate_r[:])
                c.then(nc.vector.tensor_copy(k.parts[1][:, :, 1, :], k.parts[0][:, :, 1, :]))
                dve.wait_ge(s_fold, 1)
                c.then(nc.vector.tensor_copy(k.node_w[:, 2 * D:2 * D + QW], q_fold[0:D, 0:QW]))


def onehots(k, c, cols, b):
    c.mark(k.nc.vector.tensor_tensor(k.lo_hot[b][:], bc(k.iota_b[:], 1, T), bc(k.lo_b[:, cols], 2, P), ALU.is_equal))
    c.mark(k.nc.vector.tensor_tensor(k.hi_hot[b][:], bc(k.iota_b[:, 0:HI], 1, T), bc(k.hi_b[:, cols], 2, HI), ALU.is_equal))


def histogram(k):
    nc = k.nc
    with ExitStack() as ctx:
        tile, bank, sem = helpers(k, ctx)
        total = tile("total", [P, HI])
        upto = tile("upto", [P, HI])
        end = tile("end", [P, HI])
        zeros = tile("zeros", [P, P], BF16)
        counts = bank("counts")
        below = bank("below")
        totals = bank("totals")
        s_zeros, s_hot, s_counted, s_all, s_cnt, s_pre, s_dve = (
            sem(n) for n in ("s_zeros", "s_hot0", "s_counted", "s_all", "s_cnt", "s_pre", "s_dve1"))
        with nc.Block() as block:
            @block.vector
            def _(dve):
                hot = Chain(dve, s_hot, 4)
                nc.vector.memset(zeros[:], 0.0).then_inc(s_zeros, 1)

                def body(i):
                    hot.begin(i)
                    for b in range(2):
                        wait(dve, s_counted, 2 * i + b - 1)
                        onehots(k, hot, bass.ds(i * 2 * T + b * T, T), b)
                    hot.end()

                loop(dve, body)
                c = Chain(dve, s_dve)
                dve.wait_ge(s_all, 1)
                nc.vector.tensor_copy(k.cnt[:], counts[:, 0:HI]).then_inc(s_cnt, 1)
                dve.wait_ge(s_pre, 1)
                c.then(nc.vector.tensor_copy(total[:], totals[:, 0:HI]))
                c.then(nc.vector.tensor_tensor_scan(upto[:], k.ones[:, 0:HI], total[:], 0.0, ALU.mult, ALU.add))
                c.then(nc.vector.tensor_tensor(upto[:], upto[:], total[:], ALU.subtract))
                c.then(nc.vector.tensor_tensor(k.start[:], upto[:], below[:, 0:HI], ALU.add))
                c.then(nc.vector.tensor_tensor(end[:], k.start[:], k.cnt[:], ALU.add))
                c.mark(nc.vector.tensor_scalar(k.filled[:], k.cnt[:], 1.0, None, ALU.min))
                c.mark(nc.vector.tensor_scalar(k.last_at[:], end[:], -1.0, 0.0, ALU.add, ALU.max))

            @block.tensor
            def _(pe):
                pe.wait_ge(s_zeros, 1)
                nc.tensor.matmul(counts[:, 0:HI], zeros[:], zeros[:, 0:HI], start=True, stop=False)

                def body(i):
                    for b in range(2):
                        pe.wait_ge(s_hot, 4 * i + 2 * b + 2)
                        for t in range(T):
                            last = nc.tensor.matmul(counts[:, 0:HI], k.lo_hot[b][:, t, :], k.hi_hot[b][:, t, :], start=False, stop=False)
                        last.then_inc(s_counted, 1)

                loop(pe, body)
                nc.tensor.matmul(counts[:, 0:HI], zeros[:], zeros[:, 0:HI], start=False, stop=True).then_inc(s_all, 1)
                pe.wait_ge(s_cnt, 1)
                nc.tensor.matmul(below[:, 0:HI], k.less[:], k.cnt[:], start=True, stop=True)
                nc.tensor.matmul(totals[:, 0:HI], k.ones[:], k.cnt[:], start=True, stop=True).then_inc(s_pre, 1)


def sort(k):
    nc = k.nc
    with ExitStack() as ctx:
        tile, bank, sem = helpers(k, ctx)
        lo_hot_t = [tile(f"lo_hot_t{b}", [P, G * P], BF16) for b in range(2)]
        hist = [tile(f"hist{b}", [P, G, HI], BF16) for b in range(2)]
        earlier = [tile(f"earlier{b}", [P, G, P], BF16) for b in range(2)]
        less_b = tile("less_b", [P, P], BF16)
        rest = tile("rest", [P, HI])
        picked = tile("picked", [P, G, 2, HI])
        place_gate = tile("place_gate", [P, G, 2])
        place = [tile(f"place{b}", [P, T], I32) for b in range(2)]
        logit = [tile(f"logit{b}", [P, T]) for b in range(2)]
        stage = [tile(f"stage{b}", [P, T, EC]) for b in range(2)]
        rec = [tile(f"rec{b}", [P, T, REC]) for b in range(2)]
        zero_q = tile("zero_q", [P, T * QW])
        p_t = [bank(f"p_t{b}", BF16) for b in range(2)]
        p_hist = bank("p_hist")
        p_same = [bank(f"p_same{b}") for b in range(2)]
        p_place = bank("p_place")
        p_look = [bank(f"p_look{b}") for b in range(2)]
        s_less, s_hot, s_init, s_t, s_hist, s_t_copied, s_hist_copied, s_same, s_parts = (
            sem(n) for n in ("s_less", "s_hot1", "s_init", "s_t", "s_hist", "s_t_copied", "s_hist_copied", "s_same", "s_parts"))
        s_placed, s_earlier, s_look, s_picked, s_chunk, s_filled, s_gated, s_dve, s_passed = (
            sem(n) for n in ("s_placed", "s_earlier", "s_look", "s_picked", "s_chunk", "s_filled", "s_gated", "s_dve2", "s_passed"))
        s_attr = [sem(f"s_attr{b}") for b in range(2)]
        s_sent = [sem(f"s_sent{b}") for b in range(2)]
        s_zq = sem("s_zq")
        s_zq_set = sem("s_zq_set")
        attr_v = k.attr[0:FULL * P, :].rearrange("(p t) c -> p t c", t=FULL)
        q_starts_v = by_run(k.q_starts)

        def size(g):
            return min(G, T - g * G)

        with nc.Block() as block:
            @block.sync
            def _(sp):
                sp.wait_ge(s_zq_set, 1)

                def body(i):
                    for b in range(2):
                        n = 2 * i + b
                        wait(sp, s_filled, n - 1)
                        t0 = i * 2 * T + b * T
                        have = T - 1 if at_end(i, b) else T
                        sp.dma_start(stage[b][:, 0:have, :], attr_v[:, bass.ds(t0, have), :]).then_inc(s_attr[b], 16)
                        sp.dma_start(q_starts_v[:, bass.ds(t0, T), :], zero_q[:].rearrange("p (t c) -> p t c", c=QW)).then_inc(s_zq, 16)

                loop(sp, body)
                sp.wait_ge(s_zq, 16 * CHUNKS)
                for b in range(2):
                    sp.wait_ge(s_sent[b], SCATTERED * PAIRS)

            @block.gpsimd
            def _(pool):
                def body(i):
                    for b in range(2):
                        n = 2 * i + b
                        pool.wait_ge(s_gated, n + 1)
                        pool.sem_inc(s_passed, 1)
                        for t in range(T):
                            nc.gpsimd.indirect_dma_start(
                                k.records, bass.IndirectOffsetOnAxis(ap=place[b][:, t:t + 1], axis=0),
                                rec[b][:, t, :], None).then_inc(s_sent[b], 16)

                loop(pool, body)

            @block.tensor
            def _(pe):
                pe.wait_ge(s_less, 1)
                nc.tensor.matmul(p_place[:, 0:HI], k.ident[:], k.start[:], start=True, stop=True).then_inc(s_placed, 1)

                def look(q, b, g):
                    qb = (b * GROUPS + g) % 2
                    pe.wait_ge(s_earlier, q + 1)
                    pe.wait_ge(s_hist_copied, q + 1)
                    wait(pe, s_picked, q - 1)
                    for j in range(size(g)):
                        t = g * G + j
                        at = lo_hot_t[qb][:, j * P:(j + 1) * P]
                        to = p_look[qb][:, j * 2 * HI:j * 2 * HI + HI]
                        both = p_look[qb][:, j * 2 * HI:(j + 1) * 2 * HI]
                        for part in range(3):
                            nc.tensor.matmul(both, at, k.parts[qb][:, part, :, :], start=(part == 0), stop=False)
                        for e in range(j):
                            nc.tensor.matmul(to, at, hist[qb][:, e, :], start=False, stop=False)
                        last = nc.tensor.matmul(to, earlier[qb][:, j, :], k.hi_hot[b][:, t, :], start=False, stop=True)
                    last.then_inc(s_look, 1)

                def body(i):
                    for b in range(2):
                        pe.wait_ge(s_hot, 4 * i + 2 * b + 2)
                        for g in range(GROUPS):
                            q = i * 2 * GROUPS + b * GROUPS + g
                            qb = (b * GROUPS + g) % 2
                            for j in range(size(g)):
                                last = nc.tensor.transpose(p_t[qb][:, j * P:(j + 1) * P], k.lo_hot[b][:, g * G + j, :], k.identb[:])
                            last.then_inc(s_t, 1)
                            wait(pe, s_hist_copied, q)
                            for j in range(size(g)):
                                last = nc.tensor.matmul(p_hist[:, j * HI:(j + 1) * HI], k.lo_hot[b][:, g * G + j, :], k.hi_hot[b][:, g * G + j, :], start=True, stop=True)
                            last.then_inc(s_hist, 1)
                            pe.wait_ge(s_t_copied, q + 1)
                            for j in range(size(g)):
                                at = lo_hot_t[qb][:, j * P:(j + 1) * P]
                                last = nc.tensor.matmul(p_same[qb][:, j * P:(j + 1) * P], at, at, start=True, stop=True)
                            last.then_inc(s_same, 1)
                            pe.wait_ge(s_parts, q + 1)
                            for j in range(size(g)):
                                last = nc.tensor.matmul(p_place[:, 0:HI], k.lo_hot[b][:, g * G + j, :], k.hi_hot[b][:, g * G + j, :],
                                                        start=False, stop=True, skip_group_check=True)
                            last.then_inc(s_placed, 1)
                            if g > 0:
                                look(q - 1, b, g - 1)
                            elif not at_start(i, b):
                                look(q - 1, 1 - b, GROUPS - 1)

                loop(pe, body)
                look(CHUNKS * GROUPS - 1, 1, GROUPS - 1)

            @block.scalar
            def _(act):
                def gate(n, b):
                    act.wait_ge(s_chunk, n + 1)
                    nc.scalar.activation(rec[b][:, :, GATE], logit[b][:], ACT.Sigmoid).then_inc(s_gated, 1)

                def fill(i, b):
                    n = 2 * i + b
                    act.wait_ge(s_attr[b], 16 * (i + 1))
                    wait(act, s_sent[b], SCATTERED * i)
                    cols = bass.ds(i * 2 * T + b * T, T)
                    nc.scalar.copy(rec[b][:, :, DST], k.dst_f[:, cols])
                    nc.scalar.copy(rec[b][:, :, SRC], k.src_f[:, cols])
                    have = T - 1 if at_end(i, b) else T
                    if have < T:
                        nc.scalar.copy(rec[b][:, have, 0:EC], k.last_attr[:])
                    nc.scalar.copy(rec[b][:, 0:have, 0:EC], stage[b][:, 0:have, :]).then_inc(s_filled, 1)

                def body(i):
                    for b in range(2):
                        n = 2 * i + b
                        for g in range(GROUPS):
                            q = i * 2 * GROUPS + b * GROUPS + g
                            qb = (b * GROUPS + g) % 2
                            wait(act, s_look, q - 1)
                            act.wait_ge(s_t, q + 1)
                            nc.scalar.copy(lo_hot_t[qb][:, 0:size(g) * P], p_t[qb][:, 0:size(g) * P]).then_inc(s_t_copied, 1)
                            act.wait_ge(s_hist, q + 1)
                            nc.scalar.copy(hist[qb][:, 0:size(g), :], p_hist[:, 0:size(g) * HI].rearrange("p (g h) -> p g h", h=HI)).then_inc(s_hist_copied, 1)
                            if g == 2 and not at_start(i, b):
                                gate(n - 1, 1 - b)
                            if g == 4:
                                fill(i, b)

                loop(act, body)
                gate(CHUNKS - 1, 1)

            @block.vector
            def _(dve):
                c = Chain(dve, s_dve, 2 * (6 * GROUPS - 1))
                hot = Chain(dve, s_hot, 4)
                nc.vector.memset(zero_q[:], 0.0).then_inc(s_zq_set, 1)
                for b in range(2):
                    nc.vector.memset(rec[b][:, :, GATE + 1:REC], 0.0).then_inc(s_less, 1)
                nc.vector.tensor_copy(less_b[:], k.less[:]).then_inc(s_less, 1)
                dve.wait_ge(s_less, 3)

                def pick(q, i, b, g, t0):
                    qb = (b * GROUPS + g) % 2
                    n = size(g)
                    dve.wait_ge(s_look, q + 1)
                    nc.vector.tensor_tensor(
                        picked[:, 0:n, :, :], p_look[qb][:, 0:n * 2 * HI].rearrange("p (g a h) -> p g a h", a=2, h=HI),
                        bc(k.hi_hot[b][:, g * G:g * G + n, :], 2, 2), ALU.mult).then_inc(s_picked, 1)
                    dve.wait_ge(s_picked, q + 1)
                    c.then(nc.vector.tensor_reduce(place_gate[:, 0:n, :], picked[:, 0:n, :, :], AX.X, ALU.add))
                    if g == 0:
                        wait(dve, s_sent[b], SCATTERED * i)
                    c.then(nc.vector.tensor_copy(place[b][:, g * G:g * G + n], place_gate[:, 0:n, 0]))
                    ins = nc.vector.tensor_tensor(logit[b][:, g * G:g * G + n], place_gate[:, 0:n, 1],
                                                  k.rel_gate[:, bass.ds(t0 + g * G, n)], ALU.add)
                    if g < GROUPS - 1:
                        c.then(ins)
                    else:
                        ins.then_inc(s_chunk, 1)

                def body(i):
                    c.begin(i)
                    hot.begin(i)
                    for b in range(2):
                        t0 = i * 2 * T + b * T
                        wait(dve, s_look, (2 * i + b - 1) * GROUPS)
                        onehots(k, hot, bass.ds(t0, T), b)
                        for g in range(GROUPS):
                            q = i * 2 * GROUPS + b * GROUPS + g
                            qb = (b * GROUPS + g) % 2
                            wait(dve, s_look, q - 1)
                            dve.wait_ge(s_placed, q + 1)
                            parts = k.parts[qb][:, :, 0, :]
                            c.then(nc.vector.tensor_copy(parts[:, 0, :], p_place[:, 0:HI]))
                            c.then(nc.vector.tensor_tensor(rest[:], p_place[:, 0:HI], parts[:, 0, :], ALU.subtract))
                            c.then(nc.vector.tensor_copy(parts[:, 1, :], rest[:]))
                            nc.vector.tensor_tensor(parts[:, 2, :], rest[:], parts[:, 1, :], ALU.subtract).then_inc(s_parts, 1)
                            dve.wait_ge(s_same, q + 1)
                            n = size(g)
                            nc.vector.tensor_tensor(
                                earlier[qb][:, 0:n, :], p_same[qb][:, 0:n * P].rearrange("p (g e) -> p g e", e=P),
                                bc(less_b[:], 1, n), ALU.mult).then_inc(s_earlier, 1)
                            if g > 0:
                                pick(q - 1, i, b, g - 1, t0)
                            elif b > 0:
                                pick(q - 1, i, 0, GROUPS - 1, t0 - T)
                            elif not at_start(i):
                                pick(q - 1, i - 1, 1, GROUPS - 1, t0 - T)
                    c.end()
                    hot.end()

                loop(dve, body)
                c.begin(PAIRS)
                pick(CHUNKS * GROUPS - 1, PAIRS - 1, 1, GROUPS - 1, NT - T)


def relation_layer(k):
    nc = k.nc
    with ExitStack() as ctx:
        tile, bank, sem = helpers(k, ctx)
        rows = tile("rows", [P, 1 + NT])
        rec = [tile(f"rec_r{b}", [P, T, REC]) for b in range(2)]
        idx = [tile(f"idx_r{b}", [P, T], I32) for b in range(2)]
        got = [tile(f"got_r{b}", [P, T, D]) for b in range(2)]
        keep = [tile(f"keep_r{b}", [P, D, T1]) for b in range(2)]
        add = tile("add_r", [P, D, T1])
        state = [tile(f"state_r{b}", [P, D, T1]) for b in range(2)]
        packed = [tile(f"packed_r{b}", [P, T, D]) for b in range(2)]
        s_zero, s_idx, s_add, s_state, s_keep, s_packed, s_dve, s_passed = (
            sem(n) for n in ("s_zero_r", "s_idx_r", "s_add_r", "s_state_r", "s_keep_r", "s_packed_r", "s_dve_r", "s_passed_r"))
        s_rec, s_got, s_store = ([sem(f"{n}{b}") for b in range(2)] for n in ("s_rec_r", "s_got_r", "s_store_r"))
        records_v, sums_v = by_run(k.records), by_run(k.sums0)

        with nc.Block() as block:
            @block.sync
            def _(sp):
                def body(i):
                    for b in range(2):
                        wait(sp, s_state, 2 * i + b - 1)
                        sp.dma_start(rec[b][:], records_v[:, bass.ds(i * 2 * T + b * T, T), :]).then_inc(s_rec[b], 16)

                loop(sp, body)

            @block.gpsimd
            def _(pool):
                def body(i):
                    for b in range(2):
                        n = 2 * i + b
                        wait(pool, s_add, n - 1)
                        pool.wait_ge(s_idx, n + 1)
                        pool.sem_inc(s_passed, 1)
                        for t in range(T):
                            nc.gpsimd.indirect_dma_start(
                                got[b][:, t, :], None, k.h_table,
                                bass.IndirectOffsetOnAxis(ap=idx[b][:, t:t + 1], axis=0)).then_inc(s_got[b], 16)

                loop(pool, body)

            @block.scalar
            def _(act):
                def body(i):
                    for b in range(2):
                        n = 2 * i + b
                        cols = bass.ds(i * 2 * T + b * T, T)
                        act.wait_ge(s_idx, n + 1)
                        if at_start(i, b):
                            act.wait_ge(s_zero, 4)
                        wait(act, s_state, n - 1)
                        nc.scalar.copy(keep[b][:, :, 1:T1], bc(k.same[:, cols], 1, D)).then_inc(s_keep, 1)
                        act.wait_ge(s_state, n + 1)
                        wait(act, s_store[b], 16 * i)
                        nc.scalar.copy(packed[b][:], state[b][:, :, 1:T1].rearrange("p d t -> p t d")).then_inc(s_packed, 1)
                        act.wait_ge(s_packed, n + 1)
                        act.dma_start(sums_v[:, cols, :], packed[b][:]).then_inc(s_store[b], 16)

                loop(act, body)
                for b in range(2):
                    act.wait_ge(s_store[b], 16 * PAIRS)

            @block.vector
            def _(dve):
                c = Chain(dve, s_dve, 2 * 4)

                def prepare(n, i, b):
                    t0 = i * 2 * T + b * T
                    dve.wait_ge(s_rec[b], 16 * (i + 1))
                    if at_start(i, b):
                        c.mark(nc.vector.tensor_copy(rows[:, 0:1], rec[b][:, 0:1, SRC]))
                    c.mark(nc.vector.tensor_copy(idx[b][:], rec[b][:, :, DST]))
                    c.mark(nc.vector.tensor_copy(k.dst_s[:, bass.ds(t0, T)], rec[b][:, :, DST]))
                    c.then(nc.vector.tensor_copy(rows[:, bass.ds(t0 + 1, T)], rec[b][:, :, SRC]))
                    nc.vector.tensor_tensor(k.same[:, bass.ds(t0, T)], rows[:, bass.ds(t0 + 1, T)],
                                            rows[:, bass.ds(t0, T)], ALU.is_equal).then_inc(s_idx, 1)

                def scan(n, i, b):
                    dve.wait_ge(s_got[b], SCATTERED * (i + 1))
                    if at_start(i, b):
                        c.mark(nc.vector.memset(add[:, :, 0:1], 0.0))
                    else:
                        c.mark(nc.vector.tensor_copy(add[:, :, 0:1], state[1 - b][:, :, T:T1]))
                    nc.vector.tensor_tensor(add[:, :, 1:T1], got[b][:].rearrange("p t d -> p d t"),
                                            bc(rec[b][:, :, GATE], 1, D), ALU.mult).then_inc(s_add, 1)
                    c.wait()
                    dve.wait_ge(s_add, n + 1)
                    dve.wait_ge(s_keep, n + 1)
                    wait(dve, s_packed, n - 1)
                    nc.vector.tensor_tensor_scan(state[b][:].rearrange("p d t -> p (d t)"), keep[b][:].rearrange("p d t -> p (d t)"),
                                                 add[:].rearrange("p d t -> p (d t)"), 0.0, ALU.mult, ALU.add).then_inc(s_state, 1)
                    dve.wait_ge(s_state, n + 1)

                for b in range(2):
                    nc.vector.memset(keep[b][:, :, 0:1], 0.0).then_inc(s_zero, 2)
                c.begin(0)
                prepare(0, 0, 0)

                def body(i):
                    if not at_start(i):
                        c.begin(i)
                    for b in range(2):
                        n = 2 * i + b
                        if b == 0:
                            prepare(n + 1, i, 1)
                        elif not at_end(i, b):
                            prepare(n + 1, i + 1, 0)
                        scan(n, i, b)
                    if not at_end(i):
                        c.end()

                loop(dve, body)
                c.wait()
                c.mark(nc.vector.tensor_copy(k.first_row[:], rows[:, 1:2]))
                c.mark(nc.vector.tensor_copy(k.last_row[:], rows[:, NT:NT + 1]))
                c.then(nc.vector.tensor_copy(k.tail0[:], state[1][:, :, T]))


def relation_nodes(k):
    nc = k.nc
    R = 7
    assert HI % R == 0
    with ExitStack() as ctx:
        tile, bank, sem = helpers(k, ctx)
        iota_i = tile("iota_rows", [P, ROWS], I32)
        nxt, prv = tile("nxt", [P, 1]), tile("prv", [P, 1])
        first_f = tile("first_f", [P, HI])
        rowid = tile("rowid", [P, HI])
        rowid_i = tile("rowid_i", [P, HI], I32)
        first_at = tile("first_at", [P, HI], I32)
        sums = tile("sums_n", [P, HI, D])
        h = tile("h1", [P, HI, D])
        kvq = tile("kvq", [P, HI, 2 * D + QW])
        feat = [tile(f"feat{b}", [D, R * P]) for b in range(2)]
        mean, std = tile("mean1", [P, HI]), tile("std1", [P, HI])
        first_i = tile("first_i", [P, 1], I32)
        p_tail = [bank(f"p_tail{b}") for b in range(2)]
        p_f = [bank(f"p_f{b}") for b in range(4)]
        p_out = [bank(f"p_out{b}") for b in range(2)]
        (s_set, s_shift, s_iota, s_sums, s_own, s_tail, s_added, s_f, s_feat, s_out, s_z, s_tanh, s_x, s_var, s_std, s_h,
         s_f2, s_feat2, s_node, s_kvq, s_y, s_tab, s_first, s_sent, s_init, s_dve) = (
            sem(n + "_n") for n in ("s_set", "s_shift", "s_iota", "s_sums", "s_own", "s_tail", "s_added", "s_f", "s_feat",
                                    "s_out", "s_z", "s_tanh", "s_x", "s_var", "s_std", "s_h", "s_f2", "s_feat2", "s_node",
                                    "s_kvq", "s_y", "s_tab", "s_first", "s_sent", "s_init", "s_dve"))

        with nc.Block() as block:
            @block.sync
            def _(sp):
                sp.wait_ge(s_set, 2)
                with nc.allow_non_contiguous_dma(reason="a column, one partition on"):
                    sp.dma_start(nxt[0:P - 1, :], k.first_row[1:P, :]).then_inc(s_shift, 16)
                    sp.dma_start(prv[1:P, :], k.last_row[0:P - 1, :]).then_inc(s_shift, 16)
                sp.wait_ge(s_kvq, HI)
                sp.dma_start(by_node(k.q_table), kvq[:, :, 2 * D:2 * D + QW]).then_inc(s_tab, 16)
                sp.dma_start(by_node(k.kv_table), kvq[:, :, 0:2 * D]).then_inc(s_tab, 16)
                sp.wait_ge(s_tab, 32)

            @block.gpsimd
            def _(pool):
                for hi in range(HI):
                    nc.gpsimd.indirect_dma_start(
                        sums[:, hi, :], None, k.sums0,
                        bass.IndirectOffsetOnAxis(ap=k.last_at[:, hi:hi + 1], axis=0)).then_inc(s_sums, 16)
                nc.gpsimd.iota(iota_i[:], [[1, ROWS]], base=0, channel_multiplier=0).then_inc(s_iota, 1)
                nc.gpsimd.iota(rowid_i[:], [[P, HI]], base=0, channel_multiplier=1).then_inc(s_iota, 1)
                pool.wait_ge(s_first, 1)
                pool.wait_ge(s_kvq, HI)
                for hi in range(HI):
                    nc.gpsimd.indirect_dma_start(
                        k.q_starts, bass.IndirectOffsetOnAxis(ap=first_at[:, hi:hi + 1], axis=0),
                        kvq[:, hi, 2 * D:2 * D + QW], None).then_inc(s_sent, 16)
                pool.wait_ge(s_tab, 32)
                nc.gpsimd.indirect_dma_start(
                    k.q_init[:], None, k.q_table,
                    bass.IndirectOffsetOnAxis(ap=first_i[:, 0:1], axis=0)).then_inc(s_init, 16)
                pool.wait_ge(s_sent, 16 * HI)

            @block.tensor
            def _(pe):
                pe.wait_ge(s_own, 1)
                for r in range(R):
                    if r >= 2:
                        pe.wait_ge(s_added, r - 1)
                    for j in range(R):
                        hi = r * R + j
                        last = nc.tensor.matmul(p_tail[r % 2][:, j * D:(j + 1) * D], k.own[:, hi * P:(hi + 1) * P], k.tail0[:], start=True, stop=True)
                    last.then_inc(s_tail, 1)

                def transposes(r, of, free, done):
                    if r >= 2:
                        pe.wait_ge(free, r - 1)
                    for j in range(R):
                        last = nc.tensor.transpose(p_f[2 * (r % 2) + j // 4][0:D, (j % 4) * P:(j % 4 + 1) * P], of[:, r * R + j, :], k.ident[:])
                    last.then_inc(done, 1)

                pe.wait_ge(s_added, R)
                transposes(0, sums, s_feat, s_f)
                for r in range(R):
                    if r + 1 < R:
                        transposes(r + 1, sums, s_feat, s_f)
                    pe.wait_ge(s_feat, r + 1)
                    if r >= 2:
                        pe.wait_ge(s_z, r - 1)
                    for j in range(R):
                        last = nc.tensor.matmul(p_out[r % 2][:, j * D:(j + 1) * D], feat[r % 2][:, j * P:(j + 1) * P], k.W_t[:], start=True, stop=True)
                    last.then_inc(s_out, 1)
                pe.wait_ge(s_h, 1)
                transposes(0, h, s_feat2, s_f2)
                for r in range(R):
                    if r + 1 < R:
                        transposes(r + 1, h, s_feat2, s_f2)
                    pe.wait_ge(s_feat2, r + 1)
                    for j in range(R):
                        hi = r * R + j
                        to = (p_out + p_tail)[hi % 4]
                        if hi >= 4:
                            pe.wait_ge(s_kvq, hi - 3)
                            pe.wait_ge(s_y, hi - 3)
                        nc.tensor.matmul(to[:, 0:NODE_W], feat[r % 2][:, j * P:(j + 1) * P], k.node_w[:], start=True, stop=True).then_inc(s_node, 1)

            @block.scalar
            def _(act):
                def copies(r, free, have, done):
                    act.wait_ge(have, r + 1)
                    if r >= 2:
                        act.wait_ge(free, r - 1 if free is s_out else (r - 1) * R)
                    nc.scalar.copy(feat[r % 2][:, 0:4 * P], p_f[2 * (r % 2)][0:D, :])
                    nc.scalar.copy(feat[r % 2][:, 4 * P:R * P], p_f[2 * (r % 2) + 1][0:D, 0:(R - 4) * P]).then_inc(done, 1)

                for r in range(R):
                    copies(r, s_out, s_f, s_feat)
                    act.wait_ge(s_z, r + 1)
                    z = sums[:, r * R:(r + 1) * R, :]
                    nc.scalar.activation(z, z, ACT.Tanh).then_inc(s_tanh, 1)
                act.wait_ge(s_var, 1)
                nc.scalar.activation(std[:], std[:], ACT.Sqrt, bias=k.eps[:], scale=1.0 / D).then_inc(s_std, 1)
                for r in range(R):
                    copies(r, s_node, s_f2, s_feat2)
                    for j in range(R):
                        hi = r * R + j
                        act.wait_ge(s_node, hi + 1)
                        nc.scalar.copy(kvq[:, hi, :], (p_out + p_tail)[hi % 4][:, 0:2 * D + QW]).then_inc(s_kvq, 1)

            @block.vector
            def _(dve):
                c = Chain(dve, s_dve)
                nc.vector.memset(nxt[:], -1.0).then_inc(s_set, 1)
                nc.vector.memset(prv[:], -1.0).then_inc(s_set, 1)
                dve.wait_ge(s_shift, 32)
                c.mark(nc.vector.tensor_tensor(k.goes_on[:], k.last_row[:], nxt[:], ALU.is_equal))
                c.mark(nc.vector.tensor_tensor(k.came_on[:], k.first_row[:], prv[:], ALU.is_equal))
                c.mark(nc.vector.tensor_copy(first_i[:], k.first_row[:]))
                c.wait()
                dve.wait_ge(s_iota, 2)
                nc.vector.tensor_scalar(k.own[:], iota_i[:], k.last_row[:], k.goes_on[:], ALU.is_equal, ALU.mult).then_inc(s_own, 1)
                c.then(nc.vector.tensor_copy(rowid[:], rowid_i[:]))
                c.then(nc.vector.tensor_scalar(rowid[:], rowid[:], float(STREAM), None, ALU.add))
                c.then(nc.vector.tensor_tensor(first_f[:], k.start[:], rowid[:], ALU.subtract))
                c.then(nc.vector.tensor_tensor(first_f[:], first_f[:], k.filled[:], ALU.mult))
                nc.vector.tensor_tensor(first_at[:], first_f[:], rowid[:], ALU.add).then_inc(s_first, 1)
                dve.wait_ge(s_sums, 16 * HI)
                c.then(nc.vector.tensor_tensor(sums[:], sums[:], bc(k.filled[:], 2, D), ALU.mult))
                for r in range(R):
                    dve.wait_ge(s_tail, r + 1)
                    s = sums[:, r * R:(r + 1) * R, :]
                    nc.vector.tensor_tensor(s, s, p_tail[r % 2][:, 0:R * D].rearrange("p (j d) -> p j d", d=D), ALU.add).then_inc(s_added, 1)
                for r in range(R):
                    dve.wait_ge(s_out, r + 1)
                    s = sums[:, r * R:(r + 1) * R, :]
                    nc.vector.tensor_tensor(s, p_out[r % 2][:, 0:R * D].rearrange("p (j d) -> p j d", d=D), bc(k.W_br[:], 1, R), ALU.add).then_inc(s_z, 1)
                    dve.wait_ge(s_tanh, r + 1)
                    xr = k.xs[:, r * R:(r + 1) * R, :]
                    c.then(nc.vector.tensor_tensor(xr, xr, s, ALU.add))
                layer_norm(c, k.xs, sums, h, mean, std, s_var, s_std, s_h)
                for hi in range(HI):
                    dve.wait_ge(s_kvq, hi + 1)
                    nc.vector.tensor_tensor(k.centre[:, hi, :], (p_out + p_tail)[hi % 4][:, 2 * D + QW:NODE_W], k.cen_br[:], ALU.add).then_inc(s_y, 1)
                dve.wait_ge(s_init, 16)
                c.then(nc.vector.tensor_scalar(k.q_init[:], k.q_init[:], k.came_on[:], None, ALU.mult))


def attention_layer(k):
    nc = k.nc
    with ExitStack() as ctx:
        tile, bank, sem = helpers(k, ctx)
        rec = [tile(f"rec_a{b}", [P, T, REC]) for b in range(2)]
        flat_attr = tile("flat_attr", [P, TP, EC])
        qin = [tile(f"qin{b}", [P, T, QW]) for b in range(2)]
        idx = [tile(f"idx_a{b}", [P, T], I32) for b in range(2)]
        got = [tile(f"got_a{b}", [P, T, 2 * D]) for b in range(2)]
        keep = [tile(f"keep_a{b}", [P, QW, T1]) for b in range(2)]
        query = [tile(f"query{b}", [P, QW, T1]) for b in range(2)]
        prod = tile("prod", [P, D, T])
        logit = tile("logit_a", [P, NH, T])
        fresh = tile("fresh", [P, NH, T1])
        logit1 = tile("logit_carry", [P, NH, T1])
        top = [tile(f"top{b}", [P, NH, T1]) for b in range(2)]
        drop = tile("drop", [P, NH, T1])
        below = tile("below_a", [P, NH, T])
        scale = tile("scale", [P, QW, T1])
        add = tile("add_a", [P, QW, T1])
        state = [tile(f"state_a{b}", [P, QW, T1]) for b in range(2)]
        packed = [tile(f"packed_a{b}", [P, T, SW]) for b in range(2)]
        net = [tile(f"net{b}", [P, TP, EC]) for b in range(2)]
        attr_t = tile("attr_t", [P, GROUPS * P])
        relu = tile("relu", [P, GROUPS * P])
        soft = tile("soft", [P, GROUPS * P])
        half = tile("half", [P, 1])
        p_a, p_z, p_w = ([bank(f"{n}{j}") for j in range(2)] for n in ("p_a", "p_z", "p_w"))
        (s_zero, s_idx, s_keep, s_query, s_q, s_value, s_used, s_below, s_exp, s_state, s_packed, s_dve, s_act, s_passed, s_carry) = (
            sem(n + "_a") for n in ("s_zero", "s_idx", "s_keep", "s_query", "s_q", "s_value", "s_used", "s_below", "s_exp",
                                    "s_state", "s_packed", "s_dve", "s_act", "s_passed", "s_carry"))
        s_at, s_at_copied, s_z, s_soft, s_w, s_net, s_flat = (sem(n + "_a") for n in ("s_at", "s_at_copied", "s_z", "s_soft", "s_w", "s_net", "s_flat"))
        s_rec, s_qin, s_got, s_store = ([sem(f"{n}{b}") for b in range(2)] for n in ("s_rec_a", "s_qin", "s_got_a", "s_store_a"))
        records_v, starts_v, sums_v = by_run(k.records), by_run(k.q_starts), by_run(k.sums1)
        halves = ((0, 4 * P, 4), (4 * P, GROUPS * P, GROUPS - 4))

        with nc.Block() as block:
            @block.sync
            def _(sp):
                sp.wait_ge(s_zero, 4)

                def body(i):
                    for b in range(2):
                        n = 2 * i + b
                        cols = bass.ds(i * 2 * T + b * T, T)
                        wait(sp, s_flat, n - 1)
                        sp.dma_start(rec[b][:], records_v[:, cols, :]).then_inc(s_rec[b], 16)
                        wait(sp, s_query, n - 1)
                        sp.dma_start(qin[b][:], starts_v[:, cols, :]).then_inc(s_qin[b], 16)

                loop(sp, body)

            @block.gpsimd
            def _(pool):
                def body(i):
                    for b in range(2):
                        n = 2 * i + b
                        wait(pool, s_used, n - 1)
                        pool.wait_ge(s_idx, n + 1)
                        pool.sem_inc(s_passed, 1)
                        for t in range(T):
                            nc.gpsimd.indirect_dma_start(
                                got[b][:, t, :], None, k.kv_table,
                                bass.IndirectOffsetOnAxis(ap=idx[b][:, t:t + 1], axis=0)).then_inc(s_got[b], 16)

                loop(pool, body)

            @block.tensor
            def _(pe):
                def body(i):
                    for b in range(2):
                        n = 2 * i + b
                        pe.wait_ge(s_flat, n + 1)
                        wait(pe, s_at_copied, n)
                        for g in range(GROUPS):
                            last = nc.tensor.transpose(p_a[g // 4][:, (g % 4) * P:(g % 4 + 1) * P], flat_attr[:, g * G:(g + 1) * G, :].rearrange("p t c -> p (t c)"), k.ident[:])
                        last.then_inc(s_at, 1)
                        pe.wait_ge(s_at_copied, n + 1)
                        wait(pe, s_soft, n)
                        for j, (c0, c1, _) in enumerate(halves):
                            last = nc.tensor.matmul(p_z[j][:, 0:c1 - c0], k.w1_t[:], attr_t[:, c0:c1], start=True, stop=True)
                        last.then_inc(s_z, 1)
                        pe.wait_ge(s_soft, n + 1)
                        wait(pe, s_net, n)
                        for g in range(GROUPS):
                            to = p_w[g // 4][:, (g % 4) * P:(g % 4 + 1) * P]
                            nc.tensor.matmul(to, relu[:, g * P:(g + 1) * P], k.w2_t[:], start=True, stop=False)
                            last = nc.tensor.matmul(to, soft[:, g * P:(g + 1) * P], k.w2_t[:], start=False, stop=True)
                        last.then_inc(s_w, 1)

                loop(pe, body)

            @block.scalar
            def _(act):
                c = Chain(act, s_act, 2 * 4)

                def lay_out(n, i, b):
                    cols = bass.ds(i * 2 * T + b * T, T)
                    wait(act, s_state, n - 1)
                    nc.scalar.copy(keep[b][:, :, 1:T1], bc(k.same[:, cols], 1, QW)).then_inc(s_keep, 1)
                    act.wait_ge(s_qin[b], 16 * (i + 1))
                    wait(act, s_q, n)
                    nc.scalar.copy(query[b][:, :, 1:T1], qin[b][:].rearrange("p t c -> p c t")).then_inc(s_query, 1)

                def networks(n, i, b):
                    act.wait_ge(s_rec[b], 16 * (i + 1))
                    wait(act, s_at, n)
                    nc.scalar.copy(flat_attr[:, 0:T, :], rec[b][:, :, 0:EC]).then_inc(s_flat, 1)
                    act.wait_ge(s_at, n + 1)
                    wait(act, s_z, n)
                    for j, (c0, c1, _) in enumerate(halves):
                        ins = nc.scalar.copy(attr_t[:, c0:c1], p_a[j][:, 0:c1 - c0])
                    ins.then_inc(s_at_copied, 1)
                    act.wait_ge(s_z, n + 1)
                    wait(act, s_w, n)
                    for j, (c0, c1, _) in enumerate(halves):
                        nc.scalar.activation(relu[:, c0:c1], p_z[j][:, 0:c1 - c0], ACT.Relu, bias=k.b1_c[:])
                        c.mark(nc.scalar.activation(soft[:, c0:c1], p_z[j][:, 0:c1 - c0], ACT.Abs, bias=k.b1_c[:]))
                    c.wait()
                    c.then(nc.scalar.activation(soft[:], soft[:], ACT.Exp, scale=-1.0))
                    nc.scalar.activation(soft[:], soft[:], ACT.Ln, bias=half[:], scale=0.5).then_inc(s_soft, 1)

                def finish(n, i, b):
                    act.wait_ge(s_below, n + 1)
                    nc.scalar.activation(add[:, D:QW, 1:T1], below[:], ACT.Exp).then_inc(s_exp, 1)
                    nc.scalar.activation(scale[:, 0:D, :].rearrange("p (h d) t -> p h d t", h=NH), bc(drop[:], 2, HD), ACT.Exp)
                    nc.scalar.activation(scale[:, D:QW, :], drop[:], ACT.Exp).then_inc(s_exp, 1)
                    wait(act, s_store[b], 16 * i)
                    c.mark(nc.scalar.copy(packed[b][:, :, QW:SW], top[b][:, :, 1:T1].rearrange("p h t -> p t h")))
                    act.wait_ge(s_state, n + 1)
                    nc.scalar.copy(packed[b][:, :, 0:QW], state[b][:, :, 1:T1].rearrange("p c t -> p t c")).then_inc(s_packed, 1)
                    act.wait_ge(s_packed, n + 1)
                    c.wait()
                    act.dma_start(sums_v[:, bass.ds(i * 2 * T + b * T, T), :], packed[b][:]).then_inc(s_store[b], 16)

                act.wait_ge(s_zero, 4)
                c.begin(0)
                lay_out(0, 0, 0)
                networks(0, 0, 0)

                def body(i):
                    if not at_start(i):
                        c.begin(i)
                    for b in range(2):
                        n = 2 * i + b
                        if not at_end(i, b):
                            lay_out(n + 1, i + b, 1 - b)
                            networks(n + 1, i + b, 1 - b)
                        finish(n, i, b)
                    if not at_end(i):
                        c.end()

                loop(act, body)
                for b in range(2):
                    act.wait_ge(s_store[b], 16 * PAIRS)

            @block.vector
            def _(dve):
                c = Chain(dve, s_dve, 2 * 11)

                def index(n, i, b):
                    wait(dve, s_got[b], SCATTERED * i)
                    nc.vector.tensor_copy(idx[b][:], k.dst_s[:, bass.ds(i * 2 * T + b * T, T)]).then_inc(s_idx, 1)

                def chunk(n, i, b):
                    cols = bass.ds(i * 2 * T + b * T, T)
                    dve.wait_ge(s_query, n + 1)
                    if at_start(i, b):
                        c.then(nc.vector.tensor_copy(query[b][:, :, 0], k.q_init[:]))
                    else:
                        c.then(nc.vector.tensor_copy(query[b][:, :, 0:1], query[1 - b][:, :, T:T1]))
                    flat = query[b][:].rearrange("p c t -> p (c t)")
                    nc.vector.tensor_tensor_scan(flat, keep[b][:].rearrange("p c t -> p (c t)"), flat, 0.0, ALU.mult, ALU.add).then_inc(s_q, 1)
                    dve.wait_ge(s_w, n + 1)
                    for j, (c0, c1, groups) in enumerate(halves):
                        c.mark(nc.vector.tensor_tensor(
                            net[b][:, c0 // EC:c1 // EC, :], p_w[j][:, 0:c1 - c0].rearrange("p (t o) -> p t o", o=EC),
                            bc(k.b2_r[:], 1, G * groups), ALU.add))
                    c.wait()
                    nc.vector.tensor_scalar(fresh[:, :, 1:T1], bc(k.same[:, cols], 1, NH), -1.0, FAR, ALU.add, ALU.mult).then_inc(s_net, 1)
                    dve.wait_ge(s_got[b], SCATTERED * (i + 1))
                    dve.wait_ge(s_q, n + 1)
                    dve.wait_ge(s_net, n + 1)
                    c.then(nc.vector.tensor_tensor(prod[:], got[b][:, :, 0:D].rearrange("p t c -> p c t"), query[b][:, 0:D, 1:T1], ALU.mult))
                    by_head = prod[:].rearrange("p (h d) t -> p h d t", h=NH)
                    c.then(nc.vector.tensor_tensor(by_head, by_head, bc(net[b][:, 0:T, 0:HD].rearrange("p t o -> p o t"), 1, NH), ALU.mult))
                    c.then(nc.vector.tensor_reduce(logit[:], prod[:].rearrange("p (h d) t -> p h t d", h=NH), AX.X, ALU.add))
                    if at_start(i, b):
                        c.mark(nc.vector.memset(logit1[:, :, 0:1], -FAR))
                    else:
                        c.mark(nc.vector.tensor_copy(logit1[:, :, 0:1], top[1 - b][:, :, T:T1]))
                    c.then(nc.vector.tensor_tensor(logit1[:, :, 1:T1], logit[:], query[b][:, D:QW, 1:T1], ALU.add))
                    wait(dve, s_packed, n - 1)
                    c.then(nc.vector.tensor_tensor_scan(top[b][:].rearrange("p h t -> p (h t)"), fresh[:].rearrange("p h t -> p (h t)"),
                                                        logit1[:].rearrange("p h t -> p (h t)"), -FAR, ALU.add, ALU.max))
                    wait(dve, s_exp, 2 * n)
                    c.then(nc.vector.tensor_tensor(drop[:, :, 1:T1], top[b][:, :, 0:T], top[b][:, :, 1:T1], ALU.subtract))
                    c.mark(nc.vector.tensor_tensor(drop[:, :, 1:T1], drop[:, :, 1:T1], fresh[:, :, 1:T1], ALU.add))
                    c.wait()
                    nc.vector.tensor_tensor(below[:], logit1[:, :, 1:T1], top[b][:, :, 1:T1], ALU.subtract).then_inc(s_below, 1)
                    value = got[b][:, :, D:2 * D].rearrange("p t (h d) -> p h d t", h=NH)
                    nc.vector.tensor_tensor(value, value, bc(net[b][:, 0:T, HD:EC].rearrange("p t o -> p o t"), 1, NH), ALU.mult).then_inc(s_value, 1)
                    dve.wait_ge(s_exp, 2 * n + 1)
                    dve.wait_ge(s_value, n + 1)
                    nc.vector.tensor_tensor(add[:, 0:D, 1:T1].rearrange("p (h d) t -> p h d t", h=NH), value,
                                            bc(add[:, D:QW, 1:T1], 2, HD), ALU.mult).then_inc(s_used, 1)
                    if at_start(i, b):
                        nc.vector.memset(add[:, :, 0:1], 0.0).then_inc(s_carry, 1)
                    else:
                        nc.vector.tensor_copy(add[:, :, 0:1], state[1 - b][:, :, T:T1]).then_inc(s_carry, 1)
                    dve.wait_ge(s_carry, n + 1)
                    dve.wait_ge(s_used, n + 1)
                    dve.wait_ge(s_exp, 2 * n + 2)
                    nc.vector.tensor_tensor_scan(state[b][:].rearrange("p c t -> p (c t)"), scale[:].rearrange("p c t -> p (c t)"),
                                                 add[:].rearrange("p c t -> p (c t)"), 0.0, ALU.mult, ALU.add).then_inc(s_state, 1)
                    dve.wait_ge(s_state, n + 1)

                for b in range(2):
                    c.mark(nc.vector.memset(keep[b][:, :, 0:1], 0.0))
                c.mark(nc.vector.memset(flat_attr[:, T:TP, :], 0.0))
                c.mark(nc.vector.memset(fresh[:, :, 0:1], -FAR))
                c.mark(nc.vector.memset(drop[:, :, 0:1], -FAR))
                c.wait()
                nc.vector.memset(half[:], 0.5).then_inc(s_zero, 4)
                index(0, 0, 0)

                def body(i):
                    if not at_start(i):
                        c.begin(i)
                    for b in range(2):
                        n = 2 * i + b
                        if not at_end(i, b):
                            index(n + 1, i + b, 1 - b)
                        chunk(n, i, b)
                    c.end()

                loop(dve, body)
                c.then(nc.vector.tensor_copy(k.tail1[:, 0:QW], state[1][:, :, T]))
                c.then(nc.vector.tensor_copy(k.tail1[:, QW:SW], top[1][:, :, T]))


def attention_nodes(k):
    nc = k.nc
    R = 7
    W = SW + 1
    assert HI % R == 0 and R * W <= 512
    with ExitStack() as ctx:
        tile, bank, sem = helpers(k, ctx)
        iota_i = tile("iota_rows2", [P, ROWS], I32)
        own = tile("own2", [P, ROWS])
        sums = tile("sums_f", [P, HI, SW])
        parts = tile("parts_f", [P, HI, W])
        vals = tile("vals", [P, 2 + NH])
        diag = tile("diag", [P, 2 + NH, P])
        peer = tile("peer", [P, P])
        peer_later = tile("peer_later", [P, P])
        peer_top = tile("peer_top", [P, NH, P])
        no_peer = tile("no_peer", [P, P])
        top = tile("top_f", [P, NH])
        shrink = tile("shrink", [P, NH])
        later = tile("later", [P, 1])
        pay = tile("pay", [P, W])
        top_r, fac_e, fac_t, tmp = (tile(n, [P, HI, NH]) for n in ("top_r", "fac_e", "fac_t", "tmp_f"))
        empty = tile("empty", [P, HI])
        feat = [tile(f"feat_f{b}", [D, R * P]) for b in range(2)]
        z = tile("z", [P, HI, D])
        soft = tile("soft_f", [P, HI, D])
        half = tile("half_f", [P, 1])
        p_bc = [bank(f"p_bc{b}") for b in range(2)]
        p_f = [bank(f"p_ff{b}") for b in range(4)]
        p_out = [bank(f"p_of{b}") for b in range(2)]
        (s_sums, s_iota, s_diag, s_bc, s_shrink, s_shrunk, s_pay, s_own, s_part, s_part_read, s_fac, s_facd, s_u, s_f, s_feat,
         s_out, s_z, s_soft, s_y, s_f2, s_feat2, s_out2, s_x, s_store, s_dve, s_act, s_half) = (
            sem(n + "_f") for n in ("s_sums", "s_iota", "s_diag", "s_bc", "s_shrink", "s_shrunk", "s_pay", "s_own", "s_part",
                                    "s_part_read", "s_fac", "s_facd", "s_u", "s_f", "s_feat", "s_out", "s_z", "s_soft",
                                    "s_y", "s_f2", "s_feat2", "s_out2", "s_x", "s_store", "s_dve", "s_act", "s_half"))

        with nc.Block() as block:
            @block.sync
            def _(sp):
                sp.wait_ge(s_x, R)
                sp.dma_start(k.out[0:(HI - 1) * P, :].rearrange("(h l) c -> l h c", l=P), k.xs[:, 0:HI - 1, :]).then_inc(s_store, 16)
                sp.dma_start(k.out[(HI - 1) * P:N, :], k.xs[0:LAST_ROWS, HI - 1, :]).then_inc(s_store, 16)
                sp.wait_ge(s_store, 32)

            @block.gpsimd
            def _(pool):
                nc.gpsimd.iota(iota_i[:], [[1, ROWS]], base=0, channel_multiplier=0).then_inc(s_iota, 1)
                for hi in range(HI):
                    nc.gpsimd.indirect_dma_start(
                        sums[:, hi, :], None, k.sums1,
                        bass.IndirectOffsetOnAxis(ap=k.last_at[:, hi:hi + 1], axis=0)).then_inc(s_sums, 16)

            @block.tensor
            def _(pe):
                pe.wait_ge(s_diag, 1)
                nc.tensor.matmul(p_bc[0][:, 0:NH * P], k.ones[:], diag[:, 2:2 + NH, :].rearrange("p v k -> p (v k)"), start=True, stop=True)
                nc.tensor.matmul(p_bc[1][:, 0:2 * P], k.ones[:], diag[:, 0:2, :].rearrange("p v k -> p (v k)"), start=True, stop=True).then_inc(s_bc, 1)
                pe.wait_ge(s_own, 1)
                pe.wait_ge(s_pay, 1)
                for r in range(R):
                    if r >= 2:
                        pe.wait_ge(s_part_read, r - 1)
                    for j in range(R):
                        hi = r * R + j
                        last = nc.tensor.matmul(p_out[r % 2][:, j * W:(j + 1) * W], own[:, hi * P:(hi + 1) * P], pay[:], start=True, stop=True)
                    last.then_inc(s_part, 1)

                def transposes(r, of, free, done):
                    if r >= 2:
                        pe.wait_ge(free, r - 1)
                    for j in range(R):
                        last = nc.tensor.transpose(p_f[2 * (r % 2) + j // 4][0:D, (j % 4) * P:(j % 4 + 1) * P], of[:, r * R + j, 0:D], k.ident[:])
                    last.then_inc(done, 1)

                def products(of, weight, ready, s_t, s_copied, s_done, s_read):
                    pe.wait_ge(ready, 1)
                    transposes(0, of, s_copied, s_t)
                    for r in range(R):
                        if r + 1 < R:
                            transposes(r + 1, of, s_copied, s_t)
                        pe.wait_ge(s_copied, r + 1)
                        if r >= 2:
                            pe.wait_ge(s_read, r - 1)
                        for j in range(R):
                            last = nc.tensor.matmul(p_out[r % 2][:, j * D:(j + 1) * D], feat[r % 2][:, j * P:(j + 1) * P], weight[:], start=True, stop=True)
                        last.then_inc(s_done, 1)

                pe.wait_ge(s_part_read, R)
                products(sums, k.vl_t, s_u, s_f, s_feat, s_out, s_z)
                pe.wait_ge(s_z, R)
                products(z, k.out_t, s_y, s_f2, s_feat2, s_out2, s_x)

            @block.scalar
            def _(act):
                c = Chain(act, s_act)

                def copies(s_t, s_copied, s_done):
                    for r in range(R):
                        act.wait_ge(s_t, r + 1)
                        if r >= 2:
                            act.wait_ge(s_done, r - 1)
                        nc.scalar.copy(feat[r % 2][:, 0:4 * P], p_f[2 * (r % 2)][0:D, :])
                        nc.scalar.copy(feat[r % 2][:, 4 * P:R * P], p_f[2 * (r % 2) + 1][0:D, 0:(R - 4) * P]).then_inc(s_copied, 1)

                act.wait_ge(s_shrink, 1)
                nc.scalar.activation(shrink[:], shrink[:], ACT.Exp).then_inc(s_shrunk, 1)
                act.wait_ge(s_fac, 1)
                nc.scalar.activation(fac_e[:], fac_e[:], ACT.Exp)
                nc.scalar.activation(fac_t[:], fac_t[:], ACT.Exp).then_inc(s_facd, 1)
                copies(s_f, s_feat, s_out)
                act.wait_ge(s_z, R)
                c.then(nc.scalar.activation(soft[:], z[:], ACT.Abs))
                c.then(nc.scalar.activation(soft[:], soft[:], ACT.Exp, scale=-1.0))
                act.wait_ge(s_half, 1)
                nc.scalar.activation(soft[:], soft[:], ACT.Ln, bias=half[:], scale=0.5).then_inc(s_soft, 1)
                copies(s_f2, s_feat2, s_out2)

            @block.vector
            def _(dve):
                c = Chain(dve, s_dve)
                v = nc.vector
                v.memset(half[:], 0.5).then_inc(s_half, 1)
                c.mark(v.tensor_copy(vals[:, 0:1], k.last_row[:]))
                c.mark(v.tensor_copy(vals[:, 1:2], k.goes_on[:]))
                c.then(v.tensor_copy(vals[:, 2:2 + NH], k.tail1[:, QW:SW]))
                v.tensor_tensor(diag[:], bc(k.ident[:], 1, 2 + NH), bc(vals[:], 2, P), ALU.mult).then_inc(s_diag, 1)
                dve.wait_ge(s_iota, 1)
                v.tensor_scalar(own[:], iota_i[:], k.last_row[:], k.goes_on[:], ALU.is_equal, ALU.mult).then_inc(s_own, 1)
                dve.wait_ge(s_bc, 1)
                c.then(v.tensor_scalar(peer[:], p_bc[1][:, 0:P], k.last_row[:], None, ALU.is_equal))
                c.then(v.tensor_tensor(peer[:], peer[:], p_bc[1][:, P:2 * P], ALU.mult))
                c.mark(v.tensor_tensor(peer_later[:], peer[:], k.less[:], ALU.mult))
                c.then(v.tensor_scalar(no_peer[:], peer[:], -1.0, FAR, ALU.add, ALU.mult))
                c.mark(v.tensor_reduce(later[:], peer_later[:], AX.X, ALU.add))
                c.then(v.tensor_tensor(peer_top[:], p_bc[0][:, 0:NH * P].rearrange("p (h k) -> p h k", h=NH), bc(no_peer[:], 1, NH), ALU.add))
                c.then(v.tensor_reduce(top[:], peer_top[:], AX.X, ALU.max))
                c.then(v.tensor_tensor(shrink[:], k.tail1[:, QW:SW], top[:], ALU.subtract))
                v.tensor_scalar(shrink[:], shrink[:], 0.0, None, ALU.min).then_inc(s_shrink, 1)
                c.then(v.tensor_scalar(pay[:, SW:W], later[:], 0.0, None, ALU.is_equal))
                c.mark(v.tensor_scalar(pay[:, QW:SW], top[:], pay[:, SW:W], None, ALU.mult))
                dve.wait_ge(s_shrunk, 1)
                c.mark(v.tensor_tensor(pay[:, 0:D].rearrange("p (h d) -> p h d", h=NH), k.tail1[:, 0:D].rearrange("p (h d) -> p h d", h=NH),
                                       bc(shrink[:], 2, HD), ALU.mult))
                c.wait()
                v.tensor_tensor(pay[:, D:QW], k.tail1[:, D:QW], shrink[:], ALU.mult).then_inc(s_pay, 1)
                for r in range(R):
                    dve.wait_ge(s_part, r + 1)
                    v.tensor_copy(parts[:, r * R:(r + 1) * R, :], p_out[r % 2][:, 0:R * W].rearrange("p (j w) -> p j w", w=W)).then_inc(s_part_read, 1)
                dve.wait_ge(s_part_read, R)
                c.then(v.tensor_scalar(tmp[:], bc(parts[:, :, SW], 2, NH), -1.0, FAR, ALU.add, ALU.mult))
                c.then(v.tensor_tensor(tmp[:], tmp[:], parts[:, :, QW:SW], ALU.add))
                dve.wait_ge(s_sums, 16 * HI)
                c.then(v.tensor_tensor(top_r[:], tmp[:], sums[:, :, QW:SW], ALU.max))
                c.mark(v.tensor_tensor(fac_e[:], sums[:, :, QW:SW], top_r[:], ALU.subtract))
                c.wait()
                v.tensor_tensor(fac_t[:], tmp[:], top_r[:], ALU.subtract).then_inc(s_fac, 1)
                dve.wait_ge(s_facd, 1)
                c.then(v.tensor_tensor(fac_e[:], fac_e[:], bc(k.filled[:], 2, NH), ALU.mult))
                for of, fac in ((sums, fac_e), (parts, fac_t)):
                    u = of[:, :, 0:D].rearrange("p r (h d) -> p r h d", h=NH)
                    for hd in range(NH):
                        c.mark(v.tensor_tensor(u[:, :, hd, :], u[:, :, hd, :], bc(fac[:, :, hd], 2, HD), ALU.mult))
                    c.then(v.tensor_tensor(of[:, :, D:QW], of[:, :, D:QW], fac[:], ALU.mult))
                c.then(v.tensor_tensor(sums[:, :, 0:QW], sums[:, :, 0:QW], parts[:, :, 0:QW], ALU.add))
                c.then(v.tensor_scalar(empty[:], k.filled[:], -1.0, 1.0, ALU.mult, ALU.add))
                c.then(v.tensor_tensor(tmp[:], sums[:, :, D:QW], bc(empty[:], 2, NH), ALU.add))
                c.then(v.reciprocal(tmp[:], tmp[:]))
                u = sums[:, :, 0:D].rearrange("p r (h d) -> p r h d", h=NH)
                for hd in range(NH):
                    c.mark(v.tensor_tensor(u[:, :, hd, :], u[:, :, hd, :], bc(tmp[:, :, hd], 2, HD), ALU.mult))
                c.then(v.tensor_tensor(fac_e[:], sums[:, :, D:QW], tmp[:], ALU.mult))
                for hd in range(NH):
                    c.mark(v.tensor_tensor(soft[:, :, hd * HD:(hd + 1) * HD], bc(k.vl_br[:, hd * HD:(hd + 1) * HD], 1, HI),
                                           bc(fac_e[:, :, hd], 2, HD), ALU.mult))
                c.wait()
                v.tensor_tensor(k.centre[:], k.centre[:], soft[:], ALU.add).then_inc(s_u, 1)
                dve.wait_ge(s_u, 1)
                for r in range(R):
                    dve.wait_ge(s_out, r + 1)
                    rr = slice(r * R, (r + 1) * R)
                    v.tensor_tensor(z[:, rr, :], p_out[r % 2][:, 0:R * D].rearrange("p (j d) -> p j d", d=D), k.centre[:, rr, :], ALU.add).then_inc(s_z, 1)
                dve.wait_ge(s_z, R)
                dve.wait_ge(s_soft, 1)
                v.scalar_tensor_tensor(z[:], z[:], 0.0, soft[:], ALU.max, ALU.add).then_inc(s_y, 1)
                for r in range(R):
                    rr = slice(r * R, (r + 1) * R)
                    c.then(v.tensor_tensor(k.xs[:, rr, :], k.xs[:, rr, :], bc(k.out_br[:], 1, R), ALU.add))
                    dve.wait_ge(s_out2, r + 1)
                    v.tensor_tensor(k.xs[:, rr, :], k.xs[:, rr, :], p_out[r % 2][:, 0:R * D].rearrange("p (j d) -> p j d", d=D), ALU.add).then_inc(s_x, 1)


def build(nc, args, out, phases=9):
    k = Kernel()
    k.nc, k.out = nc, out
    k.x, k.src, k.dst, k.attr, k.etype = args[0:5]
    (k.rel, k.att_w, k.att_b, k.W_w, k.W_b, k.k_w, k.q_w, k.v_w, k.kn_w1, k.kn_b1, k.kn_w2, k.kn_b2,
     k.kl_w, k.kl_b, k.vn_w1, k.vn_b1, k.vn_w2, k.vn_b2, k.vl_w, k.vl_b, k.cen_w, k.cen_b, k.out_w,
     k.out_b) = args[5:]

    def scratch(name, shape):
        return nc.dram_tensor(name, shape, F32, kind="Internal").ap()

    k.records = scratch("records", [STREAM, REC])
    k.h_table = scratch("h_table", [ROWS, D])
    k.kv_table = scratch("kv_table", [ROWS, 2 * D])
    k.q_table = scratch("q_table", [ROWS, QW])
    k.q_starts = scratch("q_starts", [STREAM + ROWS, QW])
    k.sums0 = scratch("sums0", [STREAM, D])
    k.sums1 = scratch("sums1", [STREAM, SW])

    with ExitStack() as ctx:
        tile, _, _ = helpers(k, ctx)
        k.xs = tile("xs", [P, HI, D])
        k.start = tile("start", [P, HI])
        k.filled = tile("filled", [P, HI])
        k.last_at = tile("last_at", [P, HI], I32)
        k.ident = tile("ident", [P, P])
        k.ones = tile("ones", [P, P])
        k.iota_p = tile("iota_p", [P, P])
        k.less = tile("less", [P, P])
        k.eps = tile("eps", [P, 1])
        k.same = tile("same", [P, NT])
        k.dst_s = tile("dst_s", [P, NT], I32)
        k.first_row = tile("first_row", [P, 1])
        k.last_row = tile("last_row", [P, 1])
        k.goes_on = tile("goes_on", [P, 1])
        k.came_on = tile("came_on", [P, 1])
        k.W_t = tile("W_t", [D, D])
        k.node_w = tile("node_w", [D, NODE_W])
        k.vl_t = tile("vl_t", [D, D])
        k.out_t = tile("out_t", [D, D])
        k.w1_t = tile("w1_t", [P, P])
        k.w2_t = tile("w2_t", [P, P])
        k.b1_c = tile("b1_c", [P, 1])
        k.b2_r = tile("b2_r", [P, EC])
        k.W_br = tile("W_br", [P, D])
        k.cen_br = tile("cen_br", [P, D])
        k.vl_br = tile("vl_br", [P, D])
        k.out_br = tile("out_br", [P, D])

        with ExitStack() as sort_ctx:
            node_tile = tile
            tile, _, _ = helpers(k, sort_ctx)
            k.cnt = tile("cnt", [P, HI])
            k.identb = tile("identb", [P, P], BF16)
            k.iota_b = tile("iota_b", [P, P], BF16)
            k.lo_b = tile("lo_b", [P, NT], BF16)
            k.hi_b = tile("hi_b", [P, NT], BF16)
            k.src_f = tile("src_f", [P, NT])
            k.dst_f = tile("dst_f", [P, NT])
            k.rel_gate = tile("rel_gate", [P, NT])
            k.last_attr = tile("last_attr", [P, EC])
            k.parts = [tile(f"parts{b}", [P, 3, 2, HI], BF16) for b in range(2)]
            setup(k)
            k.lo_hot = [tile(f"lo_hot{b}", [P, T, P], BF16) for b in range(2)]
            k.hi_hot = [tile(f"hi_hot{b}", [P, T, HI], BF16) for b in range(2)]
            histogram(k)
            sort(k)
        tile = node_tile
        k.tail1 = tile("tail1", [P, SW])
        k.q_init = tile("q_init", [P, QW])
        k.centre = tile("centre", [P, HI, D])
        with ExitStack() as relation_ctx:
            tile, _, _ = helpers(k, relation_ctx)
            k.tail0 = tile("tail0", [P, D])
            if phases > 1:
                relation_layer(k)
            k.own = tile("own", [P, ROWS])
            if phases > 2:
                relation_nodes(k)
        if phases > 3:
            attention_layer(k)
        if phases > 4:
            attention_nodes(k)


_INS = ["x", "src", "dst", "edge_attr_32", "edge_type_2", "L0_gnn_relation_emb", "L0_gnn_att_w", "L0_gnn_att_b",
        "L0_gnn_W_w", "L0_gnn_W_b", "L1_gnn_k_w", "L1_gnn_q_w", "L1_gnn_v_w", "L1_gnn_wkn_w1", "L1_gnn_wkn_b1",
        "L1_gnn_wkn_w2", "L1_gnn_wkn_b2", "L1_gnn_wkl_w", "L1_gnn_wkl_b", "L1_gnn_wvn_w1", "L1_gnn_wvn_b1",
        "L1_gnn_wvn_w2", "L1_gnn_wvn_b2", "L1_gnn_wvl_w", "L1_gnn_wvl_b", "L1_gnn_cen_w", "L1_gnn_cen_b",
        "L1_gnn_out_w", "L1_gnn_out_b"]


def kernel(**inputs):
    import numpy as np
    import concourse.bacc as bacc
    from concourse.bass_utils import run_bass_kernel_spmd

    nc = bacc.Bacc("TRN2", target_bir_lowering=False, num_devices=1)
    arrays, args = {}, []
    for name in _INS:
        a = np.ascontiguousarray(inputs[name])
        arrays[f"in_{name}"] = a
        args.append(nc.dram_tensor(f"in_{name}", a.shape, mybir.dt.from_np(a.dtype), kind="ExternalInput").ap())
    out = nc.dram_tensor("out", (N, D), F32, kind="ExternalOutput").ap()
    build(nc, args, out)
    return run_bass_kernel_spmd(nc, [arrays], core_ids=[0]).results[0]["out"]
```

```python
from contextlib import ExitStack

import concourse.bass as bass
from concourse import mybir

F32, BF16, I32 = mybir.dt.float32, mybir.dt.bfloat16, mybir.dt.int32
ALU, ACT, AX = mybir.AluOpType, mybir.ActivationFunctionType, mybir.AxisListType

P = 128
N, D, E, EC = 6250, 64, 206250, 32
NH, HD = 4, 16
HI = -(-N // P)
ROWS = HI * P
LAST_ROWS = N - (HI - 1) * P
NT = -(-E // P)
STREAM = NT * P
T = 26
CHUNKS = NT // T
FULL = E // (P * T)
REM_P = (E - FULL * P * T) // T
REM = E - FULL * P * T - REM_P * T
PAIRS = CHUNKS // 2
G = 4
GROUPS = -(-T // G)
TP = GROUPS * G
T1 = T + 1
DST, SRC, GATE, H0 = EC, EC + 1, EC + 2, EC + 4
REC = H0 + D
QW = D + NH
SW = D + 2 * NH
NODE_W = 2 * D + QW + D
FAR = 1e30
EPS = 1e-5
assert CHUNKS * T == NT and PAIRS * 2 == CHUNKS == FULL + 1 and P * T < E and P <= ROWS

SCATTERED = 16 * T


WEIGHTS = ["rel", "att_w", "att_b", "W_w", "W_b", "k_w", "q_w", "v_w", "kn_w1", "kn_b1", "kn_w2",
           "kn_b2", "kl_w", "kl_b", "vn_w1", "vn_b1", "vn_w2", "vn_b2", "vl_w", "vl_b", "cen_w",
           "cen_b", "out_w", "out_b"]


class Kernel:
    pass


def by_node(table):
    return table.rearrange("(h l) c -> l h c", l=P)


def by_run(stream):
    return stream[0:STREAM, :].rearrange("(p t) c -> p t c", t=NT)


def bc(ap, dim, n):
    a = ap.unsqueeze(dim)
    shape = list(a.shape)
    shape[dim] = n
    return a.broadcast_to(shape)


def wait(eng, s, n):
    if not isinstance(n, int) or n > 0:
        eng.wait_ge(s, n)


def loop(eng, body):
    body(0)
    with eng.Fori(1, PAIRS - 1) as i:
        body(i)
    body(PAIRS - 1)


class Chain:

    def __init__(self, eng, s, per_turn=0):
        self.eng, self.s, self.per_turn, self.turn, self.n, self.fewer = eng, s, per_turn, 0, 0, 0

    def begin(self, turn):
        self.turn, self.n = turn, 0

    def mark(self, ins):
        ins.then_inc(self.s, 1)
        self.n += 1

    def wait(self):
        self.eng.wait_ge(self.s, self.turn * self.per_turn + (self.n - self.fewer))

    def then(self, ins):
        self.mark(ins)
        self.wait()

    def end(self):
        if isinstance(self.turn, int) and self.turn == 0:
            self.fewer = self.per_turn - self.n
        else:
            assert self.n == self.per_turn, (self.n, self.per_turn)


def layer_norm(c, xs, work, h, mean, std, s_var, s_std, s_h):
    v = c.eng
    c.then(v.tensor_reduce(mean[:], xs[:], AX.X, ALU.add))
    c.then(v.tensor_scalar(mean[:], mean[:], -1.0 / D, None, ALU.mult))
    c.then(v.tensor_tensor(h[:], xs[:], bc(mean[:], 2, D), ALU.add))
    c.then(v.tensor_tensor(work[:], h[:], h[:], ALU.mult))
    v.tensor_reduce(std[:], work[:], AX.X, ALU.add).then_inc(s_var, 1)
    v.wait_ge(s_std, 1)
    c.then(v.reciprocal(std[:], std[:]))
    v.scalar_tensor_tensor(h[:], h[:], 0.0, bc(std[:], 2, D), ALU.max, ALU.mult).then_inc(s_h, 1)
    v.wait_ge(s_h, 1)


def split3(c, parts, value, rest):
    v = c.eng
    c.then(v.tensor_copy(parts[:, 0, :], value))
    c.then(v.tensor_tensor(rest, value, parts[:, 0, :], ALU.subtract))
    c.then(v.tensor_copy(parts[:, 1, :], rest))
    c.then(v.tensor_tensor(parts[:, 2, :], rest, parts[:, 1, :], ALU.subtract))


def at_start(i, b=0):
    return isinstance(i, int) and i == 0 and b == 0


def at_end(i, b=1):
    return isinstance(i, int) and i == PAIRS - 1 and b == 1


def helpers(k, ctx):
    nc = k.nc

    def tile(name, shape, dt=F32):
        return ctx.enter_context(nc.sbuf_tensor(name, shape, dt))

    def bank(name, dt=F32):
        return ctx.enter_context(nc.psum_tensor(name, [P, 512 if dt == F32 else 1024], dt))

    def sem(name):
        return ctx.enter_context(nc.semaphore(name))

    return tile, bank, sem


def setup(k):
    nc = k.nc
    with ExitStack() as ctx:
        tile, bank, sem = helpers(k, ctx)
        src_i, dst_i, typ_i, tmp_i = (tile(n, [P, NT], I32) for n in ("src_i", "dst_i", "typ_i", "tmp_i"))
        iota_i = tile("iota_i", [P, P], I32)
        number_i = tile("number_i", [P, 1], I32)
        typ_f = tile("typ_f", [P, NT])
        big = tile("big", [P, HI, D])
        h = tile("h0", [P, HI, D])
        mean, std, gate, gate_r = (tile(n, [P, HI]) for n in ("mean0", "std0", "gate", "gate_r"))
        a_r = tile("a_r", [P, 2, D])
        rel_r = tile("rel_r", [P, 2, D])
        b_r = tile("b_r", [P, 1])
        r01 = tile("r01", [P, 2])
        q_nat = tile("q_nat", [D, D])
        kl_bd = tile("kl_bd", [D, QW])
        q_fold = bank("q_fold")
        s_pad, s_zero, s_edges, s_x, s_small, s_w, s_pool = (
            sem(n) for n in ("s_pad", "s_zero", "s_edges", "s_x", "s_small", "s_w", "s_pool"))
        s_var, s_std, s_h, s_fold, s_table, s_dve = (
            sem(n) for n in ("s_var0", "s_std0", "s_h0", "s_fold", "s_table0", "s_dve0"))
        small, loaded = 12, 6 * G + 3 + 6 * NH
        span = tile("span", [P, 2, CHUNKS])
        span_c = tile("span_c", [CHUNKS, 2])
        base_c = tile("base_c", [CHUNKS, 3])
        base_d = tile("base_d", [CHUNKS, CHUNKS])
        base = tile("base", [P, CHUNKS])
        h3 = tile("h3", [P, HI, 3, D], BF16)
        h_rest = tile("h_rest", [P, HI, D])
        p_span = bank("p_span")
        p_base = bank("p_base")
        s_span, s_spanned, s_based, s_base, s_h3 = (sem(n) for n in ("s_span", "s_spanned", "s_based", "s_base", "s_h3"))

        with nc.Block() as block:
            @block.sync
            def _(sp):
                sp.wait_ge(s_pad, 5)
                n, last = FULL * P * T, FULL * T
                for t, v in ((src_i, k.src), (dst_i, k.dst), (typ_i, k.etype)):
                    sp.dma_start(t[:, 0:last].rearrange("p (c t) -> p c t", t=T), v[0:n].rearrange("(c p t) -> p c t", p=P, t=T)).then_inc(s_edges, 16)
                    sp.dma_start(t[0:REM_P, last:NT], v[n:n + REM_P * T].rearrange("(p t) -> p t", t=T)).then_inc(s_edges, 16)
                    sp.dma_start(t[REM_P:REM_P + 1, last:last + REM], v[n + REM_P * T:E].rearrange("(p t) -> p t", p=1)).then_inc(s_edges, 16)
                sp.dma_start(k.xs[:, 0:HI - 1, :], k.x[0:(HI - 1) * P, :].rearrange("(h l) c -> l h c", l=P)).then_inc(s_x, 16)
                sp.dma_start(k.xs[0:LAST_ROWS, HI - 1, :], k.x[(HI - 1) * P:N, :]).then_inc(s_x, 16)
                sp.dma_start(k.last_attr[0:REM_P, :, :], k.attr[n:n + REM_P * T, :].rearrange("(p t) c -> p t c", t=T)).then_inc(s_x, 16)
                sp.dma_start(k.last_attr[REM_P:REM_P + 1, 0:REM, :], k.attr[n + REM_P * T:E, :].rearrange("(p t) c -> p t c", p=1)).then_inc(s_x, 16)
                sp.wait_ge(s_h, 1)
                sp.dma_start(by_node(k.h_table), h[:]).then_inc(s_table, 16)
                sp.wait_ge(s_h3, 1)
                sp.dma_start(k.h3_table.rearrange("(h l) c -> l h c", l=P), h3[:].rearrange("p h a d -> p h (a d)")).then_inc(s_table, 16)
                sp.wait_ge(s_table, 32)

            @block.scalar
            def _(act):
                def row(to, vec, n):
                    act.dma_start(to, vec.rearrange("(a n) -> a n", a=1).broadcast_to([P, n])).then_inc(s_small, 16)

                row(a_r[:].rearrange("p a d -> p (a d)"), k.att_w.rearrange("a b -> (a b)"), 2 * D)
                row(rel_r[:].rearrange("p a d -> p (a d)"), k.rel.rearrange("a b -> (a b)"), 2 * D)
                row(b_r[:], k.att_b, 1)
                for to, b in ((k.W_br, k.W_b), (k.cen_br, k.cen_b), (k.out_br, k.out_b)):
                    row(to[:], b, D)
                row(k.b2_r[:, 0:HD], k.kn_b2, HD)
                row(k.b2_r[:, HD:EC], k.vn_b2, HD)
                row(k.vl_br[:, 0:HD], k.vl_b, HD)
                row(k.vl_br[:, HD:2 * HD], k.vl_b, HD)
                row(k.vl_br[:, 2 * HD:3 * HD], k.vl_b, HD)
                row(k.vl_br[:, 3 * HD:4 * HD], k.vl_b, HD)
                act.wait_ge(s_zero, 6)
                with nc.allow_non_contiguous_dma(reason="small weights, transposed as they are loaded"):
                    def load(to, w):
                        act.dma_start(to, w).then_inc(s_w, 16)

                    for p0 in range(0, P, EC):
                        for c0, w1, w2, b1 in ((0, k.kn_w1, k.kn_w2, k.kn_b1), (HD, k.vn_w1, k.vn_w2, k.vn_b1)):
                            r = slice(p0 + c0, p0 + c0 + HD)
                            load(k.w1_t[p0:p0 + EC, r], w1.rearrange("o i -> i o"))
                            load(k.w2_t[r, r], w2.rearrange("o i -> i o"))
                            load(k.b1_c[r, :], b1.rearrange("(o a) -> o a", a=1))
                    for w, to in ((k.W_w, k.W_t[:]), (k.cen_w, k.node_w[:, 2 * D + QW:NODE_W]), (k.out_w, k.out_t[:])):
                        load(to, w.rearrange("o i -> i o"))
                    for hd in range(NH):
                        r = slice(hd * HD, (hd + 1) * HD)
                        load(k.node_w[r, r], k.k_w[hd].rearrange("o i -> i o"))
                        load(k.node_w[r, D + hd * HD:D + (hd + 1) * HD], k.v_w[hd].rearrange("o i -> i o"))
                        load(k.vl_t[r, r], k.vl_w.rearrange("o i -> i o"))
                        load(q_nat[r, r], k.q_w[hd])
                        load(kl_bd[r, r], k.kl_w)
                        load(kl_bd[r, D + hd:D + hd + 1], k.kl_b.rearrange("(o a) -> o a", a=1))
                act.wait_ge(s_var, 1)
                nc.scalar.activation(std[:], std[:], ACT.Sqrt, bias=k.eps[:], scale=1.0 / D).then_inc(s_std, 1)

            @block.gpsimd
            def _(pool):
                nc.gpsimd.iota(iota_i[:], [[1, P]], base=0, channel_multiplier=0).then_inc(s_pool, 1)
                nc.gpsimd.iota(number_i[:], [[1, 1]], base=0, channel_multiplier=1).then_inc(s_pool, 1)
                nc.gpsimd.memset(k.ident[:], 0.0).then_inc(s_pool, 1)
                nc.gpsimd.memset(k.less[:], 1.0).then_inc(s_pool, 1)
                nc.gpsimd.memset(k.ones[:], 1.0).then_inc(s_pool, 1)
                pool.wait_ge(s_pool, 5)
                nc.gpsimd.affine_select(out=k.ident[:], in_=k.ident[:], compare_op=ALU.not_equal, fill=1.0,
                                        base=0, pattern=[[-1, P]], channel_multiplier=1).then_inc(s_pool, 1)
                nc.gpsimd.affine_select(out=k.less[:], in_=k.less[:], compare_op=ALU.is_gt, fill=0.0,
                                        base=0, pattern=[[1, P]], channel_multiplier=-1).then_inc(s_pool, 1)

            @block.tensor
            def _(pe):
                pe.wait_ge(s_w, 16 * loaded)
                nc.tensor.matmul(q_fold[0:D, 0:QW], q_nat[:], kl_bd[:], start=True, stop=True).then_inc(s_fold, 1)
                pe.wait_ge(s_span, 1)
                nc.tensor.transpose(p_span[0:CHUNKS, 0:P], span[:, 0, :], k.ident[:])
                nc.tensor.transpose(p_span[0:CHUNKS, P:2 * P], span[:, 1, :], k.ident[:]).then_inc(s_spanned, 1)
                pe.wait_ge(s_based, 1)
                nc.tensor.matmul(p_base[:, 0:CHUNKS], k.ones[0:CHUNKS, :], base_d[:], start=True, stop=True)
                nc.tensor.matmul(p_base[:, CHUNKS:CHUNKS + 1], k.ones[0:CHUNKS, :], base_c[:, 2:3], start=True, stop=True).then_inc(s_base, 1)

            @block.vector
            def _(dve):
                c = Chain(dve, s_dve)
                for t, v in ((src_i, ROWS - 1), (dst_i, N - 1), (typ_i, 0)):
                    nc.vector.memset(t[:, NT - T:NT], v).then_inc(s_pad, 1)
                nc.vector.memset(k.xs[:, HI - 1, :], 0.0).then_inc(s_pad, 1)
                nc.vector.memset(k.last_attr[:], 0.0).then_inc(s_pad, 1)
                for t in (k.w1_t, k.w2_t, k.node_w, k.vl_t, q_nat, kl_bd):
                    nc.vector.memset(t[:], 0.0).then_inc(s_zero, 1)
                c.mark(nc.vector.memset(k.eps[:], EPS))
                dve.wait_ge(s_edges, 144)
                c.then(nc.vector.tensor_single_scalar(tmp_i[:], src_i[:], P - 1, ALU.bitwise_and))
                c.then(nc.vector.tensor_copy(k.lo_b[:], tmp_i[:]))
                c.then(nc.vector.tensor_single_scalar(tmp_i[:], src_i[:], 7, ALU.arith_shift_right))
                c.mark(nc.vector.tensor_copy(k.hi_b[:], tmp_i[:]))
                c.mark(nc.vector.tensor_copy(k.src_f[:], src_i[:]))
                c.mark(nc.vector.tensor_copy(k.dst_f[:], dst_i[:]))
                c.mark(nc.vector.tensor_copy(typ_f[:], typ_i[:]))
                dve.wait_ge(s_pool, 7)
                c.mark(nc.vector.tensor_copy(k.iota_p[:], iota_i[:]))
                c.then(nc.vector.tensor_copy(k.iota_b[:], bc(iota_i[:], 2, T)))
                c.mark(nc.vector.tensor_copy(k.less_b[:], k.less[:]))
                c.mark(nc.vector.tensor_copy(k.number[:], number_i[:]))
                c.mark(nc.vector.tensor_copy(k.identb[:], k.ident[:]))
                by_chunk = k.dst_f[:].rearrange("p (c t) -> p c t", t=T)
                c.mark(nc.vector.tensor_reduce(span[:, 0, :], by_chunk, AX.X, ALU.min))
                c.wait()
                nc.vector.tensor_reduce(span[:, 1, :], by_chunk, AX.X, ALU.max).then_inc(s_span, 1)
                dve.wait_ge(s_spanned, 1)
                c.mark(nc.vector.tensor_reduce(span_c[:, 0:1], p_span[0:CHUNKS, 0:P], AX.X, ALU.min))
                c.then(nc.vector.tensor_reduce(span_c[:, 1:2], p_span[0:CHUNKS, P:2 * P], AX.X, ALU.max))
                c.then(nc.vector.tensor_scalar(base_c[:, 0:1], span_c[:, 0:1], float(ROWS - P), None, ALU.min))
                c.mark(nc.vector.tensor_scalar(base_c[:, 2:3], span_c[:, 1:2], base_c[:, 0:1], float(P), ALU.subtract, ALU.is_ge))
                c.wait()
                nc.vector.tensor_scalar(base_d[:], k.ident[0:CHUNKS, 0:CHUNKS], base_c[:, 0:1], None, ALU.mult).then_inc(s_based, 1)
                dve.wait_ge(s_base, 1)
                c.mark(nc.vector.tensor_copy(k.slow[:], p_base[:, CHUNKS:CHUNKS + 1]))
                c.then(nc.vector.tensor_copy(base[:], p_base[:, 0:CHUNKS]))
                c.mark(nc.vector.tensor_copy(k.base_i[:], base[:]))
                c.mark(nc.vector.tensor_tensor(k.dst_in[:].rearrange("p (c t) -> p c t", t=T), by_chunk, bc(base[:], 2, T), ALU.subtract))
                dve.wait_ge(s_small, 16 * small)
                c.then(nc.vector.tensor_tensor(rel_r[:], rel_r[:], bc(a_r[:, 1, :], 1, 2), ALU.mult))
                c.then(nc.vector.tensor_reduce(r01[:], rel_r[:], AX.X, ALU.add))
                c.then(nc.vector.tensor_tensor(r01[:], r01[:], b_r[:].broadcast_to([P, 2]), ALU.add))
                c.then(nc.vector.tensor_scalar(k.rel_gate[:], typ_f[:], r01[:, 1:2], None, ALU.mult))
                c.then(nc.vector.tensor_scalar(typ_f[:], typ_f[:], -1.0, 1.0, ALU.mult, ALU.add))
                c.then(nc.vector.scalar_tensor_tensor(k.rel_gate[:], typ_f[:], r01[:, 0:1], k.rel_gate[:], ALU.mult, ALU.add))
                dve.wait_ge(s_x, 64)
                layer_norm(c, k.xs, big, h, mean, std, s_var, s_std, s_h)
                c.then(nc.vector.tensor_tensor(big[:], h[:], bc(a_r[:, 0, :], 1, HI), ALU.mult))
                c.then(nc.vector.tensor_reduce(gate[:], big[:], AX.X, ALU.add))
                c.then(nc.vector.tensor_copy(h3[:, :, 0, :], h[:]))
                c.then(nc.vector.tensor_tensor(h_rest[:], h[:], h3[:, :, 0, :], ALU.subtract))
                c.then(nc.vector.tensor_copy(h3[:, :, 1, :], h_rest[:]))
                c.wait()
                nc.vector.tensor_tensor(h3[:, :, 2, :], h_rest[:], h3[:, :, 1, :], ALU.subtract).then_inc(s_h3, 1)
                split3(c, k.parts[0][:, :, 1, :], gate[:], gate_r[:])
                c.then(nc.vector.tensor_copy(k.parts[1][:, :, 1, :], k.parts[0][:, :, 1, :]))
                dve.wait_ge(s_fold, 1)
                c.then(nc.vector.tensor_copy(k.node_w[:, 2 * D:2 * D + QW], q_fold[0:D, 0:QW]))


def onehots(k, c, cols, b):
    c.mark(k.nc.vector.tensor_tensor(k.lo_hot[b][:], k.iota_b[:], bc(k.lo_b[:, cols], 1, P), ALU.is_equal))
    c.mark(k.nc.vector.tensor_tensor(k.hi_hot[b][:], k.iota_b[:, 0:HI, :], bc(k.hi_b[:, cols], 1, HI), ALU.is_equal))


def histogram(k):
    nc = k.nc
    with ExitStack() as ctx:
        tile, bank, sem = helpers(k, ctx)
        total = tile("total", [P, HI])
        upto = tile("upto", [P, HI])
        end = tile("end", [P, HI])
        zeros = tile("zeros", [P, P], BF16)
        counts = bank("counts")
        below = bank("below")
        totals = bank("totals")
        s_zeros, s_hot, s_counted, s_all, s_cnt, s_pre, s_dve = (
            sem(n) for n in ("s_zeros", "s_hot0", "s_counted", "s_all", "s_cnt", "s_pre", "s_dve1"))
        with nc.Block() as block:
            @block.vector
            def _(dve):
                hot = Chain(dve, s_hot, 4)
                nc.vector.memset(zeros[:], 0.0).then_inc(s_zeros, 1)

                def body(i):
                    hot.begin(i)
                    for b in range(2):
                        wait(dve, s_counted, 2 * i + b - 1)
                        onehots(k, hot, bass.ds(i * 2 * T + b * T, T), b)
                    hot.end()

                loop(dve, body)
                c = Chain(dve, s_dve)
                dve.wait_ge(s_all, 1)
                nc.vector.tensor_copy(k.cnt[:], counts[:, 0:HI]).then_inc(s_cnt, 1)
                dve.wait_ge(s_pre, 1)
                c.then(nc.vector.tensor_copy(total[:], totals[:, 0:HI]))
                c.then(nc.vector.tensor_tensor_scan(upto[:], k.ones[:, 0:HI], total[:], 0.0, ALU.mult, ALU.add))
                c.then(nc.vector.tensor_tensor(upto[:], upto[:], total[:], ALU.subtract))
                c.then(nc.vector.tensor_tensor(k.start[:], upto[:], below[:, 0:HI], ALU.add))
                c.then(nc.vector.tensor_tensor(end[:], k.start[:], k.cnt[:], ALU.add))
                c.mark(nc.vector.tensor_scalar(k.filled[:], k.cnt[:], 1.0, None, ALU.min))
                c.mark(nc.vector.tensor_scalar(k.last_at[:], end[:], -1.0, 0.0, ALU.add, ALU.max))

            @block.tensor
            def _(pe):
                pe.wait_ge(s_zeros, 1)
                nc.tensor.matmul(counts[:, 0:HI], zeros[:], zeros[:, 0:HI], start=True, stop=False)

                def body(i):
                    for b in range(2):
                        pe.wait_ge(s_hot, 4 * i + 2 * b + 2)
                        for t in range(T):
                            last = nc.tensor.matmul(counts[:, 0:HI], k.lo_hot[b][:, :, t], k.hi_hot[b][:, :, t], start=False, stop=False)
                        last.then_inc(s_counted, 1)

                loop(pe, body)
                nc.tensor.matmul(counts[:, 0:HI], zeros[:], zeros[:, 0:HI], start=False, stop=True).then_inc(s_all, 1)
                pe.wait_ge(s_cnt, 1)
                nc.tensor.matmul(below[:, 0:HI], k.less[:], k.cnt[:], start=True, stop=True)
                nc.tensor.matmul(totals[:, 0:HI], k.ones[:], k.cnt[:], start=True, stop=True).then_inc(s_pre, 1)


def sort(k):
    nc = k.nc
    with ExitStack() as ctx:
        tile, bank, sem = helpers(k, ctx)
        lo_hot_t = [tile(f"lo_hot_t{b}", [P, G * P], BF16) for b in range(2)]
        dst_hot = [tile(f"dst_hot{b}", [P, G * P], BF16) for b in range(2)]
        hist = [tile(f"hist{b}", [P, G, HI], BF16) for b in range(2)]
        earlier = [tile(f"earlier{b}", [P, G, P], BF16) for b in range(2)]
        window = [tile(f"window{b}", [P, 3, D], BF16) for b in range(2)]
        rest = tile("rest", [P, HI])
        picked = tile("picked", [P, G, 2, HI])
        place_gate = [tile(f"place_gate{b}", [P, G, 2]) for b in range(2)]
        place_all = tile("place_all", [P, NT], I32)
        logit_all = tile("logit_all", [P, NT])
        place = [tile(f"place{b}", [P, T], I32) for b in range(2)]
        stage = [tile(f"stage{b}", [P, T, EC]) for b in range(2)]
        h_dst = [tile(f"h_dst{b}", [P, T, D]) for b in range(2)]
        rec = [tile(f"rec{b}", [P, T, REC]) for b in range(2)]
        zero_q = tile("zero_q", [P, T * QW])
        p_t = bank("p_t", BF16)
        p_hist, p_same, p_dst, p_h = (bank(n) for n in ("p_hist", "p_same", "p_dst", "p_h"))
        p_place = bank("p_place")
        p_look = [bank(f"p_look{b}") for b in range(2)]
        (s_set, s_hot, s_t, s_hist, s_t_copied, s_hist_copied, s_same, s_parts, s_placed, s_earlier, s_look, s_picked,
         s_chunk, s_staged, s_ready, s_dve, s_passed, s_dst, s_dst_hot, s_h, s_h_copied, s_zq) = (
            sem(n + "_s") for n in ("s_set", "s_hot", "s_t", "s_hist", "s_t_copied", "s_hist_copied", "s_same", "s_parts",
                                    "s_placed", "s_earlier", "s_look", "s_picked", "s_chunk", "s_staged", "s_ready", "s_dve",
                                    "s_passed", "s_dst", "s_dst_hot", "s_h", "s_h_copied", "s_zq"))
        s_attr, s_sent, s_window = ([sem(f"{n}{b}") for b in range(2)] for n in ("s_attr", "s_sent", "s_window"))
        attr_v = k.attr[0:FULL * P * T, :].rearrange("(c p t) e -> c p t e", p=P, t=T)
        q_starts_v = by_run(k.q_starts)

        def size(g):
            return min(G, T - g * G)

        with nc.Block() as block:
            @block.sync
            def _(sp):
                sp.wait_ge(s_set, 1)

                def body(i):
                    for b in range(2):
                        n = 2 * i + b
                        base = sp.value_load(k.base_i[0:1, bass.ds(n, 1)], min_val=0, max_val=ROWS - P)
                        wait(sp, s_h, (n - 1) * GROUPS)
                        sp.dma_start(window[b][:].rearrange("p a d -> p (a d)"), k.h3_table[bass.ds(base, P), :]).then_inc(s_window[b], 16)
                        if not at_end(i, b):
                            wait(sp, s_staged, n - 1)
                            sp.dma_start(stage[b][:], attr_v[bass.ds(n, 1), :, :, :].rearrange("c p t e -> (c p) t e")).then_inc(s_attr[b], 16)
                        sp.dma_start(q_starts_v[:, bass.ds(n * T, T), :], zero_q[:].rearrange("p (t c) -> p t c", c=QW)).then_inc(s_zq, 16)

                loop(sp, body)
                sp.wait_ge(s_zq, 16 * CHUNKS)
                for b in range(2):
                    sp.wait_ge(s_sent[b], SCATTERED * PAIRS)

            @block.gpsimd
            def _(pool):
                def body(i):
                    for b in range(2):
                        n = 2 * i + b
                        pool.wait_ge(s_ready, n + 1)
                        pool.sem_inc(s_passed, 1)
                        for t in range(T):
                            nc.gpsimd.indirect_dma_start(
                                k.records, bass.IndirectOffsetOnAxis(ap=place[b][:, t:t + 1], axis=0),
                                rec[b][:, t, :], None).then_inc(s_sent[b], 16)

                loop(pool, body)

            @block.tensor
            def _(pe):
                nc.tensor.matmul(p_place[:, 0:HI], k.ident[:], k.start[:], start=True, stop=True).then_inc(s_placed, 1)

                def look(q, i, b, g):
                    qb = (b * GROUPS + g) % 2
                    pe.wait_ge(s_earlier, q + 1)
                    pe.wait_ge(s_hist_copied, q + 1)
                    wait(pe, s_picked, q - 1)
                    for j in range(size(g)):
                        at = lo_hot_t[qb][:, j * P:(j + 1) * P]
                        to = p_look[qb][:, j * 2 * HI:j * 2 * HI + HI]
                        both = p_look[qb][:, j * 2 * HI:(j + 1) * 2 * HI]
                        for part in range(3):
                            nc.tensor.matmul(both, at, k.parts[qb][:, part, :, :], start=(part == 0), stop=False)
                        for e in range(j):
                            nc.tensor.matmul(to, at, hist[qb][:, e, :], start=False, stop=False)
                        last = nc.tensor.matmul(to, earlier[qb][:, j, :], k.hi_hot[b][:, :, g * G + j], start=False, stop=True)
                    last.then_inc(s_look, 1)
                    if g == 0:
                        pe.wait_ge(s_window[b], 16 * (i + 1))
                    pe.wait_ge(s_dst_hot, q + 1)
                    wait(pe, s_h_copied, q)
                    for j in range(size(g)):
                        for part in range(3):
                            last = nc.tensor.matmul(p_h[:, j * D:(j + 1) * D], dst_hot[qb][:, j * P:(j + 1) * P], window[b][:, part, :],
                                                    start=(part == 0), stop=(part == 2))
                    last.then_inc(s_h, 1)

                def body(i):
                    for b in range(2):
                        n = 2 * i + b
                        pe.wait_ge(s_hot, 2 * n + 2)
                        for g in range(GROUPS):
                            q = n * GROUPS + g
                            qb = (b * GROUPS + g) % 2
                            tiles = range(g * G, g * G + size(g))
                            for j, t in enumerate(tiles):
                                last = nc.tensor.transpose(p_t[:, j * P:(j + 1) * P], k.lo_hot[b][:, :, t], k.identb[:])
                            last.then_inc(s_t, 1)
                            wait(pe, s_hist_copied, q)
                            for j, t in enumerate(tiles):
                                last = nc.tensor.matmul(p_hist[:, j * HI:(j + 1) * HI], k.lo_hot[b][:, :, t], k.hi_hot[b][:, :, t], start=True, stop=True)
                            last.then_inc(s_hist, 1)
                            wait(pe, s_dst_hot, q)
                            for j, t in enumerate(tiles):
                                col = k.dst_in[:, bass.ds(n * T + t, 1)]
                                last = nc.tensor.matmul(p_dst[:, j * P:(j + 1) * P], col.broadcast_to([P, P]), k.identb[:], start=True, stop=True)
                            last.then_inc(s_dst, 1)
                            if g > 0:
                                look(q - 1, i, b, g - 1)
                            elif b > 0:
                                look(q - 1, i, 0, GROUPS - 1)
                            elif not at_start(i):
                                look(q - 1, i - 1, 1, GROUPS - 1)
                            pe.wait_ge(s_t_copied, q + 1)
                            for j, t in enumerate(tiles):
                                at = lo_hot_t[qb][:, j * P:(j + 1) * P]
                                last = nc.tensor.matmul(p_same[:, j * P:(j + 1) * P], at, at, start=True, stop=True)
                            last.then_inc(s_same, 1)
                            pe.wait_ge(s_parts, q + 1)
                            for t in tiles:
                                last = nc.tensor.matmul(p_place[:, 0:HI], k.lo_hot[b][:, :, t], k.hi_hot[b][:, :, t],
                                                        start=False, stop=True, skip_group_check=True)
                            last.then_inc(s_placed, 1)

                loop(pe, body)
                look(CHUNKS * GROUPS - 1, PAIRS - 1, 1, GROUPS - 1)

            @block.scalar
            def _(act):
                def h_copy(q, b, g):
                    act.wait_ge(s_h, q + 1)
                    n = size(g)
                    nc.scalar.copy(h_dst[b][:, g * G:g * G + n, :], p_h[:, 0:n * D].rearrange("p (t d) -> p t d", d=D)).then_inc(s_h_copied, 1)

                def assemble(n, i, b):
                    wait(act, s_sent[b], SCATTERED * i)
                    act.wait_ge(s_chunk, n + 1)
                    act.wait_ge(s_h_copied, (n + 1) * GROUPS)
                    cols = bass.ds(n * T, T)
                    nc.scalar.copy(place[b][:], place_all[:, cols])
                    nc.scalar.copy(rec[b][:, :, DST], k.dst_f[:, cols])
                    nc.scalar.copy(rec[b][:, :, SRC], k.src_f[:, cols])
                    nc.scalar.copy(rec[b][:, :, H0:REC], h_dst[b][:])
                    nc.scalar.activation(rec[b][:, :, GATE], logit_all[:, cols], ACT.Sigmoid)
                    if at_end(i, b):
                        nc.scalar.copy(rec[b][:, :, 0:EC], k.last_attr[:]).then_inc(s_ready, 1)
                    else:
                        act.wait_ge(s_attr[b], 16 * (i + 1))
                        nc.scalar.copy(rec[b][:, :, 0:EC], stage[b][:]).then_inc(s_staged, 1)
                        act.wait_ge(s_staged, n + 1)
                        act.sem_inc(s_ready, 1)

                def body(i):
                    for b in range(2):
                        n = 2 * i + b
                        for g in range(GROUPS):
                            q = n * GROUPS + g
                            qb = (b * GROUPS + g) % 2
                            wait(act, s_look, q - 1)
                            act.wait_ge(s_t, q + 1)
                            nc.scalar.copy(lo_hot_t[qb][:, 0:size(g) * P], p_t[:, 0:size(g) * P]).then_inc(s_t_copied, 1)
                            act.wait_ge(s_hist, q + 1)
                            nc.scalar.copy(hist[qb][:, 0:size(g), :], p_hist[:, 0:size(g) * HI].rearrange("p (g h) -> p g h", h=HI)).then_inc(s_hist_copied, 1)
                            if g > 0:
                                h_copy(q - 1, b, g - 1)
                            elif not at_start(i, b):
                                h_copy(q - 1, 1 - b, GROUPS - 1)
                            if g == 3 and not at_start(i, b):
                                assemble(n - 1, i - 1 + b, 1 - b)

                loop(act, body)
                h_copy(CHUNKS * GROUPS - 1, 1, GROUPS - 1)
                assemble(CHUNKS - 1, PAIRS - 1, 1)

            @block.vector
            def _(dve):
                c = Chain(dve, s_dve, 2 * (6 * GROUPS - 1))
                hot = Chain(dve, s_hot, 4)
                nc.vector.memset(zero_q[:], 0.0).then_inc(s_set, 1)
                for b in range(2):
                    c.mark(nc.vector.memset(rec[b][:, :, GATE + 1:H0], 0.0))
                hot.begin(0)
                onehots(k, hot, bass.ds(0, T), 0)

                def pick(q, b, g, gb):
                    n = size(g)
                    dve.wait_ge(s_look, q + 1)
                    nc.vector.tensor_tensor(
                        picked[:, 0:n, :, :], p_look[gb][:, 0:n * 2 * HI].rearrange("p (g a h) -> p g a h", a=2, h=HI),
                        bc(k.hi_hot[b][:, :, g * G:g * G + n].rearrange("p h t -> p t h"), 2, 2), ALU.mult).then_inc(s_picked, 1)

                def summed(q, g, gb):
                    dve.wait_ge(s_picked, q + 1)
                    n = size(g)
                    c.mark(nc.vector.tensor_reduce(place_gate[gb][:, 0:n, :], picked[:, 0:n, :, :], AX.X, ALU.add))

                def placed(g, gb, t0):
                    c.wait()
                    n = size(g)
                    cols = bass.ds(t0 + g * G, n)
                    c.mark(nc.vector.tensor_copy(place_all[:, cols], place_gate[gb][:, 0:n, 0]))
                    if g == GROUPS - 1:
                        c.wait()
                    ins = nc.vector.tensor_tensor(logit_all[:, cols], place_gate[gb][:, 0:n, 1], k.rel_gate[:, cols], ALU.add)
                    if g < GROUPS - 1:
                        c.mark(ins)
                    else:
                        ins.then_inc(s_chunk, 1)

                def behind(n, i, b, g):
                    q = n * GROUPS + g - 2
                    if g >= 2:
                        return q, b, g - 2, n * T
                    return q, 1 - b, GROUPS + g - 2, n * T - T

                def body(i):
                    if not at_start(i):
                        c.begin(i)
                        hot.begin(i)
                    for b in range(2):
                        n = 2 * i + b
                        for g in range(GROUPS):
                            q = n * GROUPS + g
                            qb = (b * GROUPS + g) % 2
                            m = size(g)
                            older = None if at_start(i, b) and g < 2 else behind(n, i, b, g)
                            parts = k.parts[qb][:, :, 0, :]
                            wait(dve, s_look, q - 1)
                            dve.wait_ge(s_placed, q + 1)
                            c.mark(nc.vector.tensor_copy(parts[:, 0, :], p_place[:, 0:HI]))
                            dve.wait_ge(s_dst, q + 1)
                            wait(dve, s_h, q - 1)
                            nc.vector.tensor_scalar(dst_hot[qb][:, 0:m * P], p_dst[:, 0:m * P], k.number[:], None, ALU.is_equal).then_inc(s_dst_hot, 1)
                            c.wait()
                            c.mark(nc.vector.tensor_tensor(rest[:], p_place[:, 0:HI], parts[:, 0, :], ALU.subtract))
                            if older:
                                pick(older[0], older[1], older[2], qb)
                            c.wait()
                            c.mark(nc.vector.tensor_copy(parts[:, 1, :], rest[:]))
                            if older:
                                summed(older[0], older[2], qb)
                            c.wait()
                            nc.vector.tensor_tensor(parts[:, 2, :], rest[:], parts[:, 1, :], ALU.subtract).then_inc(s_parts, 1)
                            if older:
                                placed(older[2], qb, older[3])
                            if g == 3 and not at_end(i, b):
                                wait(dve, s_look, n * GROUPS)
                                onehots(k, hot, bass.ds(n * T + T, T), 1 - b)
                                hot.wait()
                            dve.wait_ge(s_same, q + 1)
                            nc.vector.tensor_tensor(
                                earlier[qb][:, 0:m, :], p_same[:, 0:m * P].rearrange("p (g e) -> p g e", e=P),
                                bc(k.less_b[:], 1, m), ALU.mult).then_inc(s_earlier, 1)
                    if not at_end(i):
                        c.end()
                        hot.end()

                loop(dve, body)
                for g in (GROUPS - 2, GROUPS - 1):
                    q = CHUNKS * GROUPS - GROUPS + g
                    gb = (GROUPS + g) % 2
                    pick(q, 1, g, gb)
                    summed(q, g, gb)
                    placed(g, gb, NT - T)


def relation_layer(k):
    nc = k.nc
    with ExitStack() as ctx:
        tile, bank, sem = helpers(k, ctx)
        rows = tile("rows", [P, 1 + NT])
        rec = [tile(f"rec_r{b}", [P, T, REC]) for b in range(2)]
        idx = [tile(f"idx_r{b}", [P, T], I32) for b in range(2)]
        got = [tile(f"got_r{b}", [P, T, D]) for b in range(2)]
        keep = [tile(f"keep_r{b}", [P, D, T1]) for b in range(2)]
        add = tile("add_r", [P, D, T1])
        state = [tile(f"state_r{b}", [P, D, T1]) for b in range(2)]
        packed = [tile(f"packed_r{b}", [P, T, D]) for b in range(2)]
        s_zero, s_idx, s_add, s_state, s_keep, s_packed, s_dve, s_passed = (
            sem(n) for n in ("s_zero_r", "s_idx_r", "s_add_r", "s_state_r", "s_keep_r", "s_packed_r", "s_dve_r", "s_passed_r"))
        s_rec, s_got, s_store = ([sem(f"{n}{b}") for b in range(2)] for n in ("s_rec_r", "s_got_r", "s_store_r"))
        records_v, sums_v = by_run(k.records), by_run(k.sums0)

        def either(eng, body):
            flag = eng.value_load(k.slow[0:1, 0:1], min_val=0, max_val=CHUNKS)
            with eng.If(flag != 0):
                body(True)
            with eng.Else():
                body(False)

        with nc.Block() as block:
            @block.sync
            def _(sp):
                def body(i):
                    for b in range(2):
                        wait(sp, s_add, 2 * i + b - 1)
                        sp.dma_start(rec[b][:], records_v[:, bass.ds(i * 2 * T + b * T, T), :]).then_inc(s_rec[b], 16)

                loop(sp, body)

            @block.gpsimd
            def _(pool):
                def body(i):
                    for b in range(2):
                        n = 2 * i + b
                        wait(pool, s_add, n - 1)
                        pool.wait_ge(s_idx, n + 1)
                        pool.sem_inc(s_passed, 1)
                        for t in range(T):
                            nc.gpsimd.indirect_dma_start(
                                got[b][:, t, :], None, k.h_table,
                                bass.IndirectOffsetOnAxis(ap=idx[b][:, t:t + 1], axis=0)).then_inc(s_got[b], 16)

                either(pool, lambda gather: loop(pool, body) if gather else pool.sem_inc(s_passed, 1))

            @block.scalar
            def _(act):
                def mark(n, i, b):
                    act.wait_ge(s_idx, n + 1)
                    wait(act, s_state, n - 1)
                    nc.scalar.copy(keep[b][:, :, 1:T1], bc(k.same[:, bass.ds(n * T, T)], 1, D)).then_inc(s_keep, 1)

                act.wait_ge(s_zero, 4)
                mark(0, 0, 0)

                def body(i):
                    for b in range(2):
                        n = 2 * i + b
                        if not at_end(i, b):
                            mark(n + 1, i + b, 1 - b)
                        act.wait_ge(s_state, n + 1)
                        wait(act, s_store[b], 16 * i)
                        nc.scalar.copy(packed[b][:], state[b][:, :, 1:T1].rearrange("p d t -> p t d")).then_inc(s_packed, 1)
                        act.wait_ge(s_packed, n + 1)
                        act.dma_start(sums_v[:, bass.ds(n * T, T), :], packed[b][:]).then_inc(s_store[b], 16)

                loop(act, body)
                for b in range(2):
                    act.wait_ge(s_store[b], 16 * PAIRS)

            @block.vector
            def _(dve):
                c = Chain(dve, s_dve, 2 * 4)

                def prepare(n, i, b):
                    t0 = i * 2 * T + b * T
                    dve.wait_ge(s_rec[b], 16 * (i + 1))
                    if at_start(i, b):
                        c.mark(nc.vector.tensor_copy(rows[:, 0:1], rec[b][:, 0:1, SRC]))
                    c.mark(nc.vector.tensor_copy(idx[b][:], rec[b][:, :, DST]))
                    c.mark(nc.vector.tensor_copy(k.dst_s[:, bass.ds(t0, T)], rec[b][:, :, DST]))
                    c.then(nc.vector.tensor_copy(rows[:, bass.ds(t0 + 1, T)], rec[b][:, :, SRC]))
                    nc.vector.tensor_tensor(k.same[:, bass.ds(t0, T)], rows[:, bass.ds(t0 + 1, T)],
                                            rows[:, bass.ds(t0, T)], ALU.is_equal).then_inc(s_idx, 1)

                def scan(n, i, b, gather):
                    if gather:
                        dve.wait_ge(s_got[b], SCATTERED * (i + 1))
                    h_dst = got[b][:] if gather else rec[b][:, :, H0:REC]
                    if at_start(i, b):
                        c.mark(nc.vector.memset(add[:, :, 0:1], 0.0))
                    else:
                        c.mark(nc.vector.tensor_copy(add[:, :, 0:1], state[1 - b][:, :, T:T1]))
                    nc.vector.tensor_tensor(add[:, :, 1:T1], h_dst.rearrange("p t d -> p d t"),
                                            bc(rec[b][:, :, GATE], 1, D), ALU.mult).then_inc(s_add, 1)
                    c.wait()
                    dve.wait_ge(s_add, n + 1)
                    dve.wait_ge(s_keep, n + 1)
                    wait(dve, s_packed, n - 1)
                    nc.vector.tensor_tensor_scan(state[b][:].rearrange("p d t -> p (d t)"), keep[b][:].rearrange("p d t -> p (d t)"),
                                                 add[:].rearrange("p d t -> p (d t)"), 0.0, ALU.mult, ALU.add).then_inc(s_state, 1)
                    dve.wait_ge(s_state, n + 1)

                for b in range(2):
                    nc.vector.memset(keep[b][:, :, 0:1], 0.0).then_inc(s_zero, 2)

                def way(gather):
                    c.begin(0)
                    c.fewer = 0
                    if gather:
                        prepare(0, 0, 0)

                    def body(i):
                        if not at_start(i):
                            c.begin(i)
                        for b in range(2):
                            n = 2 * i + b
                            if not gather:
                                prepare(n, i, b)
                            elif not at_end(i, b):
                                prepare(n + 1, i + b, 1 - b)
                            scan(n, i, b, gather)
                        if not at_end(i):
                            c.end()

                    loop(dve, body)

                either(dve, way)
                c.wait()
                c.mark(nc.vector.tensor_copy(k.first_row[:], rows[:, 1:2]))
                c.mark(nc.vector.tensor_copy(k.last_row[:], rows[:, NT:NT + 1]))
                c.then(nc.vector.tensor_copy(k.tail0[:], state[1][:, :, T]))


def relation_nodes(k):
    nc = k.nc
    R = 7
    assert HI % R == 0
    with ExitStack() as ctx:
        tile, bank, sem = helpers(k, ctx)
        iota_i = tile("iota_rows", [P, ROWS], I32)
        nxt, prv = tile("nxt", [P, 1]), tile("prv", [P, 1])
        first_f = tile("first_f", [P, HI])
        rowid = tile("rowid", [P, HI])
        rowid_i = tile("rowid_i", [P, HI], I32)
        first_at = tile("first_at", [P, HI], I32)
        sums = tile("sums_n", [P, HI, D])
        h = tile("h1", [P, HI, D])
        kvq = tile("kvq", [P, HI, 2 * D + QW])
        feat = [tile(f"feat{b}", [D, R * P]) for b in range(2)]
        mean, std = tile("mean1", [P, HI]), tile("std1", [P, HI])
        first_i = tile("first_i", [P, 1], I32)
        p_tail = [bank(f"p_tail{b}") for b in range(2)]
        p_f = [bank(f"p_f{b}") for b in range(4)]
        p_out = [bank(f"p_out{b}") for b in range(2)]
        (s_set, s_shift, s_iota, s_sums, s_own, s_tail, s_added, s_f, s_feat, s_out, s_z, s_tanh, s_x, s_var, s_std, s_h,
         s_f2, s_feat2, s_node, s_kvq, s_y, s_tab, s_first, s_sent, s_init, s_dve) = (
            sem(n + "_n") for n in ("s_set", "s_shift", "s_iota", "s_sums", "s_own", "s_tail", "s_added", "s_f", "s_feat",
                                    "s_out", "s_z", "s_tanh", "s_x", "s_var", "s_std", "s_h", "s_f2", "s_feat2", "s_node",
                                    "s_kvq", "s_y", "s_tab", "s_first", "s_sent", "s_init", "s_dve"))

        with nc.Block() as block:
            @block.sync
            def _(sp):
                sp.wait_ge(s_set, 2)
                with nc.allow_non_contiguous_dma(reason="a column, one partition on"):
                    sp.dma_start(nxt[0:P - 1, :], k.first_row[1:P, :]).then_inc(s_shift, 16)
                    sp.dma_start(prv[1:P, :], k.last_row[0:P - 1, :]).then_inc(s_shift, 16)
                sp.wait_ge(s_kvq, HI)
                sp.dma_start(by_node(k.q_table), kvq[:, :, 2 * D:2 * D + QW]).then_inc(s_tab, 16)
                sp.dma_start(by_node(k.kv_table), kvq[:, :, 0:2 * D]).then_inc(s_tab, 16)
                sp.wait_ge(s_tab, 32)

            @block.gpsimd
            def _(pool):
                for hi in range(HI):
                    nc.gpsimd.indirect_dma_start(
                        sums[:, hi, :], None, k.sums0,
                        bass.IndirectOffsetOnAxis(ap=k.last_at[:, hi:hi + 1], axis=0)).then_inc(s_sums, 16)
                nc.gpsimd.iota(iota_i[:], [[1, ROWS]], base=0, channel_multiplier=0).then_inc(s_iota, 1)
                nc.gpsimd.iota(rowid_i[:], [[P, HI]], base=0, channel_multiplier=1).then_inc(s_iota, 1)
                pool.wait_ge(s_first, 1)
                pool.wait_ge(s_kvq, HI)
                for hi in range(HI):
                    nc.gpsimd.indirect_dma_start(
                        k.q_starts, bass.IndirectOffsetOnAxis(ap=first_at[:, hi:hi + 1], axis=0),
                        kvq[:, hi, 2 * D:2 * D + QW], None).then_inc(s_sent, 16)
                pool.wait_ge(s_tab, 32)
                nc.gpsimd.indirect_dma_start(
                    k.q_init[:], None, k.q_table,
                    bass.IndirectOffsetOnAxis(ap=first_i[:, 0:1], axis=0)).then_inc(s_init, 16)
                pool.wait_ge(s_sent, 16 * HI)

            @block.tensor
            def _(pe):
                pe.wait_ge(s_own, 1)
                for r in range(R):
                    if r >= 2:
                        pe.wait_ge(s_added, r - 1)
                    for j in range(R):
                        hi = r * R + j
                        last = nc.tensor.matmul(p_tail[r % 2][:, j * D:(j + 1) * D], k.own[:, hi * P:(hi + 1) * P], k.tail0[:], start=True, stop=True)
                    last.then_inc(s_tail, 1)

                def transposes(r, of, free, done):
                    if r >= 2:
                        pe.wait_ge(free, r - 1)
                    for j in range(R):
                        last = nc.tensor.transpose(p_f[2 * (r % 2) + j // 4][0:D, (j % 4) * P:(j % 4 + 1) * P], of[:, r * R + j, :], k.ident[:])
                    last.then_inc(done, 1)

                pe.wait_ge(s_added, R)
                transposes(0, sums, s_feat, s_f)
                for r in range(R):
                    if r + 1 < R:
                        transposes(r + 1, sums, s_feat, s_f)
                    pe.wait_ge(s_feat, r + 1)
                    if r >= 2:
                        pe.wait_ge(s_z, r - 1)
                    for j in range(R):
                        last = nc.tensor.matmul(p_out[r % 2][:, j * D:(j + 1) * D], feat[r % 2][:, j * P:(j + 1) * P], k.W_t[:], start=True, stop=True)
                    last.then_inc(s_out, 1)
                pe.wait_ge(s_h, 1)
                transposes(0, h, s_feat2, s_f2)
                for r in range(R):
                    if r + 1 < R:
                        transposes(r + 1, h, s_feat2, s_f2)
                    pe.wait_ge(s_feat2, r + 1)
                    for j in range(R):
                        hi = r * R + j
                        to = (p_out + p_tail)[hi % 4]
                        if hi >= 4:
                            pe.wait_ge(s_kvq, hi - 3)
                            pe.wait_ge(s_y, hi - 3)
                        nc.tensor.matmul(to[:, 0:NODE_W], feat[r % 2][:, j * P:(j + 1) * P], k.node_w[:], start=True, stop=True).then_inc(s_node, 1)

            @block.scalar
            def _(act):
                def copies(r, free, have, done):
                    act.wait_ge(have, r + 1)
                    if r >= 2:
                        act.wait_ge(free, r - 1 if free is s_out else (r - 1) * R)
                    nc.scalar.copy(feat[r % 2][:, 0:4 * P], p_f[2 * (r % 2)][0:D, :])
                    nc.scalar.copy(feat[r % 2][:, 4 * P:R * P], p_f[2 * (r % 2) + 1][0:D, 0:(R - 4) * P]).then_inc(done, 1)

                for r in range(R):
                    copies(r, s_out, s_f, s_feat)
                    act.wait_ge(s_z, r + 1)
                    z = sums[:, r * R:(r + 1) * R, :]
                    nc.scalar.activation(z, z, ACT.Tanh).then_inc(s_tanh, 1)
                act.wait_ge(s_var, 1)
                nc.scalar.activation(std[:], std[:], ACT.Sqrt, bias=k.eps[:], scale=1.0 / D).then_inc(s_std, 1)
                for r in range(R):
                    copies(r, s_node, s_f2, s_feat2)
                    for j in range(R):
                        hi = r * R + j
                        act.wait_ge(s_node, hi + 1)
                        nc.scalar.copy(kvq[:, hi, :], (p_out + p_tail)[hi % 4][:, 0:2 * D + QW]).then_inc(s_kvq, 1)

            @block.vector
            def _(dve):
                c = Chain(dve, s_dve)
                nc.vector.memset(nxt[:], -1.0).then_inc(s_set, 1)
                nc.vector.memset(prv[:], -1.0).then_inc(s_set, 1)
                dve.wait_ge(s_shift, 32)
                c.mark(nc.vector.tensor_tensor(k.goes_on[:], k.last_row[:], nxt[:], ALU.is_equal))
                c.mark(nc.vector.tensor_tensor(k.came_on[:], k.first_row[:], prv[:], ALU.is_equal))
                c.mark(nc.vector.tensor_copy(first_i[:], k.first_row[:]))
                c.wait()
                dve.wait_ge(s_iota, 2)
                nc.vector.tensor_scalar(k.own[:], iota_i[:], k.last_row[:], k.goes_on[:], ALU.is_equal, ALU.mult).then_inc(s_own, 1)
                c.then(nc.vector.tensor_copy(rowid[:], rowid_i[:]))
                c.then(nc.vector.tensor_scalar(rowid[:], rowid[:], float(STREAM), None, ALU.add))
                c.then(nc.vector.tensor_tensor(first_f[:], k.start[:], rowid[:], ALU.subtract))
                c.then(nc.vector.tensor_tensor(first_f[:], first_f[:], k.filled[:], ALU.mult))
                nc.vector.tensor_tensor(first_at[:], first_f[:], rowid[:], ALU.add).then_inc(s_first, 1)
                dve.wait_ge(s_sums, 16 * HI)
                c.then(nc.vector.tensor_tensor(sums[:], sums[:], bc(k.filled[:], 2, D), ALU.mult))
                for r in range(R):
                    dve.wait_ge(s_tail, r + 1)
                    s = sums[:, r * R:(r + 1) * R, :]
                    nc.vector.tensor_tensor(s, s, p_tail[r % 2][:, 0:R * D].rearrange("p (j d) -> p j d", d=D), ALU.add).then_inc(s_added, 1)
                for r in range(R):
                    dve.wait_ge(s_out, r + 1)
                    s = sums[:, r * R:(r + 1) * R, :]
                    nc.vector.tensor_tensor(s, p_out[r % 2][:, 0:R * D].rearrange("p (j d) -> p j d", d=D), bc(k.W_br[:], 1, R), ALU.add).then_inc(s_z, 1)
                    dve.wait_ge(s_tanh, r + 1)
                    xr = k.xs[:, r * R:(r + 1) * R, :]
                    c.then(nc.vector.tensor_tensor(xr, xr, s, ALU.add))
                layer_norm(c, k.xs, sums, h, mean, std, s_var, s_std, s_h)
                for hi in range(HI):
                    dve.wait_ge(s_kvq, hi + 1)
                    nc.vector.tensor_tensor(k.centre[:, hi, :], (p_out + p_tail)[hi % 4][:, 2 * D + QW:NODE_W], k.cen_br[:], ALU.add).then_inc(s_y, 1)
                dve.wait_ge(s_init, 16)
                c.then(nc.vector.tensor_scalar(k.q_init[:], k.q_init[:], k.came_on[:], None, ALU.mult))


def attention_layer(k):
    nc = k.nc
    with ExitStack() as ctx:
        tile, bank, sem = helpers(k, ctx)
        attr = [tile(f"attr_a{b}", [P, T, EC]) for b in range(2)]
        flat_attr = tile("flat_attr", [P, TP, EC])
        qin = [tile(f"qin{b}", [P, T, QW]) for b in range(2)]
        idx = [tile(f"idx_a{b}", [P, T], I32) for b in range(2)]
        got = [tile(f"got_a{b}", [P, T, 2 * D]) for b in range(2)]
        keep = [tile(f"keep_a{b}", [P, QW, T1]) for b in range(2)]
        query = [tile(f"query{b}", [P, QW, T1]) for b in range(2)]
        prod = tile("prod", [P, D, T])
        logit = tile("logit_a", [P, NH, T])
        fresh = tile("fresh", [P, NH, T1])
        logit1 = tile("logit_carry", [P, NH, T1])
        top = [tile(f"top{b}", [P, NH, T1]) for b in range(2)]
        drop = tile("drop", [P, NH, T1])
        below = tile("below_a", [P, NH, T])
        scale = tile("scale", [P, QW, T1])
        add = tile("add_a", [P, QW, T1])
        state = [tile(f"state_a{b}", [P, QW, T1]) for b in range(2)]
        packed = [tile(f"packed_a{b}", [P, T, SW]) for b in range(2)]
        net = [tile(f"net{b}", [P, TP, EC]) for b in range(2)]
        attr_t = tile("attr_t", [P, GROUPS * P])
        relu = tile("relu", [P, GROUPS * P])
        soft = tile("soft", [P, GROUPS * P])
        half = tile("half", [P, 1])
        p_a, p_z, p_w = ([bank(f"{n}{j}") for j in range(2)] for n in ("p_a", "p_z", "p_w"))
        (s_zero, s_idx, s_keep, s_query, s_q, s_value, s_used, s_below, s_exp, s_state, s_packed, s_dve, s_act, s_passed, s_carry) = (
            sem(n + "_a") for n in ("s_zero", "s_idx", "s_keep", "s_query", "s_q", "s_value", "s_used", "s_below", "s_exp",
                                    "s_state", "s_packed", "s_dve", "s_act", "s_passed", "s_carry"))
        s_at, s_at_copied, s_z, s_soft, s_w, s_net, s_flat = (sem(n + "_a") for n in ("s_at", "s_at_copied", "s_z", "s_soft", "s_w", "s_net", "s_flat"))
        s_rec, s_qin, s_got, s_store = ([sem(f"{n}{b}") for b in range(2)] for n in ("s_rec_a", "s_qin", "s_got_a", "s_store_a"))
        records_v, starts_v, sums_v = by_run(k.records), by_run(k.q_starts), by_run(k.sums1)
        halves = ((0, 4 * P, 4), (4 * P, GROUPS * P, GROUPS - 4))

        with nc.Block() as block:
            @block.sync
            def _(sp):
                sp.wait_ge(s_zero, 4)

                def body(i):
                    for b in range(2):
                        n = 2 * i + b
                        cols = bass.ds(i * 2 * T + b * T, T)
                        wait(sp, s_flat, n - 1)
                        sp.dma_start(attr[b][:], records_v[:, cols, 0:EC]).then_inc(s_rec[b], 16)
                        wait(sp, s_query, n - 1)
                        sp.dma_start(qin[b][:], starts_v[:, cols, :]).then_inc(s_qin[b], 16)

                loop(sp, body)

            @block.gpsimd
            def _(pool):
                def body(i):
                    for b in range(2):
                        n = 2 * i + b
                        wait(pool, s_used, n - 1)
                        pool.wait_ge(s_idx, n + 1)
                        pool.sem_inc(s_passed, 1)
                        for t in range(T):
                            nc.gpsimd.indirect_dma_start(
                                got[b][:, t, :], None, k.kv_table,
                                bass.IndirectOffsetOnAxis(ap=idx[b][:, t:t + 1], axis=0)).then_inc(s_got[b], 16)

                loop(pool, body)

            @block.tensor
            def _(pe):
                def body(i):
                    for b in range(2):
                        n = 2 * i + b
                        pe.wait_ge(s_flat, n + 1)
                        wait(pe, s_at_copied, n)
                        for g in range(GROUPS):
                            last = nc.tensor.transpose(p_a[g // 4][:, (g % 4) * P:(g % 4 + 1) * P], flat_attr[:, g * G:(g + 1) * G, :].rearrange("p t c -> p (t c)"), k.ident[:])
                        last.then_inc(s_at, 1)
                        pe.wait_ge(s_at_copied, n + 1)
                        wait(pe, s_soft, n)
                        for j, (c0, c1, _) in enumerate(halves):
                            last = nc.tensor.matmul(p_z[j][:, 0:c1 - c0], k.w1_t[:], attr_t[:, c0:c1], start=True, stop=True)
                        last.then_inc(s_z, 1)
                        pe.wait_ge(s_soft, n + 1)
                        wait(pe, s_net, n)
                        for g in range(GROUPS):
                            to = p_w[g // 4][:, (g % 4) * P:(g % 4 + 1) * P]
                            nc.tensor.matmul(to, relu[:, g * P:(g + 1) * P], k.w2_t[:], start=True, stop=False)
                            last = nc.tensor.matmul(to, soft[:, g * P:(g + 1) * P], k.w2_t[:], start=False, stop=True)
                        last.then_inc(s_w, 1)

                loop(pe, body)

            @block.scalar
            def _(act):
                c = Chain(act, s_act, 2 * 4)

                def lay_out(n, i, b):
                    cols = bass.ds(i * 2 * T + b * T, T)
                    wait(act, s_state, n - 1)
                    nc.scalar.copy(keep[b][:, :, 1:T1], bc(k.same[:, cols], 1, QW)).then_inc(s_keep, 1)
                    act.wait_ge(s_qin[b], 16 * (i + 1))
                    wait(act, s_q, n)
                    nc.scalar.copy(query[b][:, :, 1:T1], qin[b][:].rearrange("p t c -> p c t")).then_inc(s_query, 1)

                def networks(n, i, b):
                    act.wait_ge(s_rec[b], 16 * (i + 1))
                    wait(act, s_at, n)
                    nc.scalar.copy(flat_attr[:, 0:T, :], attr[b][:]).then_inc(s_flat, 1)
                    act.wait_ge(s_at, n + 1)
                    wait(act, s_z, n)
                    for j, (c0, c1, _) in enumerate(halves):
                        ins = nc.scalar.copy(attr_t[:, c0:c1], p_a[j][:, 0:c1 - c0])
                    ins.then_inc(s_at_copied, 1)
                    act.wait_ge(s_z, n + 1)
                    wait(act, s_w, n)
                    for j, (c0, c1, _) in enumerate(halves):
                        nc.scalar.activation(relu[:, c0:c1], p_z[j][:, 0:c1 - c0], ACT.Relu, bias=k.b1_c[:])
                        c.mark(nc.scalar.activation(soft[:, c0:c1], p_z[j][:, 0:c1 - c0], ACT.Abs, bias=k.b1_c[:]))
                    c.wait()
                    c.then(nc.scalar.activation(soft[:], soft[:], ACT.Exp, scale=-1.0))
                    nc.scalar.activation(soft[:], soft[:], ACT.Ln, bias=half[:], scale=0.5).then_inc(s_soft, 1)

                def finish(n, i, b):
                    act.wait_ge(s_below, n + 1)
                    nc.scalar.activation(add[:, D:QW, 1:T1], below[:], ACT.Exp).then_inc(s_exp, 1)
                    nc.scalar.activation(scale[:, 0:D, :].rearrange("p (h d) t -> p h d t", h=NH), bc(drop[:], 2, HD), ACT.Exp)
                    nc.scalar.activation(scale[:, D:QW, :], drop[:], ACT.Exp).then_inc(s_exp, 1)
                    wait(act, s_store[b], 16 * i)
                    c.mark(nc.scalar.copy(packed[b][:, :, QW:SW], top[b][:, :, 1:T1].rearrange("p h t -> p t h")))
                    act.wait_ge(s_state, n + 1)
                    nc.scalar.copy(packed[b][:, :, 0:QW], state[b][:, :, 1:T1].rearrange("p c t -> p t c")).then_inc(s_packed, 1)
                    act.wait_ge(s_packed, n + 1)
                    c.wait()
                    act.dma_start(sums_v[:, bass.ds(i * 2 * T + b * T, T), :], packed[b][:]).then_inc(s_store[b], 16)

                act.wait_ge(s_zero, 4)
                c.begin(0)
                lay_out(0, 0, 0)
                networks(0, 0, 0)

                def body(i):
                    if not at_start(i):
                        c.begin(i)
                    for b in range(2):
                        n = 2 * i + b
                        if not at_end(i, b):
                            lay_out(n + 1, i + b, 1 - b)
                            networks(n + 1, i + b, 1 - b)
                        finish(n, i, b)
                    if not at_end(i):
                        c.end()

                loop(act, body)
                for b in range(2):
                    act.wait_ge(s_store[b], 16 * PAIRS)

            @block.vector
            def _(dve):
                c = Chain(dve, s_dve, 2 * 11)

                def index(n, i, b):
                    wait(dve, s_got[b], SCATTERED * i)
                    nc.vector.tensor_copy(idx[b][:], k.dst_s[:, bass.ds(i * 2 * T + b * T, T)]).then_inc(s_idx, 1)

                def chunk(n, i, b):
                    cols = bass.ds(i * 2 * T + b * T, T)
                    dve.wait_ge(s_query, n + 1)
                    if at_start(i, b):
                        c.then(nc.vector.tensor_copy(query[b][:, :, 0], k.q_init[:]))
                    else:
                        c.then(nc.vector.tensor_copy(query[b][:, :, 0:1], query[1 - b][:, :, T:T1]))
                    flat = query[b][:].rearrange("p c t -> p (c t)")
                    nc.vector.tensor_tensor_scan(flat, keep[b][:].rearrange("p c t -> p (c t)"), flat, 0.0, ALU.mult, ALU.add).then_inc(s_q, 1)
                    dve.wait_ge(s_w, n + 1)
                    for j, (c0, c1, groups) in enumerate(halves):
                        c.mark(nc.vector.tensor_tensor(
                            net[b][:, c0 // EC:c1 // EC, :], p_w[j][:, 0:c1 - c0].rearrange("p (t o) -> p t o", o=EC),
                            bc(k.b2_r[:], 1, G * groups), ALU.add))
                    c.wait()
                    nc.vector.tensor_scalar(fresh[:, :, 1:T1], bc(k.same[:, cols], 1, NH), -1.0, FAR, ALU.add, ALU.mult).then_inc(s_net, 1)
                    dve.wait_ge(s_got[b], SCATTERED * (i + 1))
                    dve.wait_ge(s_q, n + 1)
                    dve.wait_ge(s_net, n + 1)
                    c.then(nc.vector.tensor_tensor(prod[:], got[b][:, :, 0:D].rearrange("p t c -> p c t"), query[b][:, 0:D, 1:T1], ALU.mult))
                    by_head = prod[:].rearrange("p (h d) t -> p h d t", h=NH)
                    c.then(nc.vector.tensor_tensor(by_head, by_head, bc(net[b][:, 0:T, 0:HD].rearrange("p t o -> p o t"), 1, NH), ALU.mult))
                    c.then(nc.vector.tensor_reduce(logit[:], prod[:].rearrange("p (h d) t -> p h t d", h=NH), AX.X, ALU.add))
                    if at_start(i, b):
                        c.mark(nc.vector.memset(logit1[:, :, 0:1], -FAR))
                    else:
                        c.mark(nc.vector.tensor_copy(logit1[:, :, 0:1], top[1 - b][:, :, T:T1]))
                    c.then(nc.vector.tensor_tensor(logit1[:, :, 1:T1], logit[:], query[b][:, D:QW, 1:T1], ALU.add))
                    wait(dve, s_packed, n - 1)
                    c.then(nc.vector.tensor_tensor_scan(top[b][:].rearrange("p h t -> p (h t)"), fresh[:].rearrange("p h t -> p (h t)"),
                                                        logit1[:].rearrange("p h t -> p (h t)"), -FAR, ALU.add, ALU.max))
                    wait(dve, s_exp, 2 * n)
                    c.then(nc.vector.tensor_tensor(drop[:, :, 1:T1], top[b][:, :, 0:T], top[b][:, :, 1:T1], ALU.subtract))
                    c.mark(nc.vector.tensor_tensor(drop[:, :, 1:T1], drop[:, :, 1:T1], fresh[:, :, 1:T1], ALU.add))
                    c.wait()
                    nc.vector.tensor_tensor(below[:], logit1[:, :, 1:T1], top[b][:, :, 1:T1], ALU.subtract).then_inc(s_below, 1)
                    value = got[b][:, :, D:2 * D].rearrange("p t (h d) -> p h d t", h=NH)
                    nc.vector.tensor_tensor(value, value, bc(net[b][:, 0:T, HD:EC].rearrange("p t o -> p o t"), 1, NH), ALU.mult).then_inc(s_value, 1)
                    dve.wait_ge(s_exp, 2 * n + 1)
                    dve.wait_ge(s_value, n + 1)
                    nc.vector.tensor_tensor(add[:, 0:D, 1:T1].rearrange("p (h d) t -> p h d t", h=NH), value,
                                            bc(add[:, D:QW, 1:T1], 2, HD), ALU.mult).then_inc(s_used, 1)
                    if at_start(i, b):
                        nc.vector.memset(add[:, :, 0:1], 0.0).then_inc(s_carry, 1)
                    else:
                        nc.vector.tensor_copy(add[:, :, 0:1], state[1 - b][:, :, T:T1]).then_inc(s_carry, 1)
                    dve.wait_ge(s_carry, n + 1)
                    dve.wait_ge(s_used, n + 1)
                    dve.wait_ge(s_exp, 2 * n + 2)
                    nc.vector.tensor_tensor_scan(state[b][:].rearrange("p c t -> p (c t)"), scale[:].rearrange("p c t -> p (c t)"),
                                                 add[:].rearrange("p c t -> p (c t)"), 0.0, ALU.mult, ALU.add).then_inc(s_state, 1)
                    dve.wait_ge(s_state, n + 1)

                for b in range(2):
                    c.mark(nc.vector.memset(keep[b][:, :, 0:1], 0.0))
                c.mark(nc.vector.memset(flat_attr[:, T:TP, :], 0.0))
                c.mark(nc.vector.memset(fresh[:, :, 0:1], -FAR))
                c.mark(nc.vector.memset(drop[:, :, 0:1], -FAR))
                c.wait()
                nc.vector.memset(half[:], 0.5).then_inc(s_zero, 4)
                index(0, 0, 0)

                def body(i):
                    if not at_start(i):
                        c.begin(i)
                    for b in range(2):
                        n = 2 * i + b
                        if not at_end(i, b):
                            index(n + 1, i + b, 1 - b)
                        chunk(n, i, b)
                    c.end()

                loop(dve, body)
                c.then(nc.vector.tensor_copy(k.tail1[:, 0:QW], state[1][:, :, T]))
                c.then(nc.vector.tensor_copy(k.tail1[:, QW:SW], top[1][:, :, T]))


def attention_nodes(k):
    nc = k.nc
    R = 7
    W = SW + 1
    assert HI % R == 0 and R * W <= 512
    with ExitStack() as ctx:
        tile, bank, sem = helpers(k, ctx)
        iota_i = tile("iota_rows2", [P, ROWS], I32)
        own = tile("own2", [P, ROWS])
        sums = tile("sums_f", [P, HI, SW])
        parts = tile("parts_f", [P, HI, W])
        vals = tile("vals", [P, 2 + NH])
        diag = tile("diag", [P, 2 + NH, P])
        peer = tile("peer", [P, P])
        peer_later = tile("peer_later", [P, P])
        peer_top = tile("peer_top", [P, NH, P])
        no_peer = tile("no_peer", [P, P])
        top = tile("top_f", [P, NH])
        shrink = tile("shrink", [P, NH])
        later = tile("later", [P, 1])
        pay = tile("pay", [P, W])
        top_r, fac_e, fac_t, tmp = (tile(n, [P, HI, NH]) for n in ("top_r", "fac_e", "fac_t", "tmp_f"))
        empty = tile("empty", [P, HI])
        feat = [tile(f"feat_f{b}", [D, R * P]) for b in range(2)]
        z = tile("z", [P, HI, D])
        soft = tile("soft_f", [P, HI, D])
        half = tile("half_f", [P, 1])
        p_bc = [bank(f"p_bc{b}") for b in range(2)]
        p_f = [bank(f"p_ff{b}") for b in range(4)]
        p_out = [bank(f"p_of{b}") for b in range(2)]
        (s_sums, s_iota, s_diag, s_bc, s_shrink, s_shrunk, s_pay, s_own, s_part, s_part_read, s_fac, s_facd, s_u, s_f, s_feat,
         s_out, s_z, s_soft, s_y, s_f2, s_feat2, s_out2, s_x, s_store, s_dve, s_act, s_half) = (
            sem(n + "_f") for n in ("s_sums", "s_iota", "s_diag", "s_bc", "s_shrink", "s_shrunk", "s_pay", "s_own", "s_part",
                                    "s_part_read", "s_fac", "s_facd", "s_u", "s_f", "s_feat", "s_out", "s_z", "s_soft",
                                    "s_y", "s_f2", "s_feat2", "s_out2", "s_x", "s_store", "s_dve", "s_act", "s_half"))

        with nc.Block() as block:
            @block.sync
            def _(sp):
                sp.wait_ge(s_x, R)
                sp.dma_start(k.out[0:(HI - 1) * P, :].rearrange("(h l) c -> l h c", l=P), k.xs[:, 0:HI - 1, :]).then_inc(s_store, 16)
                sp.dma_start(k.out[(HI - 1) * P:N, :], k.xs[0:LAST_ROWS, HI - 1, :]).then_inc(s_store, 16)
                sp.wait_ge(s_store, 32)

            @block.gpsimd
            def _(pool):
                nc.gpsimd.iota(iota_i[:], [[1, ROWS]], base=0, channel_multiplier=0).then_inc(s_iota, 1)
                for hi in range(HI):
                    nc.gpsimd.indirect_dma_start(
                        sums[:, hi, :], None, k.sums1,
                        bass.IndirectOffsetOnAxis(ap=k.last_at[:, hi:hi + 1], axis=0)).then_inc(s_sums, 16)

            @block.tensor
            def _(pe):
                pe.wait_ge(s_diag, 1)
                nc.tensor.matmul(p_bc[0][:, 0:NH * P], k.ones[:], diag[:, 2:2 + NH, :].rearrange("p v k -> p (v k)"), start=True, stop=True)
                nc.tensor.matmul(p_bc[1][:, 0:2 * P], k.ones[:], diag[:, 0:2, :].rearrange("p v k -> p (v k)"), start=True, stop=True).then_inc(s_bc, 1)
                pe.wait_ge(s_own, 1)
                pe.wait_ge(s_pay, 1)
                for r in range(R):
                    if r >= 2:
                        pe.wait_ge(s_part_read, r - 1)
                    for j in range(R):
                        hi = r * R + j
                        last = nc.tensor.matmul(p_out[r % 2][:, j * W:(j + 1) * W], own[:, hi * P:(hi + 1) * P], pay[:], start=True, stop=True)
                    last.then_inc(s_part, 1)

                def transposes(r, of, free, done):
                    if r >= 2:
                        pe.wait_ge(free, r - 1)
                    for j in range(R):
                        last = nc.tensor.transpose(p_f[2 * (r % 2) + j // 4][0:D, (j % 4) * P:(j % 4 + 1) * P], of[:, r * R + j, 0:D], k.ident[:])
                    last.then_inc(done, 1)

                def products(of, weight, ready, s_t, s_copied, s_done, s_read):
                    pe.wait_ge(ready, 1)
                    transposes(0, of, s_copied, s_t)
                    for r in range(R):
                        if r + 1 < R:
                            transposes(r + 1, of, s_copied, s_t)
                        pe.wait_ge(s_copied, r + 1)
                        if r >= 2:
                            pe.wait_ge(s_read, r - 1)
                        for j in range(R):
                            last = nc.tensor.matmul(p_out[r % 2][:, j * D:(j + 1) * D], feat[r % 2][:, j * P:(j + 1) * P], weight[:], start=True, stop=True)
                        last.then_inc(s_done, 1)

                pe.wait_ge(s_part_read, R)
                products(sums, k.vl_t, s_u, s_f, s_feat, s_out, s_z)
                pe.wait_ge(s_z, R)
                products(z, k.out_t, s_y, s_f2, s_feat2, s_out2, s_x)

            @block.scalar
            def _(act):
                c = Chain(act, s_act)

                def copies(s_t, s_copied, s_done):
                    for r in range(R):
                        act.wait_ge(s_t, r + 1)
                        if r >= 2:
                            act.wait_ge(s_done, r - 1)
                        nc.scalar.copy(feat[r % 2][:, 0:4 * P], p_f[2 * (r % 2)][0:D, :])
                        nc.scalar.copy(feat[r % 2][:, 4 * P:R * P], p_f[2 * (r % 2) + 1][0:D, 0:(R - 4) * P]).then_inc(s_copied, 1)

                act.wait_ge(s_shrink, 1)
                nc.scalar.activation(shrink[:], shrink[:], ACT.Exp).then_inc(s_shrunk, 1)
                act.wait_ge(s_fac, 1)
                nc.scalar.activation(fac_e[:], fac_e[:], ACT.Exp)
                nc.scalar.activation(fac_t[:], fac_t[:], ACT.Exp).then_inc(s_facd, 1)
                copies(s_f, s_feat, s_out)
                act.wait_ge(s_z, R)
                c.then(nc.scalar.activation(soft[:], z[:], ACT.Abs))
                c.then(nc.scalar.activation(soft[:], soft[:], ACT.Exp, scale=-1.0))
                act.wait_ge(s_half, 1)
                nc.scalar.activation(soft[:], soft[:], ACT.Ln, bias=half[:], scale=0.5).then_inc(s_soft, 1)
                copies(s_f2, s_feat2, s_out2)

            @block.vector
            def _(dve):
                c = Chain(dve, s_dve)
                v = nc.vector
                v.memset(half[:], 0.5).then_inc(s_half, 1)
                c.mark(v.tensor_copy(vals[:, 0:1], k.last_row[:]))
                c.mark(v.tensor_copy(vals[:, 1:2], k.goes_on[:]))
                c.then(v.tensor_copy(vals[:, 2:2 + NH], k.tail1[:, QW:SW]))
                v.tensor_tensor(diag[:], bc(k.ident[:], 1, 2 + NH), bc(vals[:], 2, P), ALU.mult).then_inc(s_diag, 1)
                dve.wait_ge(s_iota, 1)
                v.tensor_scalar(own[:], iota_i[:], k.last_row[:], k.goes_on[:], ALU.is_equal, ALU.mult).then_inc(s_own, 1)
                dve.wait_ge(s_bc, 1)
                c.then(v.tensor_scalar(peer[:], p_bc[1][:, 0:P], k.last_row[:], None, ALU.is_equal))
                c.then(v.tensor_tensor(peer[:], peer[:], p_bc[1][:, P:2 * P], ALU.mult))
                c.mark(v.tensor_tensor(peer_later[:], peer[:], k.less[:], ALU.mult))
                c.then(v.tensor_scalar(no_peer[:], peer[:], -1.0, FAR, ALU.add, ALU.mult))
                c.mark(v.tensor_reduce(later[:], peer_later[:], AX.X, ALU.add))
                c.then(v.tensor_tensor(peer_top[:], p_bc[0][:, 0:NH * P].rearrange("p (h k) -> p h k", h=NH), bc(no_peer[:], 1, NH), ALU.add))
                c.then(v.tensor_reduce(top[:], peer_top[:], AX.X, ALU.max))
                c.then(v.tensor_tensor(shrink[:], k.tail1[:, QW:SW], top[:], ALU.subtract))
                v.tensor_scalar(shrink[:], shrink[:], 0.0, None, ALU.min).then_inc(s_shrink, 1)
                c.then(v.tensor_scalar(pay[:, SW:W], later[:], 0.0, None, ALU.is_equal))
                c.mark(v.tensor_scalar(pay[:, QW:SW], top[:], pay[:, SW:W], None, ALU.mult))
                dve.wait_ge(s_shrunk, 1)
                c.mark(v.tensor_tensor(pay[:, 0:D].rearrange("p (h d) -> p h d", h=NH), k.tail1[:, 0:D].rearrange("p (h d) -> p h d", h=NH),
                                       bc(shrink[:], 2, HD), ALU.mult))
                c.wait()
                v.tensor_tensor(pay[:, D:QW], k.tail1[:, D:QW], shrink[:], ALU.mult).then_inc(s_pay, 1)
                for r in range(R):
                    dve.wait_ge(s_part, r + 1)
                    v.tensor_copy(parts[:, r * R:(r + 1) * R, :], p_out[r % 2][:, 0:R * W].rearrange("p (j w) -> p j w", w=W)).then_inc(s_part_read, 1)
                dve.wait_ge(s_part_read, R)
                c.then(v.tensor_scalar(tmp[:], bc(parts[:, :, SW], 2, NH), -1.0, FAR, ALU.add, ALU.mult))
                c.then(v.tensor_tensor(tmp[:], tmp[:], parts[:, :, QW:SW], ALU.add))
                dve.wait_ge(s_sums, 16 * HI)
                c.then(v.tensor_tensor(top_r[:], tmp[:], sums[:, :, QW:SW], ALU.max))
                c.mark(v.tensor_tensor(fac_e[:], sums[:, :, QW:SW], top_r[:], ALU.subtract))
                c.wait()
                v.tensor_tensor(fac_t[:], tmp[:], top_r[:], ALU.subtract).then_inc(s_fac, 1)
                dve.wait_ge(s_facd, 1)
                c.then(v.tensor_tensor(fac_e[:], fac_e[:], bc(k.filled[:], 2, NH), ALU.mult))
                for of, fac in ((sums, fac_e), (parts, fac_t)):
                    u = of[:, :, 0:D].rearrange("p r (h d) -> p r h d", h=NH)
                    for hd in range(NH):
                        c.mark(v.tensor_tensor(u[:, :, hd, :], u[:, :, hd, :], bc(fac[:, :, hd], 2, HD), ALU.mult))
                    c.then(v.tensor_tensor(of[:, :, D:QW], of[:, :, D:QW], fac[:], ALU.mult))
                c.then(v.tensor_tensor(sums[:, :, 0:QW], sums[:, :, 0:QW], parts[:, :, 0:QW], ALU.add))
                c.then(v.tensor_scalar(empty[:], k.filled[:], -1.0, 1.0, ALU.mult, ALU.add))
                c.then(v.tensor_tensor(tmp[:], sums[:, :, D:QW], bc(empty[:], 2, NH), ALU.add))
                c.then(v.reciprocal(tmp[:], tmp[:]))
                u = sums[:, :, 0:D].rearrange("p r (h d) -> p r h d", h=NH)
                for hd in range(NH):
                    c.mark(v.tensor_tensor(u[:, :, hd, :], u[:, :, hd, :], bc(tmp[:, :, hd], 2, HD), ALU.mult))
                c.then(v.tensor_tensor(fac_e[:], sums[:, :, D:QW], tmp[:], ALU.mult))
                for hd in range(NH):
                    c.mark(v.tensor_tensor(soft[:, :, hd * HD:(hd + 1) * HD], bc(k.vl_br[:, hd * HD:(hd + 1) * HD], 1, HI),
                                           bc(fac_e[:, :, hd], 2, HD), ALU.mult))
                c.wait()
                v.tensor_tensor(k.centre[:], k.centre[:], soft[:], ALU.add).then_inc(s_u, 1)
                dve.wait_ge(s_u, 1)
                for r in range(R):
                    dve.wait_ge(s_out, r + 1)
                    rr = slice(r * R, (r + 1) * R)
                    v.tensor_tensor(z[:, rr, :], p_out[r % 2][:, 0:R * D].rearrange("p (j d) -> p j d", d=D), k.centre[:, rr, :], ALU.add).then_inc(s_z, 1)
                dve.wait_ge(s_z, R)
                dve.wait_ge(s_soft, 1)
                v.scalar_tensor_tensor(z[:], z[:], 0.0, soft[:], ALU.max, ALU.add).then_inc(s_y, 1)
                for r in range(R):
                    rr = slice(r * R, (r + 1) * R)
                    c.then(v.tensor_tensor(k.xs[:, rr, :], k.xs[:, rr, :], bc(k.out_br[:], 1, R), ALU.add))
                    dve.wait_ge(s_out2, r + 1)
                    v.tensor_tensor(k.xs[:, rr, :], k.xs[:, rr, :], p_out[r % 2][:, 0:R * D].rearrange("p (j d) -> p j d", d=D), ALU.add).then_inc(s_x, 1)


def build(nc, args, out, phases=9):
    k = Kernel()
    k.nc, k.out = nc, out
    k.x, k.src, k.dst, k.attr, k.etype = args[0:5]
    (k.rel, k.att_w, k.att_b, k.W_w, k.W_b, k.k_w, k.q_w, k.v_w, k.kn_w1, k.kn_b1, k.kn_w2, k.kn_b2,
     k.kl_w, k.kl_b, k.vn_w1, k.vn_b1, k.vn_w2, k.vn_b2, k.vl_w, k.vl_b, k.cen_w, k.cen_b, k.out_w,
     k.out_b) = args[5:]

    def scratch(name, shape, dt=F32):
        return nc.dram_tensor(name, shape, dt, kind="Internal").ap()

    k.records = scratch("records", [STREAM, REC])
    k.h_table = scratch("h_table", [ROWS, D])
    k.h3_table = scratch("h3_table", [ROWS, 3 * D], BF16)
    k.kv_table = scratch("kv_table", [ROWS, 2 * D])
    k.q_table = scratch("q_table", [ROWS, QW])
    k.q_starts = scratch("q_starts", [STREAM + ROWS, QW])
    k.sums0 = scratch("sums0", [STREAM, D])
    k.sums1 = scratch("sums1", [STREAM, SW])

    with ExitStack() as ctx:
        tile, _, _ = helpers(k, ctx)
        k.xs = tile("xs", [P, HI, D])
        k.start = tile("start", [P, HI])
        k.filled = tile("filled", [P, HI])
        k.last_at = tile("last_at", [P, HI], I32)
        k.ident = tile("ident", [P, P])
        k.ones = tile("ones", [P, P])
        k.iota_p = tile("iota_p", [P, P])
        k.less = tile("less", [P, P])
        k.eps = tile("eps", [P, 1])
        k.same = tile("same", [P, NT])
        k.dst_s = tile("dst_s", [P, NT], I32)
        k.first_row = tile("first_row", [P, 1])
        k.last_row = tile("last_row", [P, 1])
        k.goes_on = tile("goes_on", [P, 1])
        k.came_on = tile("came_on", [P, 1])
        k.slow = tile("slow", [P, 1], I32)
        k.W_t = tile("W_t", [D, D])
        k.node_w = tile("node_w", [D, NODE_W])
        k.vl_t = tile("vl_t", [D, D])
        k.out_t = tile("out_t", [D, D])
        k.w1_t = tile("w1_t", [P, P])
        k.w2_t = tile("w2_t", [P, P])
        k.b1_c = tile("b1_c", [P, 1])
        k.b2_r = tile("b2_r", [P, EC])
        k.W_br = tile("W_br", [P, D])
        k.cen_br = tile("cen_br", [P, D])
        k.vl_br = tile("vl_br", [P, D])
        k.out_br = tile("out_br", [P, D])

        with ExitStack() as sort_ctx:
            node_tile = tile
            tile, _, _ = helpers(k, sort_ctx)
            k.cnt = tile("cnt", [P, HI])
            k.identb = tile("identb", [P, P], BF16)
            k.iota_b = tile("iota_b", [P, P, T], BF16)
            k.less_b = tile("less_b", [P, P], BF16)
            k.number = tile("number", [P, 1])
            k.base_i = tile("base_i", [P, CHUNKS], I32)
            k.dst_in = tile("dst_in", [P, NT], BF16)
            k.lo_b = tile("lo_b", [P, NT], BF16)
            k.hi_b = tile("hi_b", [P, NT], BF16)
            k.src_f = tile("src_f", [P, NT])
            k.dst_f = tile("dst_f", [P, NT])
            k.rel_gate = tile("rel_gate", [P, NT])
            k.last_attr = tile("last_attr", [P, T, EC])
            k.parts = [tile(f"parts{b}", [P, 3, 2, HI], BF16) for b in range(2)]
            setup(k)
            k.lo_hot = [tile(f"lo_hot{b}", [P, P, T], BF16) for b in range(2)]
            k.hi_hot = [tile(f"hi_hot{b}", [P, HI, T], BF16) for b in range(2)]
            histogram(k)
            sort(k)
        tile = node_tile
        k.tail1 = tile("tail1", [P, SW])
        k.q_init = tile("q_init", [P, QW])
        k.centre = tile("centre", [P, HI, D])
        with ExitStack() as relation_ctx:
            tile, _, _ = helpers(k, relation_ctx)
            k.tail0 = tile("tail0", [P, D])
            if phases > 1:
                relation_layer(k)
            k.own = tile("own", [P, ROWS])
            if phases > 2:
                relation_nodes(k)
        if phases > 3:
            attention_layer(k)
        if phases > 4:
            attention_nodes(k)


_INS = ["x", "src", "dst", "edge_attr_32", "edge_type_2", "L0_gnn_relation_emb", "L0_gnn_att_w", "L0_gnn_att_b",
        "L0_gnn_W_w", "L0_gnn_W_b", "L1_gnn_k_w", "L1_gnn_q_w", "L1_gnn_v_w", "L1_gnn_wkn_w1", "L1_gnn_wkn_b1",
        "L1_gnn_wkn_w2", "L1_gnn_wkn_b2", "L1_gnn_wkl_w", "L1_gnn_wkl_b", "L1_gnn_wvn_w1", "L1_gnn_wvn_b1",
        "L1_gnn_wvn_w2", "L1_gnn_wvn_b2", "L1_gnn_wvl_w", "L1_gnn_wvl_b", "L1_gnn_cen_w", "L1_gnn_cen_b",
        "L1_gnn_out_w", "L1_gnn_out_b"]


def kernel(**inputs):
    import numpy as np
    import concourse.bacc as bacc
    from concourse.bass_utils import run_bass_kernel_spmd

    nc = bacc.Bacc("TRN2", target_bir_lowering=False, num_devices=1)
    arrays, args = {}, []
    for name in _INS:
        a = np.ascontiguousarray(inputs[name])
        arrays[f"in_{name}"] = a
        args.append(nc.dram_tensor(f"in_{name}", a.shape, mybir.dt.from_np(a.dtype), kind="ExternalInput").ap())
    out = nc.dram_tensor("out", (N, D), F32, kind="ExternalOutput").ap()
    build(nc, args, out)
    return run_bass_kernel_spmd(nc, [arrays], core_ids=[0]).results[0]["out"]
```

```python
from contextlib import ExitStack

import concourse.bass as bass
from concourse import mybir

F32, BF16, I32 = mybir.dt.float32, mybir.dt.bfloat16, mybir.dt.int32
ALU, ACT, AX = mybir.AluOpType, mybir.ActivationFunctionType, mybir.AxisListType

P = 128
N, D, E, EC = 6250, 64, 206250, 32
NH, HD = 4, 16
HI = -(-N // P)
ROWS = HI * P
LAST_ROWS = N - (HI - 1) * P
NT = -(-E // P)
STREAM = NT * P
T = 26
CHUNKS = NT // T
FULL = E // (P * T)
REM_P = (E - FULL * P * T) // T
REM = E - FULL * P * T - REM_P * T
PAIRS = CHUNKS // 2
G = 4
GROUPS = -(-T // G)
TP = GROUPS * G
T1 = T + 1
DST, SRC, GATE, H0 = EC, EC + 1, EC + 2, EC + 4
REC = H0 + D
QW = D + NH
SW = D + 2 * NH
NODE_W = 2 * D + QW + D
FAR = 1e30
EPS = 1e-5
assert CHUNKS * T == NT and PAIRS * 2 == CHUNKS == FULL + 1 and P * T < E and P <= ROWS

SCATTERED = 16 * T


WEIGHTS = ["rel", "att_w", "att_b", "W_w", "W_b", "k_w", "q_w", "v_w", "kn_w1", "kn_b1", "kn_w2",
           "kn_b2", "kl_w", "kl_b", "vn_w1", "vn_b1", "vn_w2", "vn_b2", "vl_w", "vl_b", "cen_w",
           "cen_b", "out_w", "out_b"]


class Kernel:
    pass


def by_node(table):
    return table.rearrange("(h l) c -> l h c", l=P)


def by_run(stream):
    return stream[0:STREAM, :].rearrange("(p t) c -> p t c", t=NT)


def bc(ap, dim, n):
    a = ap.unsqueeze(dim)
    shape = list(a.shape)
    shape[dim] = n
    return a.broadcast_to(shape)


def wait(eng, s, n):
    if not isinstance(n, int) or n > 0:
        eng.wait_ge(s, n)


def loop(eng, body):
    body(0)
    with eng.Fori(1, PAIRS - 1) as i:
        body(i)
    body(PAIRS - 1)


class Chain:

    def __init__(self, eng, s, per_turn=0):
        self.eng, self.s, self.per_turn, self.turn, self.n, self.fewer = eng, s, per_turn, 0, 0, 0

    def begin(self, turn):
        self.turn, self.n = turn, 0

    def mark(self, ins):
        ins.then_inc(self.s, 1)
        self.n += 1

    def wait(self):
        self.eng.wait_ge(self.s, self.turn * self.per_turn + (self.n - self.fewer))

    def then(self, ins):
        self.mark(ins)
        self.wait()

    def end(self):
        if isinstance(self.turn, int) and self.turn == 0:
            self.fewer = self.per_turn - self.n
        else:
            assert self.n == self.per_turn, (self.n, self.per_turn)


def layer_norm(c, xs, work, h, mean, std, s_var, s_std, s_h, done=1):
    v = c.eng
    c.then(v.tensor_reduce(mean, xs, AX.X, ALU.add))
    c.then(v.tensor_scalar(mean, mean, -1.0 / D, None, ALU.mult))
    c.then(v.tensor_tensor(h, xs, bc(mean, 2, D), ALU.add))
    c.then(v.tensor_tensor(work, h, h, ALU.mult))
    v.tensor_reduce(std, work, AX.X, ALU.add).then_inc(s_var, 1)
    v.wait_ge(s_std, done)
    c.then(v.reciprocal(std, std))
    v.scalar_tensor_tensor(h, h, 0.0, bc(std, 2, D), ALU.max, ALU.mult).then_inc(s_h, 1)
    v.wait_ge(s_h, done)


def split3(c, parts, value, rest):
    v = c.eng
    c.then(v.tensor_copy(parts[:, 0, :], value))
    c.then(v.tensor_tensor(rest, value, parts[:, 0, :], ALU.subtract))
    c.then(v.tensor_copy(parts[:, 1, :], rest))
    c.then(v.tensor_tensor(parts[:, 2, :], rest, parts[:, 1, :], ALU.subtract))


def at_start(i, b=0):
    return isinstance(i, int) and i == 0 and b == 0


def at_end(i, b=1):
    return isinstance(i, int) and i == PAIRS - 1 and b == 1


def helpers(k, ctx):
    nc = k.nc

    def tile(name, shape, dt=F32):
        return ctx.enter_context(nc.sbuf_tensor(name, shape, dt))

    def bank(name, dt=F32):
        return ctx.enter_context(nc.psum_tensor(name, [P, 512 if dt == F32 else 1024], dt))

    def sem(name):
        return ctx.enter_context(nc.semaphore(name))

    return tile, bank, sem


def setup(k):
    nc = k.nc
    with ExitStack() as ctx:
        tile, bank, sem = helpers(k, ctx)
        src_i, dst_i, typ_i, tmp_i = (tile(n, [P, NT], I32) for n in ("src_i", "dst_i", "typ_i", "tmp_i"))
        iota_i = tile("iota_i", [P, P], I32)
        number_i = tile("number_i", [P, 1], I32)
        typ_f = tile("typ_f", [P, NT])
        big = tile("big", [P, HI, D])
        h = tile("h0", [P, HI, D])
        mean, std, gate, gate_r = (tile(n, [P, HI]) for n in ("mean0", "std0", "gate", "gate_r"))
        a_r = tile("a_r", [P, 2, D])
        rel_r = tile("rel_r", [P, 2, D])
        b_r = tile("b_r", [P, 1])
        r01 = tile("r01", [P, 2])
        q_nat = tile("q_nat", [D, D])
        kl_bd = tile("kl_bd", [D, QW])
        q_fold = bank("q_fold")
        s_pad, s_zero, s_edges, s_x, s_small, s_w, s_pool = (
            sem(n) for n in ("s_pad", "s_zero", "s_edges", "s_x", "s_small", "s_w", "s_pool"))
        s_var, s_std, s_h, s_fold, s_table, s_dve = (
            sem(n) for n in ("s_var0", "s_std0", "s_h0", "s_fold", "s_table0", "s_dve0"))
        small, loaded = 12, 6 * G + 3 + 6 * NH
        span = tile("span", [P, 2, CHUNKS])
        span_c = tile("span_c", [CHUNKS, 2])
        base_c = tile("base_c", [CHUNKS, 3])
        base_d = tile("base_d", [CHUNKS, CHUNKS])
        base = tile("base", [P, CHUNKS])
        h3 = tile("h3", [P, HI, 3, D], BF16)
        h_rest = tile("h_rest", [P, HI, D])
        p_span = bank("p_span")
        p_base = bank("p_base")
        s_span, s_spanned, s_based, s_base, s_h3 = (sem(n) for n in ("s_span", "s_spanned", "s_based", "s_base", "s_h3"))

        with nc.Block() as block:
            @block.sync
            def _(sp):
                sp.wait_ge(s_pad, 5)
                n, last = FULL * P * T, FULL * T
                for t, v in ((src_i, k.src), (dst_i, k.dst), (typ_i, k.etype)):
                    sp.dma_start(t[:, 0:last].rearrange("p (c t) -> p c t", t=T), v[0:n].rearrange("(c p t) -> p c t", p=P, t=T)).then_inc(s_edges, 16)
                    sp.dma_start(t[0:REM_P, last:NT], v[n:n + REM_P * T].rearrange("(p t) -> p t", t=T)).then_inc(s_edges, 16)
                    sp.dma_start(t[REM_P:REM_P + 1, last:last + REM], v[n + REM_P * T:E].rearrange("(p t) -> p t", p=1)).then_inc(s_edges, 16)
                sp.dma_start(k.xs[:, 0:HI - 1, :], k.x[0:(HI - 1) * P, :].rearrange("(h l) c -> l h c", l=P)).then_inc(s_x, 16)
                sp.dma_start(k.xs[0:LAST_ROWS, HI - 1, :], k.x[(HI - 1) * P:N, :]).then_inc(s_x, 16)
                sp.dma_start(k.last_attr[0:REM_P, :, :], k.attr[n:n + REM_P * T, :].rearrange("(p t) c -> p t c", t=T)).then_inc(s_x, 16)
                sp.dma_start(k.last_attr[REM_P:REM_P + 1, 0:REM, :], k.attr[n + REM_P * T:E, :].rearrange("(p t) c -> p t c", p=1)).then_inc(s_x, 16)
                sp.wait_ge(s_h, 1)
                sp.dma_start(by_node(k.h_table), h[:]).then_inc(s_table, 16)
                sp.wait_ge(s_h3, 1)
                sp.dma_start(k.h3_table.rearrange("(h l) c -> l h c", l=P), h3[:].rearrange("p h a d -> p h (a d)")).then_inc(s_table, 16)
                sp.wait_ge(s_table, 32)

            @block.scalar
            def _(act):
                def row(to, vec, n):
                    act.dma_start(to, vec.rearrange("(a n) -> a n", a=1).broadcast_to([P, n])).then_inc(s_small, 16)

                row(a_r[:].rearrange("p a d -> p (a d)"), k.att_w.rearrange("a b -> (a b)"), 2 * D)
                row(rel_r[:].rearrange("p a d -> p (a d)"), k.rel.rearrange("a b -> (a b)"), 2 * D)
                row(b_r[:], k.att_b, 1)
                for to, b in ((k.W_br, k.W_b), (k.cen_br, k.cen_b), (k.out_br, k.out_b)):
                    row(to[:], b, D)
                row(k.b2_r[:, 0:HD], k.kn_b2, HD)
                row(k.b2_r[:, HD:EC], k.vn_b2, HD)
                row(k.vl_br[:, 0:HD], k.vl_b, HD)
                row(k.vl_br[:, HD:2 * HD], k.vl_b, HD)
                row(k.vl_br[:, 2 * HD:3 * HD], k.vl_b, HD)
                row(k.vl_br[:, 3 * HD:4 * HD], k.vl_b, HD)
                act.wait_ge(s_zero, 6)
                with nc.allow_non_contiguous_dma(reason="small weights, transposed as they are loaded"):
                    def load(to, w):
                        act.dma_start(to, w).then_inc(s_w, 16)

                    for p0 in range(0, P, EC):
                        for c0, w1, w2, b1 in ((0, k.kn_w1, k.kn_w2, k.kn_b1), (HD, k.vn_w1, k.vn_w2, k.vn_b1)):
                            r = slice(p0 + c0, p0 + c0 + HD)
                            load(k.w1_t[p0:p0 + EC, r], w1.rearrange("o i -> i o"))
                            load(k.w2_t[r, r], w2.rearrange("o i -> i o"))
                            load(k.b1_c[r, :], b1.rearrange("(o a) -> o a", a=1))
                    for w, to in ((k.W_w, k.W_t[:]), (k.cen_w, k.node_w[:, 2 * D + QW:NODE_W]), (k.out_w, k.out_t[:])):
                        load(to, w.rearrange("o i -> i o"))
                    for hd in range(NH):
                        r = slice(hd * HD, (hd + 1) * HD)
                        load(k.node_w[r, r], k.k_w[hd].rearrange("o i -> i o"))
                        load(k.node_w[r, D + hd * HD:D + (hd + 1) * HD], k.v_w[hd].rearrange("o i -> i o"))
                        load(k.vl_t[r, r], k.vl_w.rearrange("o i -> i o"))
                        load(q_nat[r, r], k.q_w[hd])
                        load(kl_bd[r, r], k.kl_w)
                        load(kl_bd[r, D + hd:D + hd + 1], k.kl_b.rearrange("(o a) -> o a", a=1))
                act.wait_ge(s_var, 1)
                nc.scalar.activation(std[:], std[:], ACT.Sqrt, bias=k.eps[:], scale=1.0 / D).then_inc(s_std, 1)

            @block.gpsimd
            def _(pool):
                nc.gpsimd.iota(iota_i[:], [[1, P]], base=0, channel_multiplier=0).then_inc(s_pool, 1)
                nc.gpsimd.iota(number_i[:], [[1, 1]], base=0, channel_multiplier=1).then_inc(s_pool, 1)
                nc.gpsimd.memset(k.ident[:], 0.0).then_inc(s_pool, 1)
                nc.gpsimd.memset(k.less[:], 1.0).then_inc(s_pool, 1)
                nc.gpsimd.memset(k.ones[:], 1.0).then_inc(s_pool, 1)
                pool.wait_ge(s_pool, 5)
                nc.gpsimd.affine_select(out=k.ident[:], in_=k.ident[:], compare_op=ALU.not_equal, fill=1.0,
                                        base=0, pattern=[[-1, P]], channel_multiplier=1).then_inc(s_pool, 1)
                nc.gpsimd.affine_select(out=k.less[:], in_=k.less[:], compare_op=ALU.is_gt, fill=0.0,
                                        base=0, pattern=[[1, P]], channel_multiplier=-1).then_inc(s_pool, 1)

            @block.tensor
            def _(pe):
                pe.wait_ge(s_span, 1)
                nc.tensor.transpose(p_span[0:CHUNKS, 0:P], span[:, 0, :], k.ident[:])
                nc.tensor.transpose(p_span[0:CHUNKS, P:2 * P], span[:, 1, :], k.ident[:]).then_inc(s_spanned, 1)
                pe.wait_ge(s_based, 1)
                nc.tensor.matmul(p_base[:, 0:CHUNKS], k.ones[0:CHUNKS, :], base_d[:], start=True, stop=True)
                nc.tensor.matmul(p_base[:, CHUNKS:CHUNKS + 1], k.ones[0:CHUNKS, :], base_c[:, 2:3], start=True, stop=True).then_inc(s_base, 1)
                pe.wait_ge(s_w, 16 * loaded)
                nc.tensor.matmul(q_fold[0:D, 0:QW], q_nat[:], kl_bd[:], start=True, stop=True).then_inc(s_fold, 1)

            @block.vector
            def _(dve):
                c = Chain(dve, s_dve)
                for t, v in ((src_i, ROWS - 1), (dst_i, N - 1), (typ_i, 0)):
                    nc.vector.memset(t[:, NT - T:NT], v).then_inc(s_pad, 1)
                nc.vector.memset(k.xs[:, HI - 1, :], 0.0).then_inc(s_pad, 1)
                nc.vector.memset(k.last_attr[:], 0.0).then_inc(s_pad, 1)
                for t in (k.w1_t, k.w2_t, k.node_w, k.vl_t, q_nat, kl_bd):
                    nc.vector.memset(t[:], 0.0).then_inc(s_zero, 1)
                c.mark(nc.vector.memset(k.eps[:], EPS))
                dve.wait_ge(s_edges, 144)
                c.then(nc.vector.tensor_single_scalar(tmp_i[:], src_i[:], P - 1, ALU.bitwise_and))
                c.then(nc.vector.tensor_copy(k.lo_b[:], tmp_i[:]))
                c.then(nc.vector.tensor_single_scalar(tmp_i[:], src_i[:], 7, ALU.arith_shift_right))
                c.mark(nc.vector.tensor_copy(k.hi_b[:], tmp_i[:]))
                c.mark(nc.vector.tensor_copy(k.src_f[:], src_i[:]))
                c.mark(nc.vector.tensor_copy(k.dst_f[:], dst_i[:]))
                c.mark(nc.vector.tensor_copy(typ_f[:], typ_i[:]))
                dve.wait_ge(s_pool, 7)
                c.mark(nc.vector.tensor_copy(k.iota_p[:], iota_i[:]))
                c.then(nc.vector.tensor_copy(k.iota_b[:], bc(iota_i[:], 2, T)))
                c.mark(nc.vector.tensor_copy(k.less_b[:], k.less[:]))
                c.mark(nc.vector.tensor_copy(k.number[:], number_i[:]))
                c.mark(nc.vector.tensor_copy(k.identb[:], k.ident[:]))
                by_chunk = k.dst_f[:].rearrange("p (c t) -> p c t", t=T)
                c.mark(nc.vector.tensor_reduce(span[:, 0, :], by_chunk, AX.X, ALU.min))
                c.wait()
                nc.vector.tensor_reduce(span[:, 1, :], by_chunk, AX.X, ALU.max).then_inc(s_span, 1)
                dve.wait_ge(s_spanned, 1)
                c.mark(nc.vector.tensor_reduce(span_c[:, 0:1], p_span[0:CHUNKS, 0:P], AX.X, ALU.min))
                c.then(nc.vector.tensor_reduce(span_c[:, 1:2], p_span[0:CHUNKS, P:2 * P], AX.X, ALU.max))
                c.then(nc.vector.tensor_scalar(base_c[:, 0:1], span_c[:, 0:1], float(ROWS - P), None, ALU.min))
                c.mark(nc.vector.tensor_scalar(base_c[:, 2:3], span_c[:, 1:2], base_c[:, 0:1], float(P), ALU.subtract, ALU.is_ge))
                c.wait()
                nc.vector.tensor_scalar(base_d[:], k.ident[0:CHUNKS, 0:CHUNKS], base_c[:, 0:1], None, ALU.mult).then_inc(s_based, 1)
                dve.wait_ge(s_base, 1)
                c.mark(nc.vector.tensor_copy(k.slow[:], p_base[:, CHUNKS:CHUNKS + 1]))
                c.then(nc.vector.tensor_copy(base[:], p_base[:, 0:CHUNKS]))
                c.mark(nc.vector.tensor_copy(k.base_i[:], base[:]))
                c.mark(nc.vector.tensor_tensor(k.dst_in[:].rearrange("p (c t) -> p c t", t=T), by_chunk, bc(base[:], 2, T), ALU.subtract))
                dve.wait_ge(s_small, 16 * small)
                c.then(nc.vector.tensor_tensor(rel_r[:], rel_r[:], bc(a_r[:, 1, :], 1, 2), ALU.mult))
                c.then(nc.vector.tensor_reduce(r01[:], rel_r[:], AX.X, ALU.add))
                c.then(nc.vector.tensor_tensor(r01[:], r01[:], b_r[:].broadcast_to([P, 2]), ALU.add))
                c.then(nc.vector.tensor_scalar(k.rel_gate[:], typ_f[:], r01[:, 1:2], None, ALU.mult))
                c.then(nc.vector.tensor_scalar(typ_f[:], typ_f[:], -1.0, 1.0, ALU.mult, ALU.add))
                c.then(nc.vector.scalar_tensor_tensor(k.rel_gate[:], typ_f[:], r01[:, 0:1], k.rel_gate[:], ALU.mult, ALU.add))
                dve.wait_ge(s_x, 64)
                layer_norm(c, k.xs[:], big[:], h[:], mean[:], std[:], s_var, s_std, s_h)
                c.then(nc.vector.tensor_tensor(big[:], h[:], bc(a_r[:, 0, :], 1, HI), ALU.mult))
                c.then(nc.vector.tensor_reduce(gate[:], big[:], AX.X, ALU.add))
                c.then(nc.vector.tensor_copy(h3[:, :, 0, :], h[:]))
                c.then(nc.vector.tensor_tensor(h_rest[:], h[:], h3[:, :, 0, :], ALU.subtract))
                c.then(nc.vector.tensor_copy(h3[:, :, 1, :], h_rest[:]))
                c.wait()
                nc.vector.tensor_tensor(h3[:, :, 2, :], h_rest[:], h3[:, :, 1, :], ALU.subtract).then_inc(s_h3, 1)
                split3(c, k.parts[0][:, :, 1, :], gate[:], gate_r[:])
                c.then(nc.vector.tensor_copy(k.parts[1][:, :, 1, :], k.parts[0][:, :, 1, :]))
                dve.wait_ge(s_fold, 1)
                c.then(nc.vector.tensor_copy(k.node_w[:, 2 * D:2 * D + QW], q_fold[0:D, 0:QW]))


def onehots(k, c, cols, b):
    c.mark(k.nc.vector.tensor_tensor(k.lo_hot[b][:], k.iota_b[:], bc(k.lo_b[:, cols], 1, P), ALU.is_equal))
    c.mark(k.nc.vector.tensor_tensor(k.hi_hot[b][:], k.iota_b[:, 0:HI, :], bc(k.hi_b[:, cols], 1, HI), ALU.is_equal))


def histogram(k):
    nc = k.nc
    with ExitStack() as ctx:
        tile, bank, sem = helpers(k, ctx)
        total = tile("total", [P, HI])
        upto = tile("upto", [P, HI])
        end = tile("end", [P, HI])
        zeros = tile("zeros", [P, P], BF16)
        counts = bank("counts")
        below = bank("below")
        totals = bank("totals")
        s_zeros, s_hot, s_counted, s_all, s_cnt, s_pre, s_dve = (
            sem(n) for n in ("s_zeros", "s_hot0", "s_counted", "s_all", "s_cnt", "s_pre", "s_dve1"))
        with nc.Block() as block:
            @block.vector
            def _(dve):
                hot = Chain(dve, s_hot, 4)
                nc.vector.memset(zeros[:], 0.0).then_inc(s_zeros, 1)

                def body(i):
                    hot.begin(i)
                    for b in range(2):
                        wait(dve, s_counted, 2 * i + b - 1)
                        onehots(k, hot, bass.ds(i * 2 * T + b * T, T), b)
                    hot.end()

                loop(dve, body)
                c = Chain(dve, s_dve)
                dve.wait_ge(s_all, 1)
                nc.vector.tensor_copy(k.cnt[:], counts[:, 0:HI]).then_inc(s_cnt, 1)
                dve.wait_ge(s_pre, 1)
                c.then(nc.vector.tensor_copy(total[:], totals[:, 0:HI]))
                c.then(nc.vector.tensor_tensor_scan(upto[:], k.ones[:, 0:HI], total[:], 0.0, ALU.mult, ALU.add))
                c.then(nc.vector.tensor_tensor(upto[:], upto[:], total[:], ALU.subtract))
                c.then(nc.vector.tensor_tensor(k.start[:], upto[:], below[:, 0:HI], ALU.add))
                c.then(nc.vector.tensor_tensor(end[:], k.start[:], k.cnt[:], ALU.add))
                c.mark(nc.vector.tensor_scalar(k.filled[:], k.cnt[:], 1.0, None, ALU.min))
                c.mark(nc.vector.tensor_scalar(k.last_at[:], end[:], -1.0, 0.0, ALU.add, ALU.max))

            @block.tensor
            def _(pe):
                pe.wait_ge(s_zeros, 1)
                nc.tensor.matmul(counts[:, 0:HI], zeros[:], zeros[:, 0:HI], start=True, stop=False)

                def body(i):
                    for b in range(2):
                        pe.wait_ge(s_hot, 4 * i + 2 * b + 2)
                        for t in range(T):
                            last = nc.tensor.matmul(counts[:, 0:HI], k.lo_hot[b][:, :, t], k.hi_hot[b][:, :, t], start=False, stop=False)
                        last.then_inc(s_counted, 1)

                loop(pe, body)
                nc.tensor.matmul(counts[:, 0:HI], zeros[:], zeros[:, 0:HI], start=False, stop=True).then_inc(s_all, 1)
                pe.wait_ge(s_cnt, 1)
                nc.tensor.matmul(below[:, 0:HI], k.less[:], k.cnt[:], start=True, stop=True)
                nc.tensor.matmul(totals[:, 0:HI], k.ones[:], k.cnt[:], start=True, stop=True).then_inc(s_pre, 1)


def sort(k):
    nc = k.nc
    with ExitStack() as ctx:
        tile, bank, sem = helpers(k, ctx)
        lo_hot_t = [tile(f"lo_hot_t{b}", [P, G * P], BF16) for b in range(2)]
        dst_hot = [tile(f"dst_hot{b}", [P, G * P], BF16) for b in range(2)]
        hist = [tile(f"hist{b}", [P, G, HI], BF16) for b in range(2)]
        earlier = [tile(f"earlier{b}", [P, G, P], BF16) for b in range(2)]
        window = [tile(f"window{b}", [P, 3, D], BF16) for b in range(2)]
        rest = tile("rest", [P, HI])
        picked = tile("picked", [P, G, 2, HI])
        place_gate = [tile(f"place_gate{b}", [P, G, 2]) for b in range(2)]
        place_all = tile("place_all", [P, NT], I32)
        logit_all = tile("logit_all", [P, NT])
        place = [tile(f"place{b}", [P, T], I32) for b in range(2)]
        stage = [tile(f"stage{b}", [P, T, EC]) for b in range(2)]
        h_dst = [tile(f"h_dst{b}", [P, T, D]) for b in range(2)]
        rec = [tile(f"rec{b}", [P, T, REC]) for b in range(2)]
        zero_q = tile("zero_q", [P, T * QW])
        p_t = bank("p_t", BF16)
        p_hist, p_same, p_dst, p_h = (bank(n) for n in ("p_hist", "p_same", "p_dst", "p_h"))
        p_place = bank("p_place")
        p_look = [bank(f"p_look{b}") for b in range(2)]
        (s_set, s_hot, s_t, s_hist, s_t_copied, s_hist_copied, s_same, s_parts, s_placed, s_earlier, s_look, s_picked,
         s_chunk, s_staged, s_ready, s_dve, s_passed, s_dst, s_dst_hot, s_h, s_h_copied, s_zq) = (
            sem(n + "_s") for n in ("s_set", "s_hot", "s_t", "s_hist", "s_t_copied", "s_hist_copied", "s_same", "s_parts",
                                    "s_placed", "s_earlier", "s_look", "s_picked", "s_chunk", "s_staged", "s_ready", "s_dve",
                                    "s_passed", "s_dst", "s_dst_hot", "s_h", "s_h_copied", "s_zq"))
        s_attr, s_sent, s_window = ([sem(f"{n}{b}") for b in range(2)] for n in ("s_attr", "s_sent", "s_window"))
        attr_v = k.attr[0:FULL * P * T, :].rearrange("(c p t) e -> c p t e", p=P, t=T)
        q_starts_v = by_run(k.q_starts)

        def size(g):
            return min(G, T - g * G)

        with nc.Block() as block:
            @block.sync
            def _(sp):
                sp.wait_ge(s_set, 1)

                def body(i):
                    for b in range(2):
                        n = 2 * i + b
                        base = sp.value_load(k.base_i[0:1, bass.ds(n, 1)], min_val=0, max_val=ROWS - P)
                        wait(sp, s_h, (n - 1) * GROUPS)
                        sp.dma_start(window[b][:].rearrange("p a d -> p (a d)"), k.h3_table[bass.ds(base, P), :]).then_inc(s_window[b], 16)
                        if not at_end(i, b):
                            wait(sp, s_staged, n - 1)
                            sp.dma_start(stage[b][:], attr_v[bass.ds(n, 1), :, :, :].rearrange("c p t e -> (c p) t e")).then_inc(s_attr[b], 16)
                        sp.dma_start(q_starts_v[:, bass.ds(n * T, T), :], zero_q[:].rearrange("p (t c) -> p t c", c=QW)).then_inc(s_zq, 16)

                loop(sp, body)
                sp.wait_ge(s_zq, 16 * CHUNKS)
                for b in range(2):
                    sp.wait_ge(s_sent[b], SCATTERED * PAIRS)

            @block.gpsimd
            def _(pool):
                def body(i):
                    for b in range(2):
                        n = 2 * i + b
                        pool.wait_ge(s_ready, n + 1)
                        pool.sem_inc(s_passed, 1)
                        for t in range(T):
                            nc.gpsimd.indirect_dma_start(
                                k.records, bass.IndirectOffsetOnAxis(ap=place[b][:, t:t + 1], axis=0),
                                rec[b][:, t, :], None).then_inc(s_sent[b], 16)

                loop(pool, body)

            @block.tensor
            def _(pe):
                nc.tensor.matmul(p_place[:, 0:HI], k.ident[:], k.start[:], start=True, stop=True).then_inc(s_placed, 1)

                def look(q, i, b, g):
                    qb = (b * GROUPS + g) % 2
                    pe.wait_ge(s_earlier, q + 1)
                    pe.wait_ge(s_hist_copied, q + 1)
                    wait(pe, s_picked, q - 1)
                    for j in range(size(g)):
                        at = lo_hot_t[qb][:, j * P:(j + 1) * P]
                        to = p_look[qb][:, j * 2 * HI:j * 2 * HI + HI]
                        both = p_look[qb][:, j * 2 * HI:(j + 1) * 2 * HI]
                        for part in range(3):
                            nc.tensor.matmul(both, at, k.parts[qb][:, part, :, :], start=(part == 0), stop=False)
                        for e in range(j):
                            nc.tensor.matmul(to, at, hist[qb][:, e, :], start=False, stop=False)
                        last = nc.tensor.matmul(to, earlier[qb][:, j, :], k.hi_hot[b][:, :, g * G + j], start=False, stop=True)
                    last.then_inc(s_look, 1)
                    if g == 0:
                        pe.wait_ge(s_window[b], 16 * (i + 1))
                    pe.wait_ge(s_dst_hot, q + 1)
                    wait(pe, s_h_copied, q)
                    for j in range(size(g)):
                        for part in range(3):
                            last = nc.tensor.matmul(p_h[:, j * D:(j + 1) * D], dst_hot[qb][:, j * P:(j + 1) * P], window[b][:, part, :],
                                                    start=(part == 0), stop=(part == 2))
                    last.then_inc(s_h, 1)

                def body(i):
                    for b in range(2):
                        n = 2 * i + b
                        pe.wait_ge(s_hot, 2 * n + 2)
                        for g in range(GROUPS):
                            q = n * GROUPS + g
                            qb = (b * GROUPS + g) % 2
                            tiles = range(g * G, g * G + size(g))
                            for j, t in enumerate(tiles):
                                last = nc.tensor.transpose(p_t[:, j * P:(j + 1) * P], k.lo_hot[b][:, :, t], k.identb[:])
                            last.then_inc(s_t, 1)
                            wait(pe, s_hist_copied, q)
                            for j, t in enumerate(tiles):
                                last = nc.tensor.matmul(p_hist[:, j * HI:(j + 1) * HI], k.lo_hot[b][:, :, t], k.hi_hot[b][:, :, t], start=True, stop=True)
                            last.then_inc(s_hist, 1)
                            wait(pe, s_dst_hot, q)
                            for j, t in enumerate(tiles):
                                col = k.dst_in[:, bass.ds(n * T + t, 1)]
                                last = nc.tensor.matmul(p_dst[:, j * P:(j + 1) * P], col.broadcast_to([P, P]), k.identb[:], start=True, stop=True)
                            last.then_inc(s_dst, 1)
                            if g > 0:
                                look(q - 1, i, b, g - 1)
                            elif b > 0:
                                look(q - 1, i, 0, GROUPS - 1)
                            elif not at_start(i):
                                look(q - 1, i - 1, 1, GROUPS - 1)
                            pe.wait_ge(s_t_copied, q + 1)
                            for j, t in enumerate(tiles):
                                at = lo_hot_t[qb][:, j * P:(j + 1) * P]
                                last = nc.tensor.matmul(p_same[:, j * P:(j + 1) * P], at, at, start=True, stop=True)
                            last.then_inc(s_same, 1)
                            pe.wait_ge(s_parts, q + 1)
                            for t in tiles:
                                last = nc.tensor.matmul(p_place[:, 0:HI], k.lo_hot[b][:, :, t], k.hi_hot[b][:, :, t],
                                                        start=False, stop=True, skip_group_check=True)
                            last.then_inc(s_placed, 1)

                loop(pe, body)
                look(CHUNKS * GROUPS - 1, PAIRS - 1, 1, GROUPS - 1)

            @block.scalar
            def _(act):
                def h_copy(q, b, g):
                    act.wait_ge(s_h, q + 1)
                    n = size(g)
                    nc.scalar.copy(h_dst[b][:, g * G:g * G + n, :], p_h[:, 0:n * D].rearrange("p (t d) -> p t d", d=D)).then_inc(s_h_copied, 1)

                def assemble(n, i, b):
                    wait(act, s_sent[b], SCATTERED * i)
                    act.wait_ge(s_chunk, n + 1)
                    act.wait_ge(s_h_copied, (n + 1) * GROUPS)
                    cols = bass.ds(n * T, T)
                    nc.scalar.copy(place[b][:], place_all[:, cols])
                    nc.scalar.copy(rec[b][:, :, DST], k.dst_f[:, cols])
                    nc.scalar.copy(rec[b][:, :, SRC], k.src_f[:, cols])
                    nc.scalar.copy(rec[b][:, :, H0:REC], h_dst[b][:])
                    nc.scalar.activation(rec[b][:, :, GATE], logit_all[:, cols], ACT.Sigmoid)
                    if at_end(i, b):
                        nc.scalar.copy(rec[b][:, :, 0:EC], k.last_attr[:]).then_inc(s_ready, 1)
                    else:
                        act.wait_ge(s_attr[b], 16 * (i + 1))
                        nc.scalar.copy(rec[b][:, :, 0:EC], stage[b][:]).then_inc(s_staged, 1)
                        act.wait_ge(s_staged, n + 1)
                        act.sem_inc(s_ready, 1)

                def body(i):
                    for b in range(2):
                        n = 2 * i + b
                        for g in range(GROUPS):
                            q = n * GROUPS + g
                            qb = (b * GROUPS + g) % 2
                            wait(act, s_look, q - 1)
                            act.wait_ge(s_t, q + 1)
                            nc.scalar.copy(lo_hot_t[qb][:, 0:size(g) * P], p_t[:, 0:size(g) * P]).then_inc(s_t_copied, 1)
                            act.wait_ge(s_hist, q + 1)
                            nc.scalar.copy(hist[qb][:, 0:size(g), :], p_hist[:, 0:size(g) * HI].rearrange("p (g h) -> p g h", h=HI)).then_inc(s_hist_copied, 1)
                            if g > 0:
                                h_copy(q - 1, b, g - 1)
                            elif not at_start(i, b):
                                h_copy(q - 1, 1 - b, GROUPS - 1)
                            if g == 3 and not at_start(i, b):
                                assemble(n - 1, i - 1 + b, 1 - b)

                loop(act, body)
                h_copy(CHUNKS * GROUPS - 1, 1, GROUPS - 1)
                assemble(CHUNKS - 1, PAIRS - 1, 1)

            @block.vector
            def _(dve):
                c = Chain(dve, s_dve, 2 * (6 * GROUPS - 1))
                hot = Chain(dve, s_hot, 4)
                nc.vector.memset(zero_q[:], 0.0).then_inc(s_set, 1)
                for b in range(2):
                    c.mark(nc.vector.memset(rec[b][:, :, GATE + 1:H0], 0.0))
                hot.begin(0)
                onehots(k, hot, bass.ds(0, T), 0)

                def pick(q, b, g, gb):
                    n = size(g)
                    dve.wait_ge(s_look, q + 1)
                    nc.vector.tensor_tensor(
                        picked[:, 0:n, :, :], p_look[gb][:, 0:n * 2 * HI].rearrange("p (g a h) -> p g a h", a=2, h=HI),
                        bc(k.hi_hot[b][:, :, g * G:g * G + n].rearrange("p h t -> p t h"), 2, 2), ALU.mult).then_inc(s_picked, 1)

                def summed(q, g, gb):
                    dve.wait_ge(s_picked, q + 1)
                    n = size(g)
                    c.mark(nc.vector.tensor_reduce(place_gate[gb][:, 0:n, :], picked[:, 0:n, :, :], AX.X, ALU.add))

                def placed(g, gb, t0):
                    c.wait()
                    n = size(g)
                    cols = bass.ds(t0 + g * G, n)
                    c.mark(nc.vector.tensor_copy(place_all[:, cols], place_gate[gb][:, 0:n, 0]))
                    if g == GROUPS - 1:
                        c.wait()
                    ins = nc.vector.tensor_tensor(logit_all[:, cols], place_gate[gb][:, 0:n, 1], k.rel_gate[:, cols], ALU.add)
                    if g < GROUPS - 1:
                        c.mark(ins)
                    else:
                        ins.then_inc(s_chunk, 1)

                def behind(n, i, b, g):
                    q = n * GROUPS + g - 2
                    if g >= 2:
                        return q, b, g - 2, n * T
                    return q, 1 - b, GROUPS + g - 2, n * T - T

                def body(i):
                    if not at_start(i):
                        c.begin(i)
                        hot.begin(i)
                    for b in range(2):
                        n = 2 * i + b
                        for g in range(GROUPS):
                            q = n * GROUPS + g
                            qb = (b * GROUPS + g) % 2
                            m = size(g)
                            older = None if at_start(i, b) and g < 2 else behind(n, i, b, g)
                            parts = k.parts[qb][:, :, 0, :]
                            wait(dve, s_look, q - 1)
                            dve.wait_ge(s_placed, q + 1)
                            c.mark(nc.vector.tensor_copy(parts[:, 0, :], p_place[:, 0:HI]))
                            dve.wait_ge(s_dst, q + 1)
                            wait(dve, s_h, q - 1)
                            nc.vector.tensor_scalar(dst_hot[qb][:, 0:m * P], p_dst[:, 0:m * P], k.number[:], None, ALU.is_equal).then_inc(s_dst_hot, 1)
                            c.wait()
                            c.mark(nc.vector.tensor_tensor(rest[:], p_place[:, 0:HI], parts[:, 0, :], ALU.subtract))
                            if older:
                                pick(older[0], older[1], older[2], qb)
                            c.wait()
                            c.mark(nc.vector.tensor_copy(parts[:, 1, :], rest[:]))
                            if older:
                                summed(older[0], older[2], qb)
                            c.wait()
                            nc.vector.tensor_tensor(parts[:, 2, :], rest[:], parts[:, 1, :], ALU.subtract).then_inc(s_parts, 1)
                            if older:
                                placed(older[2], qb, older[3])
                            if g == 3 and not at_end(i, b):
                                wait(dve, s_look, n * GROUPS)
                                onehots(k, hot, bass.ds(n * T + T, T), 1 - b)
                                hot.wait()
                            dve.wait_ge(s_same, q + 1)
                            nc.vector.tensor_tensor(
                                earlier[qb][:, 0:m, :], p_same[:, 0:m * P].rearrange("p (g e) -> p g e", e=P),
                                bc(k.less_b[:], 1, m), ALU.mult).then_inc(s_earlier, 1)
                    if not at_end(i):
                        c.end()
                        hot.end()

                loop(dve, body)
                for g in (GROUPS - 2, GROUPS - 1):
                    q = CHUNKS * GROUPS - GROUPS + g
                    gb = (GROUPS + g) % 2
                    pick(q, 1, g, gb)
                    summed(q, g, gb)
                    placed(g, gb, NT - T)


def relation_layer(k):
    nc = k.nc
    with ExitStack() as ctx:
        tile, bank, sem = helpers(k, ctx)
        rows = tile("rows", [P, 1 + NT])
        rec = [tile(f"rec_r{b}", [P, T, REC]) for b in range(2)]
        idx = [tile(f"idx_r{b}", [P, T], I32) for b in range(2)]
        got = [tile(f"got_r{b}", [P, T, D]) for b in range(2)]
        keep = [tile(f"keep_r{b}", [P, D, T1]) for b in range(2)]
        add = tile("add_r", [P, D, T1])
        state = [tile(f"state_r{b}", [P, D, T1]) for b in range(2)]
        packed = [tile(f"packed_r{b}", [P, T, D]) for b in range(2)]
        s_zero, s_idx, s_add, s_state, s_keep, s_packed, s_dve, s_passed = (
            sem(n) for n in ("s_zero_r", "s_idx_r", "s_add_r", "s_state_r", "s_keep_r", "s_packed_r", "s_dve_r", "s_passed_r"))
        s_rec, s_got, s_store = ([sem(f"{n}{b}") for b in range(2)] for n in ("s_rec_r", "s_got_r", "s_store_r"))
        records_v, sums_v = by_run(k.records), by_run(k.sums0)

        def either(eng, body):
            flag = eng.value_load(k.slow[0:1, 0:1], min_val=0, max_val=CHUNKS)
            with eng.If(flag != 0):
                body(True)
            with eng.Else():
                body(False)

        with nc.Block() as block:
            @block.sync
            def _(sp):
                def body(i):
                    for b in range(2):
                        wait(sp, s_add, 2 * i + b - 1)
                        sp.dma_start(rec[b][:], records_v[:, bass.ds(i * 2 * T + b * T, T), :]).then_inc(s_rec[b], 16)

                loop(sp, body)

            @block.gpsimd
            def _(pool):
                def body(i):
                    for b in range(2):
                        n = 2 * i + b
                        wait(pool, s_add, n - 1)
                        pool.wait_ge(s_idx, n + 1)
                        pool.sem_inc(s_passed, 1)
                        for t in range(T):
                            nc.gpsimd.indirect_dma_start(
                                got[b][:, t, :], None, k.h_table,
                                bass.IndirectOffsetOnAxis(ap=idx[b][:, t:t + 1], axis=0)).then_inc(s_got[b], 16)

                either(pool, lambda gather: loop(pool, body) if gather else pool.sem_inc(s_passed, 1))

            @block.scalar
            def _(act):
                def mark(n, i, b):
                    act.wait_ge(s_idx, n + 1)
                    wait(act, s_state, n - 1)
                    nc.scalar.copy(keep[b][:, :, 1:T1], bc(k.same[:, bass.ds(n * T, T)], 1, D)).then_inc(s_keep, 1)

                act.wait_ge(s_zero, 4)
                mark(0, 0, 0)

                def body(i):
                    for b in range(2):
                        n = 2 * i + b
                        if not at_end(i, b):
                            mark(n + 1, i + b, 1 - b)
                        act.wait_ge(s_state, n + 1)
                        wait(act, s_store[b], 16 * i)
                        nc.scalar.copy(packed[b][:], state[b][:, :, 1:T1].rearrange("p d t -> p t d")).then_inc(s_packed, 1)
                        act.wait_ge(s_packed, n + 1)
                        act.dma_start(sums_v[:, bass.ds(n * T, T), :], packed[b][:]).then_inc(s_store[b], 16)

                loop(act, body)
                for b in range(2):
                    act.wait_ge(s_store[b], 16 * PAIRS)

            @block.vector
            def _(dve):
                c = Chain(dve, s_dve, 2 * 4)

                def prepare(n, i, b):
                    t0 = i * 2 * T + b * T
                    dve.wait_ge(s_rec[b], 16 * (i + 1))
                    if at_start(i, b):
                        c.mark(nc.vector.tensor_copy(rows[:, 0:1], rec[b][:, 0:1, SRC]))
                    c.mark(nc.vector.tensor_copy(idx[b][:], rec[b][:, :, DST]))
                    c.mark(nc.vector.tensor_copy(k.dst_s[:, bass.ds(t0, T)], rec[b][:, :, DST]))
                    c.then(nc.vector.tensor_copy(rows[:, bass.ds(t0 + 1, T)], rec[b][:, :, SRC]))
                    nc.vector.tensor_tensor(k.same[:, bass.ds(t0, T)], rows[:, bass.ds(t0 + 1, T)],
                                            rows[:, bass.ds(t0, T)], ALU.is_equal).then_inc(s_idx, 1)

                def scan(n, i, b, gather):
                    if gather:
                        dve.wait_ge(s_got[b], SCATTERED * (i + 1))
                    h_dst = got[b][:] if gather else rec[b][:, :, H0:REC]
                    if at_start(i, b):
                        c.mark(nc.vector.memset(add[:, :, 0:1], 0.0))
                    else:
                        c.mark(nc.vector.tensor_copy(add[:, :, 0:1], state[1 - b][:, :, T:T1]))
                    nc.vector.tensor_tensor(add[:, :, 1:T1], h_dst.rearrange("p t d -> p d t"),
                                            bc(rec[b][:, :, GATE], 1, D), ALU.mult).then_inc(s_add, 1)
                    c.wait()
                    dve.wait_ge(s_add, n + 1)
                    dve.wait_ge(s_keep, n + 1)
                    wait(dve, s_packed, n - 1)
                    nc.vector.tensor_tensor_scan(state[b][:].rearrange("p d t -> p (d t)"), keep[b][:].rearrange("p d t -> p (d t)"),
                                                 add[:].rearrange("p d t -> p (d t)"), 0.0, ALU.mult, ALU.add).then_inc(s_state, 1)
                    dve.wait_ge(s_state, n + 1)

                for b in range(2):
                    nc.vector.memset(keep[b][:, :, 0:1], 0.0).then_inc(s_zero, 2)

                def way(gather):
                    c.begin(0)
                    c.fewer = 0
                    if gather:
                        prepare(0, 0, 0)

                    def body(i):
                        if not at_start(i):
                            c.begin(i)
                        for b in range(2):
                            n = 2 * i + b
                            if not gather:
                                prepare(n, i, b)
                            elif not at_end(i, b):
                                prepare(n + 1, i + b, 1 - b)
                            scan(n, i, b, gather)
                        if not at_end(i):
                            c.end()

                    loop(dve, body)

                either(dve, way)
                c.wait()
                c.mark(nc.vector.tensor_copy(k.first_row[:], rows[:, 1:2]))
                c.mark(nc.vector.tensor_copy(k.last_row[:], rows[:, NT:NT + 1]))
                c.then(nc.vector.tensor_copy(k.tail0[:], state[1][:, :, T]))


def relation_nodes(k):
    nc = k.nc
    R = 7
    assert HI == R * R
    with ExitStack() as ctx:
        tile, bank, sem = helpers(k, ctx)
        nxt, prv = tile("nxt", [P, 1]), tile("prv", [P, 1])
        hi_at_i = tile("hi_at_i", [P, HI], I32)
        hi_at = tile("hi_at", [P, HI])
        going = tile("going", [P, 1])
        first_f = tile("first_f", [P, HI])
        rowid = tile("rowid", [P, HI])
        rowid_i = tile("rowid_i", [P, HI], I32)
        first_at = tile("first_at", [P, HI], I32)
        sums = tile("sums_n", [P, HI, D])
        tails = tile("tails", [P, HI, D])
        h = tile("h1", [P, HI, D])
        kvq = tile("kvq", [P, HI, 2 * D + QW])
        feat = [tile(f"feat{b}", [D, R * P]) for b in range(2)]
        mean, std = tile("mean1", [P, HI]), tile("std1", [P, HI])
        first_i = tile("first_i", [P, 1], I32)
        p_tail = [bank(f"p_tail{b}") for b in range(2)]
        p_f = [[bank(f"p_f{b}{j}") for j in range(2)] for b in range(2)]
        p_out = [bank(f"p_out{b}") for b in range(2)]
        (s_set, s_shift, s_iota, s_own, s_tail, s_tails, s_added, s_f, s_feat, s_out, s_z, s_tanh, s_var, s_std, s_h,
         s_f2, s_feat2, s_node, s_kvq, s_y, s_tab, s_first, s_sent, s_init, s_dve) = (
            sem(n + "_n") for n in ("s_set", "s_shift", "s_iota", "s_own", "s_tail", "s_tails", "s_added", "s_f", "s_feat",
                                    "s_out", "s_z", "s_tanh", "s_var", "s_std", "s_h", "s_f2", "s_feat2", "s_node",
                                    "s_kvq", "s_y", "s_tab", "s_first", "s_sent", "s_init", "s_dve"))
        s_sums = [sem(f"s_sums_n{r}") for r in range(R)]

        def of_round(r):
            return slice(r * R, (r + 1) * R)

        with nc.Block() as block:
            @block.sync
            def _(sp):
                sp.wait_ge(s_set, 2)
                with nc.allow_non_contiguous_dma(reason="a column, one partition on"):
                    sp.dma_start(nxt[0:P - 1, :], k.first_row[1:P, :]).then_inc(s_shift, 16)
                    sp.dma_start(prv[1:P, :], k.last_row[0:P - 1, :]).then_inc(s_shift, 16)
                for r in range(R):
                    rr = of_round(r)
                    sp.wait_ge(s_kvq, (r + 1) * R)
                    sp.dma_start(by_node(k.q_table)[:, rr, :], kvq[:, rr, 2 * D:2 * D + QW]).then_inc(s_tab, 16)
                    sp.dma_start(by_node(k.kv_table)[:, rr, :], kvq[:, rr, 0:2 * D]).then_inc(s_tab, 16)
                sp.wait_ge(s_tab, 32 * R)

            @block.gpsimd
            def _(pool):
                nc.gpsimd.iota(hi_at_i[:], [[P, HI]], base=0, channel_multiplier=0).then_inc(s_iota, 1)
                nc.gpsimd.iota(rowid_i[:], [[P, HI]], base=0, channel_multiplier=1).then_inc(s_iota, 1)
                for hi in range(HI):
                    nc.gpsimd.indirect_dma_start(
                        sums[:, hi, :], None, k.sums0,
                        bass.IndirectOffsetOnAxis(ap=k.last_at[:, hi:hi + 1], axis=0)).then_inc(s_sums[hi // R], 16)
                pool.wait_ge(s_first, 1)
                for hi in range(HI):
                    pool.wait_ge(s_kvq, hi + 1)
                    nc.gpsimd.indirect_dma_start(
                        k.q_starts, bass.IndirectOffsetOnAxis(ap=first_at[:, hi:hi + 1], axis=0),
                        kvq[:, hi, 2 * D:2 * D + QW], None).then_inc(s_sent, 16)
                pool.wait_ge(s_tab, 32 * R)
                nc.gpsimd.indirect_dma_start(
                    k.q_init[:], None, k.q_table,
                    bass.IndirectOffsetOnAxis(ap=first_i[:, 0:1], axis=0)).then_inc(s_init, 16)
                pool.wait_ge(s_sent, 16 * HI)

            @block.tensor
            def _(pe):
                pe.wait_ge(s_own, 1)
                for r in range(R):
                    if r >= 2:
                        pe.wait_ge(s_tails, r - 1)
                    for j in range(R):
                        hi = r * R + j
                        last = nc.tensor.matmul(p_tail[r % 2][:, j * D:(j + 1) * D], k.own[:, hi * P:(hi + 1) * P], k.tail0[:], start=True, stop=True)
                    last.then_inc(s_tail, 1)

                def transposes(r, to, of, copied, done):
                    if r >= 1:
                        pe.wait_ge(copied, r)
                    for j in range(R):
                        last = nc.tensor.transpose(to[j // 4][0:D, (j % 4) * P:(j % 4 + 1) * P], of[:, r * R + j, :], k.ident[:])
                    last.then_inc(done, 1)

                def first_half(r):
                    pe.wait_ge(s_added, r + 1)
                    transposes(r, p_f[0], sums, s_feat, s_f)
                    pe.wait_ge(s_feat, r + 1)
                    if r >= 2:
                        pe.wait_ge(s_z, r - 1)
                    for j in range(R):
                        last = nc.tensor.matmul(p_out[r % 2][:, j * D:(j + 1) * D], feat[0][:, j * P:(j + 1) * P], k.W_t[:], start=True, stop=True)
                    last.then_inc(s_out, 1)

                def second_half(r):
                    pe.wait_ge(s_h, r + 1)
                    transposes(r, p_f[1], h, s_feat2, s_f2)
                    pe.wait_ge(s_feat2, r + 1)
                    for j in range(R):
                        hi = r * R + j
                        if hi < 2:
                            pe.wait_ge(s_tails, R)
                        else:
                            pe.wait_ge(s_kvq, hi - 1)
                            pe.wait_ge(s_y, hi - 1)
                        nc.tensor.matmul(p_tail[hi % 2][:, 0:NODE_W], feat[1][:, j * P:(j + 1) * P], k.node_w[:], start=True, stop=True).then_inc(s_node, 1)

                for r in range(R + 1):
                    if r < R:
                        first_half(r)
                    if r >= 1:
                        second_half(r - 1)

            @block.scalar
            def _(act):
                def copies(b, r, have, done):
                    act.wait_ge(have, r + 1)
                    nc.scalar.copy(feat[b][:, 0:4 * P], p_f[b][0][0:D, :])
                    nc.scalar.copy(feat[b][:, 4 * P:R * P], p_f[b][1][0:D, 0:(R - 4) * P]).then_inc(done, 1)

                for r in range(R + 1):
                    if r < R:
                        if r >= 1:
                            act.wait_ge(s_out, r)
                        copies(0, r, s_f, s_feat)
                        act.wait_ge(s_z, r + 1)
                        z = sums[:, of_round(r), :]
                        nc.scalar.activation(z, z, ACT.Tanh).then_inc(s_tanh, 1)
                        act.wait_ge(s_var, r + 1)
                        root = std[:, of_round(r)]
                        nc.scalar.activation(root, root, ACT.Sqrt, bias=k.eps[:], scale=1.0 / D).then_inc(s_std, 1)
                    if r >= 1:
                        if r >= 2:
                            act.wait_ge(s_node, (r - 1) * R)
                        copies(1, r - 1, s_f2, s_feat2)
                        for hi in range((r - 1) * R, r * R):
                            act.wait_ge(s_node, hi + 1)
                            nc.scalar.copy(kvq[:, hi, :], p_tail[hi % 2][:, 0:2 * D + QW]).then_inc(s_kvq, 1)

            @block.vector
            def _(dve):
                c = Chain(dve, s_dve)
                nc.vector.memset(nxt[:], -1.0).then_inc(s_set, 1)
                nc.vector.memset(prv[:], -1.0).then_inc(s_set, 1)
                dve.wait_ge(s_iota, 2)
                c.mark(nc.vector.tensor_copy(hi_at[:], hi_at_i[:]))
                c.then(nc.vector.tensor_copy(rowid[:], rowid_i[:]))
                c.then(nc.vector.tensor_scalar(rowid[:], rowid[:], float(STREAM), None, ALU.add))
                c.then(nc.vector.tensor_tensor(first_f[:], k.start[:], rowid[:], ALU.subtract))
                c.then(nc.vector.tensor_tensor(first_f[:], first_f[:], k.filled[:], ALU.mult))
                nc.vector.tensor_tensor(first_at[:], first_f[:], rowid[:], ALU.add).then_inc(s_first, 1)
                dve.wait_ge(s_shift, 32)
                c.mark(nc.vector.tensor_tensor(k.goes_on[:], k.last_row[:], nxt[:], ALU.is_equal))
                c.mark(nc.vector.tensor_tensor(k.came_on[:], k.first_row[:], prv[:], ALU.is_equal))
                c.mark(nc.vector.tensor_copy(first_i[:], k.first_row[:]))
                c.then(nc.vector.tensor_scalar(going[:], k.last_row[:], 1.0, None, ALU.add))
                c.then(nc.vector.tensor_scalar(going[:], going[:], k.goes_on[:], -1.0, ALU.mult, ALU.add))
                c.then(nc.vector.tensor_scalar(k.own_at[:], hi_at[:], -1.0, going[:], ALU.mult, ALU.add))
                nc.vector.tensor_tensor(k.own[:].rearrange("p (r l) -> p r l", l=P), bc(k.iota_p[:], 1, HI), bc(k.own_at[:], 2, P),
                                        ALU.is_equal).then_inc(s_own, 1)
                for r in range(R):
                    dve.wait_ge(s_tail, r + 1)
                    nc.vector.tensor_copy(tails[:, of_round(r), :], p_tail[r % 2][:, 0:R * D].rearrange("p (j d) -> p j d", d=D)).then_inc(s_tails, 1)
                dve.wait_ge(s_tails, R)

                def first_half(r):
                    rr = of_round(r)
                    s, xr = sums[:, rr, :], k.xs[:, rr, :]
                    dve.wait_ge(s_sums[r], 16 * R)
                    c.then(nc.vector.tensor_tensor(s, s, bc(k.filled[:, rr], 2, D), ALU.mult))
                    nc.vector.tensor_tensor(s, s, tails[:, rr, :], ALU.add).then_inc(s_added, 1)
                    dve.wait_ge(s_out, r + 1)
                    nc.vector.tensor_tensor(s, p_out[r % 2][:, 0:R * D].rearrange("p (j d) -> p j d", d=D), bc(k.W_br[:], 1, R), ALU.add).then_inc(s_z, 1)
                    dve.wait_ge(s_tanh, r + 1)
                    c.then(nc.vector.tensor_tensor(xr, xr, s, ALU.add))
                    layer_norm(c, xr, s, h[:, rr, :], mean[:, rr], std[:, rr], s_var, s_std, s_h, r + 1)

                for r in range(R + 1):
                    if r < R:
                        first_half(r)
                    if r >= 1:
                        for hi in range((r - 1) * R, r * R):
                            dve.wait_ge(s_kvq, hi + 1)
                            nc.vector.tensor_tensor(k.centre[:, hi, :], p_tail[hi % 2][:, 2 * D + QW:NODE_W], k.cen_br[:], ALU.add).then_inc(s_y, 1)
                dve.wait_ge(s_init, 16)
                c.then(nc.vector.tensor_scalar(k.q_init[:], k.q_init[:], k.came_on[:], None, ALU.mult))


def attention_layer(k):
    nc = k.nc
    with ExitStack() as ctx:
        tile, bank, sem = helpers(k, ctx)
        attr = [tile(f"attr_a{b}", [P, T, EC]) for b in range(2)]
        flat_attr = tile("flat_attr", [P, TP, EC])
        qin = [tile(f"qin{b}", [P, T, QW]) for b in range(2)]
        idx = [tile(f"idx_a{b}", [P, T], I32) for b in range(2)]
        got = [tile(f"got_a{b}", [P, T, 2 * D]) for b in range(2)]
        keep = [tile(f"keep_a{b}", [P, QW, T1]) for b in range(2)]
        query = [tile(f"query{b}", [P, QW, T1]) for b in range(2)]
        prod = tile("prod", [P, D, T])
        logit = tile("logit_a", [P, NH, T])
        fresh = tile("fresh", [P, NH, T1])
        logit1 = tile("logit_carry", [P, NH, T1])
        top = [tile(f"top{b}", [P, NH, T1]) for b in range(2)]
        drop = tile("drop", [P, NH, T1])
        below = tile("below_a", [P, NH, T])
        scale = tile("scale", [P, QW, T1])
        add = tile("add_a", [P, QW, T1])
        state = [tile(f"state_a{b}", [P, QW, T1]) for b in range(2)]
        packed = [tile(f"packed_a{b}", [P, T, SW]) for b in range(2)]
        net = [tile(f"net{b}", [P, TP, EC]) for b in range(2)]
        attr_t = tile("attr_t", [P, GROUPS * P])
        relu = tile("relu", [P, GROUPS * P])
        soft = tile("soft", [P, GROUPS * P])
        half = tile("half", [P, 1])
        p_a, p_z, p_w = ([bank(f"{n}{j}") for j in range(2)] for n in ("p_a", "p_z", "p_w"))
        (s_zero, s_idx, s_keep, s_query, s_q, s_value, s_used, s_below, s_exp, s_state, s_packed, s_dve, s_act, s_passed, s_carry) = (
            sem(n + "_a") for n in ("s_zero", "s_idx", "s_keep", "s_query", "s_q", "s_value", "s_used", "s_below", "s_exp",
                                    "s_state", "s_packed", "s_dve", "s_act", "s_passed", "s_carry"))
        s_at, s_at_copied, s_z, s_soft, s_w, s_net, s_flat = (sem(n + "_a") for n in ("s_at", "s_at_copied", "s_z", "s_soft", "s_w", "s_net", "s_flat"))
        s_rec, s_qin, s_got, s_store = ([sem(f"{n}{b}") for b in range(2)] for n in ("s_rec_a", "s_qin", "s_got_a", "s_store_a"))
        records_v, starts_v, sums_v = by_run(k.records), by_run(k.q_starts), by_run(k.sums1)
        halves = ((0, 4 * P, 4), (4 * P, GROUPS * P, GROUPS - 4))

        with nc.Block() as block:
            @block.sync
            def _(sp):
                sp.wait_ge(s_zero, 4)

                def body(i):
                    for b in range(2):
                        n = 2 * i + b
                        cols = bass.ds(i * 2 * T + b * T, T)
                        wait(sp, s_flat, n - 1)
                        sp.dma_start(attr[b][:], records_v[:, cols, 0:EC]).then_inc(s_rec[b], 16)
                        wait(sp, s_query, n - 1)
                        sp.dma_start(qin[b][:], starts_v[:, cols, :]).then_inc(s_qin[b], 16)

                loop(sp, body)

            @block.gpsimd
            def _(pool):
                def body(i):
                    for b in range(2):
                        n = 2 * i + b
                        wait(pool, s_used, n - 1)
                        pool.wait_ge(s_idx, n + 1)
                        pool.sem_inc(s_passed, 1)
                        for t in range(T):
                            nc.gpsimd.indirect_dma_start(
                                got[b][:, t, :], None, k.kv_table,
                                bass.IndirectOffsetOnAxis(ap=idx[b][:, t:t + 1], axis=0)).then_inc(s_got[b], 16)

                loop(pool, body)

            @block.tensor
            def _(pe):
                def body(i):
                    for b in range(2):
                        n = 2 * i + b
                        pe.wait_ge(s_flat, n + 1)
                        wait(pe, s_at_copied, n)
                        for g in range(GROUPS):
                            last = nc.tensor.transpose(p_a[g // 4][:, (g % 4) * P:(g % 4 + 1) * P], flat_attr[:, g * G:(g + 1) * G, :].rearrange("p t c -> p (t c)"), k.ident[:])
                        last.then_inc(s_at, 1)
                        pe.wait_ge(s_at_copied, n + 1)
                        wait(pe, s_soft, n)
                        for j, (c0, c1, _) in enumerate(halves):
                            last = nc.tensor.matmul(p_z[j][:, 0:c1 - c0], k.w1_t[:], attr_t[:, c0:c1], start=True, stop=True)
                        last.then_inc(s_z, 1)
                        pe.wait_ge(s_soft, n + 1)
                        wait(pe, s_net, n)
                        for g in range(GROUPS):
                            to = p_w[g // 4][:, (g % 4) * P:(g % 4 + 1) * P]
                            nc.tensor.matmul(to, relu[:, g * P:(g + 1) * P], k.w2_t[:], start=True, stop=False)
                            last = nc.tensor.matmul(to, soft[:, g * P:(g + 1) * P], k.w2_t[:], start=False, stop=True)
                        last.then_inc(s_w, 1)

                loop(pe, body)

            @block.scalar
            def _(act):
                c = Chain(act, s_act, 2 * 4)

                def lay_out(n, i, b):
                    cols = bass.ds(i * 2 * T + b * T, T)
                    wait(act, s_state, n - 1)
                    nc.scalar.copy(keep[b][:, :, 1:T1], bc(k.same[:, cols], 1, QW)).then_inc(s_keep, 1)
                    act.wait_ge(s_qin[b], 16 * (i + 1))
                    wait(act, s_q, n)
                    nc.scalar.copy(query[b][:, :, 1:T1], qin[b][:].rearrange("p t c -> p c t")).then_inc(s_query, 1)

                def networks(n, i, b):
                    act.wait_ge(s_rec[b], 16 * (i + 1))
                    wait(act, s_at, n)
                    nc.scalar.copy(flat_attr[:, 0:T, :], attr[b][:]).then_inc(s_flat, 1)
                    act.wait_ge(s_at, n + 1)
                    wait(act, s_z, n)
                    for j, (c0, c1, _) in enumerate(halves):
                        ins = nc.scalar.copy(attr_t[:, c0:c1], p_a[j][:, 0:c1 - c0])
                    ins.then_inc(s_at_copied, 1)
                    act.wait_ge(s_z, n + 1)
                    wait(act, s_w, n)
                    for j, (c0, c1, _) in enumerate(halves):
                        nc.scalar.activation(relu[:, c0:c1], p_z[j][:, 0:c1 - c0], ACT.Relu, bias=k.b1_c[:])
                        c.mark(nc.scalar.activation(soft[:, c0:c1], p_z[j][:, 0:c1 - c0], ACT.Abs, bias=k.b1_c[:]))
                    c.wait()
                    c.then(nc.scalar.activation(soft[:], soft[:], ACT.Exp, scale=-1.0))
                    nc.scalar.activation(soft[:], soft[:], ACT.Ln, bias=half[:], scale=0.5).then_inc(s_soft, 1)

                def finish(n, i, b):
                    act.wait_ge(s_below, n + 1)
                    nc.scalar.activation(add[:, D:QW, 1:T1], below[:], ACT.Exp).then_inc(s_exp, 1)
                    nc.scalar.activation(scale[:, 0:D, :].rearrange("p (h d) t -> p h d t", h=NH), bc(drop[:], 2, HD), ACT.Exp)
                    nc.scalar.activation(scale[:, D:QW, :], drop[:], ACT.Exp).then_inc(s_exp, 1)
                    wait(act, s_store[b], 16 * i)
                    c.mark(nc.scalar.copy(packed[b][:, :, QW:SW], top[b][:, :, 1:T1].rearrange("p h t -> p t h")))
                    act.wait_ge(s_state, n + 1)
                    nc.scalar.copy(packed[b][:, :, 0:QW], state[b][:, :, 1:T1].rearrange("p c t -> p t c")).then_inc(s_packed, 1)
                    act.wait_ge(s_packed, n + 1)
                    c.wait()
                    act.dma_start(sums_v[:, bass.ds(i * 2 * T + b * T, T), :], packed[b][:]).then_inc(s_store[b], 16)

                act.wait_ge(s_zero, 4)
                c.begin(0)
                lay_out(0, 0, 0)
                networks(0, 0, 0)

                def body(i):
                    if not at_start(i):
                        c.begin(i)
                    for b in range(2):
                        n = 2 * i + b
                        if not at_end(i, b):
                            lay_out(n + 1, i + b, 1 - b)
                            networks(n + 1, i + b, 1 - b)
                        finish(n, i, b)
                    if not at_end(i):
                        c.end()

                loop(act, body)
                for b in range(2):
                    act.wait_ge(s_store[b], 16 * PAIRS)

            @block.vector
            def _(dve):
                c = Chain(dve, s_dve, 2 * 11)

                def index(n, i, b):
                    wait(dve, s_got[b], SCATTERED * i)
                    nc.vector.tensor_copy(idx[b][:], k.dst_s[:, bass.ds(i * 2 * T + b * T, T)]).then_inc(s_idx, 1)

                def chunk(n, i, b):
                    cols = bass.ds(i * 2 * T + b * T, T)
                    dve.wait_ge(s_query, n + 1)
                    if at_start(i, b):
                        c.then(nc.vector.tensor_copy(query[b][:, :, 0], k.q_init[:]))
                    else:
                        c.then(nc.vector.tensor_copy(query[b][:, :, 0:1], query[1 - b][:, :, T:T1]))
                    flat = query[b][:].rearrange("p c t -> p (c t)")
                    nc.vector.tensor_tensor_scan(flat, keep[b][:].rearrange("p c t -> p (c t)"), flat, 0.0, ALU.mult, ALU.add).then_inc(s_q, 1)
                    dve.wait_ge(s_w, n + 1)
                    for j, (c0, c1, groups) in enumerate(halves):
                        c.mark(nc.vector.tensor_tensor(
                            net[b][:, c0 // EC:c1 // EC, :], p_w[j][:, 0:c1 - c0].rearrange("p (t o) -> p t o", o=EC),
                            bc(k.b2_r[:], 1, G * groups), ALU.add))
                    c.wait()
                    nc.vector.tensor_scalar(fresh[:, :, 1:T1], bc(k.same[:, cols], 1, NH), -1.0, FAR, ALU.add, ALU.mult).then_inc(s_net, 1)
                    dve.wait_ge(s_got[b], SCATTERED * (i + 1))
                    dve.wait_ge(s_q, n + 1)
                    dve.wait_ge(s_net, n + 1)
                    c.then(nc.vector.tensor_tensor(prod[:], got[b][:, :, 0:D].rearrange("p t c -> p c t"), query[b][:, 0:D, 1:T1], ALU.mult))
                    by_head = prod[:].rearrange("p (h d) t -> p h d t", h=NH)
                    c.then(nc.vector.tensor_tensor(by_head, by_head, bc(net[b][:, 0:T, 0:HD].rearrange("p t o -> p o t"), 1, NH), ALU.mult))
                    c.then(nc.vector.tensor_reduce(logit[:], prod[:].rearrange("p (h d) t -> p h t d", h=NH), AX.X, ALU.add))
                    if at_start(i, b):
                        c.mark(nc.vector.memset(logit1[:, :, 0:1], -FAR))
                    else:
                        c.mark(nc.vector.tensor_copy(logit1[:, :, 0:1], top[1 - b][:, :, T:T1]))
                    c.then(nc.vector.tensor_tensor(logit1[:, :, 1:T1], logit[:], query[b][:, D:QW, 1:T1], ALU.add))
                    wait(dve, s_packed, n - 1)
                    c.then(nc.vector.tensor_tensor_scan(top[b][:].rearrange("p h t -> p (h t)"), fresh[:].rearrange("p h t -> p (h t)"),
                                                        logit1[:].rearrange("p h t -> p (h t)"), -FAR, ALU.add, ALU.max))
                    wait(dve, s_exp, 2 * n)
                    c.then(nc.vector.tensor_tensor(drop[:, :, 1:T1], top[b][:, :, 0:T], top[b][:, :, 1:T1], ALU.subtract))
                    c.mark(nc.vector.tensor_tensor(drop[:, :, 1:T1], drop[:, :, 1:T1], fresh[:, :, 1:T1], ALU.add))
                    c.wait()
                    nc.vector.tensor_tensor(below[:], logit1[:, :, 1:T1], top[b][:, :, 1:T1], ALU.subtract).then_inc(s_below, 1)
                    value = got[b][:, :, D:2 * D].rearrange("p t (h d) -> p h d t", h=NH)
                    nc.vector.tensor_tensor(value, value, bc(net[b][:, 0:T, HD:EC].rearrange("p t o -> p o t"), 1, NH), ALU.mult).then_inc(s_value, 1)
                    dve.wait_ge(s_exp, 2 * n + 1)
                    dve.wait_ge(s_value, n + 1)
                    nc.vector.tensor_tensor(add[:, 0:D, 1:T1].rearrange("p (h d) t -> p h d t", h=NH), value,
                                            bc(add[:, D:QW, 1:T1], 2, HD), ALU.mult).then_inc(s_used, 1)
                    if at_start(i, b):
                        nc.vector.memset(add[:, :, 0:1], 0.0).then_inc(s_carry, 1)
                    else:
                        nc.vector.tensor_copy(add[:, :, 0:1], state[1 - b][:, :, T:T1]).then_inc(s_carry, 1)
                    dve.wait_ge(s_carry, n + 1)
                    dve.wait_ge(s_used, n + 1)
                    dve.wait_ge(s_exp, 2 * n + 2)
                    nc.vector.tensor_tensor_scan(state[b][:].rearrange("p c t -> p (c t)"), scale[:].rearrange("p c t -> p (c t)"),
                                                 add[:].rearrange("p c t -> p (c t)"), 0.0, ALU.mult, ALU.add).then_inc(s_state, 1)
                    dve.wait_ge(s_state, n + 1)

                for b in range(2):
                    c.mark(nc.vector.memset(keep[b][:, :, 0:1], 0.0))
                c.mark(nc.vector.memset(flat_attr[:, T:TP, :], 0.0))
                c.mark(nc.vector.memset(fresh[:, :, 0:1], -FAR))
                c.mark(nc.vector.memset(drop[:, :, 0:1], -FAR))
                c.wait()
                nc.vector.memset(half[:], 0.5).then_inc(s_zero, 4)
                index(0, 0, 0)

                def body(i):
                    if not at_start(i):
                        c.begin(i)
                    for b in range(2):
                        n = 2 * i + b
                        if not at_end(i, b):
                            index(n + 1, i + b, 1 - b)
                        chunk(n, i, b)
                    c.end()

                loop(dve, body)
                c.then(nc.vector.tensor_copy(k.tail1[:, 0:QW], state[1][:, :, T]))
                c.then(nc.vector.tensor_copy(k.tail1[:, QW:SW], top[1][:, :, T]))


def attention_nodes(k):
    nc = k.nc
    R = 7
    W = SW + 1
    assert HI % R == 0 and R * W <= 512
    with ExitStack() as ctx:
        tile, bank, sem = helpers(k, ctx)
        own = tile("own2", [P, ROWS])
        sums = tile("sums_f", [P, HI, SW])
        parts = tile("parts_f", [P, HI, W])
        vals = tile("vals", [P, 2 + NH])
        diag = tile("diag", [P, 2 + NH, P])
        peer = tile("peer", [P, P])
        peer_later = tile("peer_later", [P, P])
        peer_top = tile("peer_top", [P, NH, P])
        no_peer = tile("no_peer", [P, P])
        top = tile("top_f", [P, NH])
        shrink = tile("shrink", [P, NH])
        later = tile("later", [P, 1])
        pay = tile("pay", [P, W])
        top_r, fac_e, fac_t, tmp = (tile(n, [P, HI, NH]) for n in ("top_r", "fac_e", "fac_t", "tmp_f"))
        empty = tile("empty", [P, HI])
        feat = [tile(f"feat_f{b}", [D, R * P]) for b in range(2)]
        z = tile("z", [P, HI, D])
        soft = tile("soft_f", [P, HI, D])
        half = tile("half_f", [P, 1])
        p_bc = [bank(f"p_bc{b}") for b in range(2)]
        p_f = [[bank(f"p_ff{b}{j}") for j in range(2)] for b in range(2)]
        p_out = [bank(f"p_of{b}") for b in range(2)]
        s_sums = [sem(f"s_sums_f{r}") for r in range(R)]
        (s_made, s_bc, s_exp_in, s_exp_out, s_part, s_part_read, s_u, s_f, s_feat, s_out, s_z, s_soft, s_y, s_f2, s_feat2,
         s_out2, s_x, s_store, s_dve, s_act) = (
            sem(n + "_f") for n in ("s_made", "s_bc", "s_exp_in", "s_exp_out", "s_part", "s_part_read", "s_u", "s_f", "s_feat",
                                    "s_out", "s_z", "s_soft", "s_y", "s_f2", "s_feat2", "s_out2", "s_x", "s_store", "s_dve",
                                    "s_act"))

        def of_round(r):
            return slice(r * R, (r + 1) * R)

        with nc.Block() as block:
            @block.sync
            def _(sp):
                for r in range(R):
                    sp.wait_ge(s_x, r + 1)
                    first, end = r * R, min((r + 1) * R, HI - 1)
                    sp.dma_start(k.out[first * P:end * P, :].rearrange("(h l) c -> l h c", l=P), k.xs[:, first:end, :]).then_inc(s_store, 16)
                sp.dma_start(k.out[(HI - 1) * P:N, :], k.xs[0:LAST_ROWS, HI - 1, :]).then_inc(s_store, 16)
                sp.wait_ge(s_store, 16 * (R + 1))

            @block.gpsimd
            def _(pool):
                for hi in range(HI):
                    nc.gpsimd.indirect_dma_start(
                        sums[:, hi, :], None, k.sums1,
                        bass.IndirectOffsetOnAxis(ap=k.last_at[:, hi:hi + 1], axis=0)).then_inc(s_sums[hi // R], 16)

            @block.tensor
            def _(pe):
                pe.wait_ge(s_made, 1)
                nc.tensor.matmul(p_bc[0][:, 0:NH * P], k.ones[:], diag[:, 2:2 + NH, :].rearrange("p v k -> p (v k)"), start=True, stop=True)
                nc.tensor.matmul(p_bc[1][:, 0:2 * P], k.ones[:], diag[:, 0:2, :].rearrange("p v k -> p (v k)"), start=True, stop=True).then_inc(s_bc, 1)
                pe.wait_ge(s_made, 3)
                for r in range(R):
                    if r >= 2:
                        pe.wait_ge(s_part_read, r - 1)
                    for j in range(R):
                        hi = r * R + j
                        last = nc.tensor.matmul(p_out[r % 2][:, j * W:(j + 1) * W], own[:, hi * P:(hi + 1) * P], pay[:], start=True, stop=True)
                    last.then_inc(s_part, 1)

                def products(r, b, of, weight, to, s_t, s_copied, s_done, s_read):
                    if r >= 1:
                        pe.wait_ge(s_copied, r)
                    for j in range(R):
                        last = nc.tensor.transpose(p_f[b][j // 4][0:D, (j % 4) * P:(j % 4 + 1) * P], of[:, r * R + j, 0:D], k.ident[:])
                    last.then_inc(s_t, 1)
                    pe.wait_ge(s_copied, r + 1)
                    if r >= 2:
                        pe.wait_ge(s_read, r - 1)
                    for j in range(R):
                        last = nc.tensor.matmul(to[r % 2][:, j * D:(j + 1) * D], feat[b][:, j * P:(j + 1) * P], weight[:], start=True, stop=True)
                    last.then_inc(s_done, 1)

                pe.wait_ge(s_part_read, R)
                for r in range(R + 1):
                    if r < R:
                        pe.wait_ge(s_u, r + 1)
                        products(r, 0, sums, k.vl_t, p_out, s_f, s_feat, s_out, s_z)
                    if r >= 1:
                        pe.wait_ge(s_y, r)
                        products(r - 1, 1, z, k.out_t, p_bc, s_f2, s_feat2, s_out2, s_x)

            @block.scalar
            def _(act):
                c = Chain(act, s_act)

                def copies(r, b, s_t, s_copied, s_done):
                    act.wait_ge(s_t, r + 1)
                    if r >= 1:
                        act.wait_ge(s_done, r)
                    nc.scalar.copy(feat[b][:, 0:4 * P], p_f[b][0][0:D, :])
                    nc.scalar.copy(feat[b][:, 4 * P:R * P], p_f[b][1][0:D, 0:(R - 4) * P]).then_inc(s_copied, 1)

                act.wait_ge(s_exp_in, 1)
                nc.scalar.activation(shrink[:], shrink[:], ACT.Exp).then_inc(s_exp_out, 1)
                for r in range(R + 1):
                    if r < R:
                        rr = of_round(r)
                        act.wait_ge(s_exp_in, 2 * r + 3)
                        nc.scalar.activation(fac_e[:, rr, :], fac_e[:, rr, :], ACT.Exp)
                        nc.scalar.activation(fac_t[:, rr, :], fac_t[:, rr, :], ACT.Exp).then_inc(s_exp_out, 1)
                        copies(r, 0, s_f, s_feat, s_out)
                    if r >= 1:
                        soft_r = soft[:, of_round(r - 1), :]
                        act.wait_ge(s_z, r)
                        c.then(nc.scalar.activation(soft_r, z[:, of_round(r - 1), :], ACT.Abs))
                        c.then(nc.scalar.activation(soft_r, soft_r, ACT.Exp, scale=-1.0))
                        nc.scalar.activation(soft_r, soft_r, ACT.Ln, bias=half[:], scale=0.5).then_inc(s_soft, 1)
                        copies(r - 1, 1, s_f2, s_feat2, s_out2)

            @block.vector
            def _(dve):
                c = Chain(dve, s_dve)
                v = nc.vector
                c.mark(v.memset(half[:], 0.5))
                c.mark(v.tensor_copy(vals[:, 0:1], k.last_row[:]))
                c.mark(v.tensor_copy(vals[:, 1:2], k.goes_on[:]))
                c.then(v.tensor_copy(vals[:, 2:2 + NH], k.tail1[:, QW:SW]))
                v.tensor_tensor(diag[:], bc(k.ident[:], 1, 2 + NH), bc(vals[:], 2, P), ALU.mult).then_inc(s_made, 1)
                v.tensor_tensor(own[:].rearrange("p (r l) -> p r l", l=P), bc(k.iota_p[:], 1, HI), bc(k.own_at[:], 2, P), ALU.is_equal).then_inc(s_made, 1)
                dve.wait_ge(s_bc, 1)
                c.then(v.tensor_scalar(peer[:], p_bc[1][:, 0:P], k.last_row[:], None, ALU.is_equal))
                c.then(v.tensor_tensor(peer[:], peer[:], p_bc[1][:, P:2 * P], ALU.mult))
                c.mark(v.tensor_tensor(peer_later[:], peer[:], k.less[:], ALU.mult))
                c.then(v.tensor_scalar(no_peer[:], peer[:], -1.0, FAR, ALU.add, ALU.mult))
                c.mark(v.tensor_reduce(later[:], peer_later[:], AX.X, ALU.add))
                c.then(v.tensor_tensor(peer_top[:], p_bc[0][:, 0:NH * P].rearrange("p (h k) -> p h k", h=NH), bc(no_peer[:], 1, NH), ALU.add))
                c.then(v.tensor_reduce(top[:], peer_top[:], AX.X, ALU.max))
                c.then(v.tensor_tensor(shrink[:], k.tail1[:, QW:SW], top[:], ALU.subtract))
                v.tensor_scalar(shrink[:], shrink[:], 0.0, None, ALU.min).then_inc(s_exp_in, 1)
                c.then(v.tensor_scalar(pay[:, SW:W], later[:], 0.0, None, ALU.is_equal))
                c.mark(v.tensor_scalar(pay[:, QW:SW], top[:], pay[:, SW:W], None, ALU.mult))
                dve.wait_ge(s_exp_out, 1)
                c.mark(v.tensor_tensor(pay[:, 0:D].rearrange("p (h d) -> p h d", h=NH), k.tail1[:, 0:D].rearrange("p (h d) -> p h d", h=NH),
                                       bc(shrink[:], 2, HD), ALU.mult))
                c.wait()
                v.tensor_tensor(pay[:, D:QW], k.tail1[:, D:QW], shrink[:], ALU.mult).then_inc(s_made, 1)
                for r in range(R):
                    dve.wait_ge(s_part, r + 1)
                    v.tensor_copy(parts[:, r * R:(r + 1) * R, :], p_out[r % 2][:, 0:R * W].rearrange("p (j w) -> p j w", w=W)).then_inc(s_part_read, 1)
                dve.wait_ge(s_part_read, R)
                c.then(v.tensor_scalar(tmp[:], bc(parts[:, :, SW], 2, NH), -1.0, FAR, ALU.add, ALU.mult))
                c.then(v.tensor_tensor(tmp[:], tmp[:], parts[:, :, QW:SW], ALU.add))
                c.then(v.tensor_scalar(empty[:], k.filled[:], -1.0, 1.0, ALU.mult, ALU.add))

                def attended(r):
                    rr = of_round(r)
                    sums_r, parts_r, tmp_r, top_rr, e, t = (x[:, rr, :] for x in (sums, parts, tmp, top_r, fac_e, fac_t))
                    dve.wait_ge(s_sums[r], 16 * R)
                    c.then(v.tensor_tensor(top_rr, tmp_r, sums_r[:, :, QW:SW], ALU.max))
                    v.tensor_tensor(t, tmp_r, top_rr, ALU.subtract).then_inc(s_exp_in, 1)
                    v.tensor_tensor(e, sums_r[:, :, QW:SW], top_rr, ALU.subtract).then_inc(s_exp_in, 1)
                    dve.wait_ge(s_exp_out, r + 2)
                    c.then(v.tensor_tensor(e, e, bc(k.filled[:, rr], 2, NH), ALU.mult))
                    for of, fac in ((sums_r, e), (parts_r, t)):
                        for hd in range(NH):
                            u = of[:, :, hd * HD:(hd + 1) * HD]
                            c.mark(v.tensor_tensor(u, u, bc(fac[:, :, hd], 2, HD), ALU.mult))
                        c.mark(v.tensor_tensor(of[:, :, D:QW], of[:, :, D:QW], fac, ALU.mult))
                    c.wait()
                    c.then(v.tensor_tensor(sums_r[:, :, 0:QW], sums_r[:, :, 0:QW], parts_r[:, :, 0:QW], ALU.add))
                    c.then(v.tensor_tensor(tmp_r, sums_r[:, :, D:QW], bc(empty[:, rr], 2, NH), ALU.add))
                    c.then(v.reciprocal(tmp_r, tmp_r))
                    for hd in range(NH):
                        u = sums_r[:, :, hd * HD:(hd + 1) * HD]
                        c.mark(v.tensor_tensor(u, u, bc(tmp_r[:, :, hd], 2, HD), ALU.mult))
                    c.then(v.tensor_tensor(e, sums_r[:, :, D:QW], tmp_r, ALU.mult))
                    for hd in range(NH):
                        c.mark(v.tensor_tensor(soft[:, rr, hd * HD:(hd + 1) * HD], bc(k.vl_br[:, hd * HD:(hd + 1) * HD], 1, R),
                                               bc(e[:, :, hd], 2, HD), ALU.mult))
                    c.mark(v.tensor_tensor(k.xs[:, rr, :], k.xs[:, rr, :], bc(k.out_br[:], 1, R), ALU.add))
                    c.wait()
                    v.tensor_tensor(k.centre[:, rr, :], k.centre[:, rr, :], soft[:, rr, :], ALU.add).then_inc(s_u, 1)
                    dve.wait_ge(s_u, r + 1)

                def activated(r):
                    rr = of_round(r)
                    dve.wait_ge(s_out, r + 1)
                    v.tensor_tensor(z[:, rr, :], p_out[r % 2][:, 0:R * D].rearrange("p (j d) -> p j d", d=D), k.centre[:, rr, :], ALU.add).then_inc(s_z, 1)
                    dve.wait_ge(s_z, r + 1)
                    dve.wait_ge(s_soft, r + 1)
                    v.scalar_tensor_tensor(z[:, rr, :], z[:, rr, :], 0.0, soft[:, rr, :], ALU.max, ALU.add).then_inc(s_y, 1)

                def added(r):
                    rr = of_round(r)
                    dve.wait_ge(s_out2, r + 1)
                    v.tensor_tensor(k.xs[:, rr, :], k.xs[:, rr, :], p_bc[r % 2][:, 0:R * D].rearrange("p (j d) -> p j d", d=D), ALU.add).then_inc(s_x, 1)

                for r in range(R + 2):
                    if r < R:
                        attended(r)
                    if 1 <= r <= R:
                        activated(r - 1)
                    if r >= 2:
                        added(r - 2)


def build(nc, args, out, phases=9):
    k = Kernel()
    k.nc, k.out = nc, out
    k.x, k.src, k.dst, k.attr, k.etype = args[0:5]
    (k.rel, k.att_w, k.att_b, k.W_w, k.W_b, k.k_w, k.q_w, k.v_w, k.kn_w1, k.kn_b1, k.kn_w2, k.kn_b2,
     k.kl_w, k.kl_b, k.vn_w1, k.vn_b1, k.vn_w2, k.vn_b2, k.vl_w, k.vl_b, k.cen_w, k.cen_b, k.out_w,
     k.out_b) = args[5:]

    def scratch(name, shape, dt=F32):
        return nc.dram_tensor(name, shape, dt, kind="Internal").ap()

    k.records = scratch("records", [STREAM, REC])
    k.h_table = scratch("h_table", [ROWS, D])
    k.h3_table = scratch("h3_table", [ROWS, 3 * D], BF16)
    k.kv_table = scratch("kv_table", [ROWS, 2 * D])
    k.q_table = scratch("q_table", [ROWS, QW])
    k.q_starts = scratch("q_starts", [STREAM + ROWS, QW])
    k.sums0 = scratch("sums0", [STREAM, D])
    k.sums1 = scratch("sums1", [STREAM, SW])

    with ExitStack() as ctx:
        tile, _, _ = helpers(k, ctx)
        k.xs = tile("xs", [P, HI, D])
        k.start = tile("start", [P, HI])
        k.filled = tile("filled", [P, HI])
        k.last_at = tile("last_at", [P, HI], I32)
        k.ident = tile("ident", [P, P])
        k.ones = tile("ones", [P, P])
        k.iota_p = tile("iota_p", [P, P])
        k.less = tile("less", [P, P])
        k.eps = tile("eps", [P, 1])
        k.same = tile("same", [P, NT])
        k.dst_s = tile("dst_s", [P, NT], I32)
        k.first_row = tile("first_row", [P, 1])
        k.last_row = tile("last_row", [P, 1])
        k.goes_on = tile("goes_on", [P, 1])
        k.came_on = tile("came_on", [P, 1])
        k.slow = tile("slow", [P, 1], I32)
        k.own_at = tile("own_at", [P, HI])
        k.W_t = tile("W_t", [D, D])
        k.node_w = tile("node_w", [D, NODE_W])
        k.vl_t = tile("vl_t", [D, D])
        k.out_t = tile("out_t", [D, D])
        k.w1_t = tile("w1_t", [P, P])
        k.w2_t = tile("w2_t", [P, P])
        k.b1_c = tile("b1_c", [P, 1])
        k.b2_r = tile("b2_r", [P, EC])
        k.W_br = tile("W_br", [P, D])
        k.cen_br = tile("cen_br", [P, D])
        k.vl_br = tile("vl_br", [P, D])
        k.out_br = tile("out_br", [P, D])

        with ExitStack() as sort_ctx:
            node_tile = tile
            tile, _, _ = helpers(k, sort_ctx)
            k.cnt = tile("cnt", [P, HI])
            k.identb = tile("identb", [P, P], BF16)
            k.iota_b = tile("iota_b", [P, P, T], BF16)
            k.less_b = tile("less_b", [P, P], BF16)
            k.number = tile("number", [P, 1])
            k.base_i = tile("base_i", [P, CHUNKS], I32)
            k.dst_in = tile("dst_in", [P, NT], BF16)
            k.lo_b = tile("lo_b", [P, NT], BF16)
            k.hi_b = tile("hi_b", [P, NT], BF16)
            k.src_f = tile("src_f", [P, NT])
            k.dst_f = tile("dst_f", [P, NT])
            k.rel_gate = tile("rel_gate", [P, NT])
            k.last_attr = tile("last_attr", [P, T, EC])
            k.parts = [tile(f"parts{b}", [P, 3, 2, HI], BF16) for b in range(2)]
            setup(k)
            k.lo_hot = [tile(f"lo_hot{b}", [P, P, T], BF16) for b in range(2)]
            k.hi_hot = [tile(f"hi_hot{b}", [P, HI, T], BF16) for b in range(2)]
            histogram(k)
            sort(k)
        tile = node_tile
        k.tail1 = tile("tail1", [P, SW])
        k.q_init = tile("q_init", [P, QW])
        k.centre = tile("centre", [P, HI, D])
        with ExitStack() as relation_ctx:
            tile, _, _ = helpers(k, relation_ctx)
            k.tail0 = tile("tail0", [P, D])
            if phases > 1:
                relation_layer(k)
            k.own = tile("own", [P, ROWS])
            if phases > 2:
                relation_nodes(k)
        if phases > 3:
            attention_layer(k)
        if phases > 4:
            attention_nodes(k)


_INS = ["x", "src", "dst", "edge_attr_32", "edge_type_2", "L0_gnn_relation_emb", "L0_gnn_att_w", "L0_gnn_att_b",
        "L0_gnn_W_w", "L0_gnn_W_b", "L1_gnn_k_w", "L1_gnn_q_w", "L1_gnn_v_w", "L1_gnn_wkn_w1", "L1_gnn_wkn_b1",
        "L1_gnn_wkn_w2", "L1_gnn_wkn_b2", "L1_gnn_wkl_w", "L1_gnn_wkl_b", "L1_gnn_wvn_w1", "L1_gnn_wvn_b1",
        "L1_gnn_wvn_w2", "L1_gnn_wvn_b2", "L1_gnn_wvl_w", "L1_gnn_wvl_b", "L1_gnn_cen_w", "L1_gnn_cen_b",
        "L1_gnn_out_w", "L1_gnn_out_b"]


def kernel(**inputs):
    import numpy as np
    import concourse.bacc as bacc
    from concourse.bass_utils import run_bass_kernel_spmd

    nc = bacc.Bacc("TRN2", target_bir_lowering=False, num_devices=1)
    arrays, args = {}, []
    for name in _INS:
        a = np.ascontiguousarray(inputs[name])
        arrays[f"in_{name}"] = a
        args.append(nc.dram_tensor(f"in_{name}", a.shape, mybir.dt.from_np(a.dtype), kind="ExternalInput").ap())
    out = nc.dram_tensor("out", (N, D), F32, kind="ExternalOutput").ap()
    build(nc, args, out)
    return run_bass_kernel_spmd(nc, [arrays], core_ids=[0]).results[0]["out"]
```
